# Optimizing a Trainium2 kernel written in Bass

```python
import numpy as np
import jax
import jax.numpy as jnp

def _softmax(x, axis=-1):
    return jax.nn.softmax(x, axis=axis)

def _gelu(x):
    return jax.nn.gelu(x, approximate=True)

def _silu(x):
    return jax.nn.silu(x)

def _sigmoid(x):
    return jax.nn.sigmoid(x)

def _layernorm(x, axis=-1, eps=1e-05):
    m = jnp.mean(x, axis=axis, keepdims=True)
    v = jnp.var(x, axis=axis, keepdims=True)
    return (x - m) / jnp.sqrt(v + eps)

def _scatter_add(tgt, idx, src, axis=0):
    return tgt.at[idx].add(src)

def _segment_sum(src, seg, n):
    return jax.ops.segment_sum(src, seg, n)
kernel_name = 'mk_vit_tower_cls_d1_tok_img512_r4_aca6d5'

def setup_inputs(seed: int=0):
    np.random.seed(seed)
    _w = jnp.asarray

    def _rec_inputs():
        import jax
        import jax.numpy as jnp
        _rk = jax.random.key(seed)
        x = 7.57192e-06 + 1.00007 * jax.random.normal(jax.random.fold_in(_rk, 1), (128, 3, 224, 224), jnp.float32)
        cls_tok = 0.02 * jax.random.normal(jax.random.fold_in(_rk, 5), (1, 1, 128), jnp.float32)
        return (x, cls_tok)
    x, cls_tok = _rec_inputs()

    def _L0_tok_setup():
        import jax, jax.numpy as jnp
        import numpy as np
        DEPTH = 4
        HEADS = 8
        DIM = 128
        HID = 256
        P = 16
        IMG = 224
        GRID = IMG // P
        NPATCH = GRID * GRID
        NTOK = NPATCH + 1
        BATCH = 64
        EPS = 1e-05

        def layernorm(x, w, b):
            mu = jnp.mean(x, axis=-1, keepdims=True)
            var = jnp.mean(jnp.square(x - mu), axis=-1, keepdims=True)
            return (x - mu) * jax.lax.rsqrt(var + EPS) * w + b
        key = jax.random.key(seed)
        ks = jax.random.split(key, 12)
        s = 0.02
        inp = {'x': jax.random.normal(ks[0], (BATCH, 3, IMG, IMG), jnp.float32), 'conv_w': jax.random.normal(ks[1], (3 * P * P, DIM), jnp.float32) * s, 'conv_b': jnp.zeros((DIM,), jnp.float32), 'cls_token': jax.random.normal(ks[2], (1, 1, DIM), jnp.float32) * s, 'pos_embed': jax.random.normal(ks[3], (1, NTOK, DIM), jnp.float32) * s, 'ln1_w': jnp.ones((DEPTH, DIM), jnp.float32), 'ln1_b': jnp.zeros((DEPTH, DIM), jnp.float32), 'qkv_w': jax.random.normal(ks[4], (DEPTH, DIM, 3 * DIM), jnp.float32) * s, 'qkv_b': jnp.zeros((DEPTH, 3 * DIM), jnp.float32), 'proj_w': jax.random.normal(ks[5], (DEPTH, DIM, DIM), jnp.float32) * s, 'proj_b': jnp.zeros((DEPTH, DIM), jnp.float32), 'ln2_w': jnp.ones((DEPTH, DIM), jnp.float32), 'ln2_b': jnp.zeros((DEPTH, DIM), jnp.float32), 'fc1_w': jax.random.normal(ks[6], (DEPTH, DIM, HID), jnp.float32) * s, 'fc1_b': jnp.zeros((DEPTH, HID), jnp.float32), 'fc2_w': jax.random.normal(ks[7], (DEPTH, HID, DIM), jnp.float32) * s, 'fc2_b': jnp.zeros((DEPTH, DIM), jnp.float32), 'norm_w': jnp.ones((DIM,), jnp.float32), 'norm_b': jnp.zeros((DIM,), jnp.float32)}
        return inp
    _L0_tok_all = _L0_tok_setup()
    _L0_tok_in = {k: v for k, v in _L0_tok_all.items() if k in ('conv_w', 'conv_b', 'cls_token', 'pos_embed', 'ln1_w', 'ln1_b', 'qkv_w', 'qkv_b', 'proj_w', 'proj_b', 'ln2_w', 'ln2_b', 'fc1_w', 'fc1_b', 'fc2_w', 'fc2_b', 'norm_w', 'norm_b')}
    del _L0_tok_all

    def _L0_attn_setup():
        import jax, jax.numpy as jnp
        import numpy as np
        H, DH, M, DIN = (8, 64, 32, 128)
        INNER = H * DH
        key = jax.random.key(seed)
        ks = jax.random.split(key, 12)
        s = 0.02
        B, N = (4, 4096)
        return {'x': jax.random.normal(ks[0], (B, N, DIN), jnp.float32), 'Wx': jax.random.normal(ks[1], (INNER, DIN), jnp.float32) * s, 'bx': jnp.zeros((INNER,), jnp.float32), 'Wfx': jax.random.normal(ks[2], (INNER, DIN), jnp.float32) * s, 'bfx': jnp.zeros((INNER,), jnp.float32), 'Wslice': jax.random.normal(ks[3], (M, DH), jnp.float32) * s, 'bslice': jnp.zeros((M,), jnp.float32), 'Wq': jax.random.normal(ks[4], (DH, DH), jnp.float32) * s, 'Wk': jax.random.normal(ks[5], (DH, DH), jnp.float32) * s, 'Wv': jax.random.normal(ks[6], (DH, DH), jnp.float32) * s, 'Wout': jax.random.normal(ks[7], (DIN, INNER), jnp.float32) * s, 'bout': jnp.zeros((DIN,), jnp.float32), 'temperature': jnp.full((1, H, 1, 1), 0.5, jnp.float32)}
    _L0_attn_all = _L0_attn_setup()
    _L0_attn_in = {k: v for k, v in _L0_attn_all.items() if k in ('Wx', 'bx', 'Wfx', 'bfx', 'Wslice', 'bslice', 'Wq', 'Wk', 'Wv', 'Wout', 'bout', 'temperature')}
    del _L0_attn_all

    def _L0_ffn_setup():
        import jax, jax.numpy as jnp
        import numpy as np
        B, S, D, E, O = (256, 64, 128, 16, 128)
        key = jax.random.key(seed)
        k_x, k_wg, k_bg, k_we, k_be = jax.random.split(key, 5)
        scale_g = 1.0 / np.sqrt(D)
        scale_e = 1.0 / np.sqrt(D)
        return {'x': jax.random.normal(k_x, (B, S, D), dtype=jnp.float32), 'Wg': jax.random.uniform(k_wg, (D, E), jnp.float32, -scale_g, scale_g), 'bg': jax.random.uniform(k_bg, (E,), jnp.float32, -scale_g, scale_g), 'We': jax.random.uniform(k_we, (E, D, O), jnp.float32, -scale_e, scale_e), 'be': jax.random.uniform(k_be, (E, O), jnp.float32, -scale_e, scale_e)}
    _L0_ffn_all = _L0_ffn_setup()
    _L0_ffn_in = {k: v for k, v in _L0_ffn_all.items() if k in ('Wg', 'bg', 'We', 'be')}
    del _L0_ffn_all
    return {'x': x, 'cls_tok': cls_tok, 'L0_tok_conv_w': _L0_tok_in['conv_w'], 'L0_tok_conv_b': _L0_tok_in['conv_b'], 'L0_tok_cls_token': _L0_tok_in['cls_token'], 'L0_tok_pos_embed': _L0_tok_in['pos_embed'], 'L0_tok_ln1_w': _L0_tok_in['ln1_w'], 'L0_tok_ln1_b': _L0_tok_in['ln1_b'], 'L0_tok_qkv_w': _L0_tok_in['qkv_w'], 'L0_tok_qkv_b': _L0_tok_in['qkv_b'], 'L0_tok_proj_w': _L0_tok_in['proj_w'], 'L0_tok_proj_b': _L0_tok_in['proj_b'], 'L0_tok_ln2_w': _L0_tok_in['ln2_w'], 'L0_tok_ln2_b': _L0_tok_in['ln2_b'], 'L0_tok_fc1_w': _L0_tok_in['fc1_w'], 'L0_tok_fc1_b': _L0_tok_in['fc1_b'], 'L0_tok_fc2_w': _L0_tok_in['fc2_w'], 'L0_tok_fc2_b': _L0_tok_in['fc2_b'], 'L0_tok_norm_w': _L0_tok_in['norm_w'], 'L0_tok_norm_b': _L0_tok_in['norm_b'], 'L0_attn_Wx': _L0_attn_in['Wx'], 'L0_attn_bx': _L0_attn_in['bx'], 'L0_attn_Wfx': _L0_attn_in['Wfx'], 'L0_attn_bfx': _L0_attn_in['bfx'], 'L0_attn_Wslice': _L0_attn_in['Wslice'], 'L0_attn_bslice': _L0_attn_in['bslice'], 'L0_attn_Wq': _L0_attn_in['Wq'], 'L0_attn_Wk': _L0_attn_in['Wk'], 'L0_attn_Wv': _L0_attn_in['Wv'], 'L0_attn_Wout': _L0_attn_in['Wout'], 'L0_attn_bout': _L0_attn_in['bout'], 'L0_attn_temperature': _L0_attn_in['temperature'], 'L0_ffn_Wg': _L0_ffn_in['Wg'], 'L0_ffn_bg': _L0_ffn_in['bg'], 'L0_ffn_We': _L0_ffn_in['We'], 'L0_ffn_be': _L0_ffn_in['be']}

def reference(x, cls_tok, L0_tok_conv_w, L0_tok_conv_b, L0_tok_cls_token, L0_tok_pos_embed, L0_tok_ln1_w, L0_tok_ln1_b, L0_tok_qkv_w, L0_tok_qkv_b, L0_tok_proj_w, L0_tok_proj_b, L0_tok_ln2_w, L0_tok_ln2_b, L0_tok_fc1_w, L0_tok_fc1_b, L0_tok_fc2_w, L0_tok_fc2_b, L0_tok_norm_w, L0_tok_norm_b, L0_attn_Wx, L0_attn_bx, L0_attn_Wfx, L0_attn_bfx, L0_attn_Wslice, L0_attn_bslice, L0_attn_Wq, L0_attn_Wk, L0_attn_Wv, L0_attn_Wout, L0_attn_bout, L0_attn_temperature, L0_ffn_Wg, L0_ffn_bg, L0_ffn_We, L0_ffn_be):
    import jax
    import jax.numpy as jnp

    def _L0_tok_ref(x, conv_w, conv_b, cls_token, pos_embed, ln1_w, ln1_b, qkv_w, qkv_b, proj_w, proj_b, ln2_w, ln2_b, fc1_w, fc1_b, fc2_w, fc2_b, norm_w, norm_b):
        import jax, jax.numpy as jnp
        import numpy as np
        DEPTH = 4
        HEADS = 8
        DIM = 128
        HID = 256
        P = 16
        IMG = 224
        GRID = IMG // P
        NPATCH = GRID * GRID
        NTOK = NPATCH + 1
        BATCH = 64
        EPS = 1e-05

        def layernorm(x, w, b):
            mu = jnp.mean(x, axis=-1, keepdims=True)
            var = jnp.mean(jnp.square(x - mu), axis=-1, keepdims=True)
            return (x - mu) * jax.lax.rsqrt(var + EPS) * w + b
        B = x.shape[0]
        hd = DIM // HEADS
        scale = hd ** (-0.5)
        patches = x.reshape(B, 3, GRID, P, GRID, P)
        patches = patches.transpose(0, 2, 4, 1, 3, 5).reshape(B, NPATCH, 3 * P * P)
        tok = patches @ conv_w + conv_b
        cls = jnp.broadcast_to(cls_token, (B, 1, DIM))
        h = jnp.concatenate([cls, tok], axis=1) + pos_embed
        for i in range(DEPTH):
            y = layernorm(h, ln1_w[i], ln1_b[i])
            qkv = (y @ qkv_w[i] + qkv_b[i]).reshape(B, NTOK, 3, HEADS, hd)
            qkv = qkv.transpose(2, 0, 3, 1, 4)
            q, k, v = (qkv[0], qkv[1], qkv[2])
            attn = jax.nn.softmax(jnp.einsum('bhnd,bhmd->bhnm', q, k) * scale, axis=-1)
            o = jnp.einsum('bhnm,bhmd->bhnd', attn, v)
            o = o.transpose(0, 2, 1, 3).reshape(B, NTOK, DIM)
            h = h + (o @ proj_w[i] + proj_b[i])
            y = layernorm(h, ln2_w[i], ln2_b[i])
            y = jax.nn.gelu(y @ fc1_w[i] + fc1_b[i], approximate=False)
            h = h + (y @ fc2_w[i] + fc2_b[i])
        return layernorm(h, norm_w, norm_b)

    def _L0_attn_ref(x, Wx, bx, Wfx, bfx, Wslice, bslice, Wq, Wk, Wv, Wout, bout, temperature):
        import jax, jax.numpy as jnp
        import numpy as np
        H, DH, M, DIN = (8, 64, 32, 128)
        INNER = H * DH
        B, N, D = x.shape
        scale = DH ** (-0.5)
        x_mid = (x @ Wx.T + bx).reshape(B, N, H, DH).transpose(0, 2, 1, 3)
        fx_mid = (x @ Wfx.T + bfx).reshape(B, N, H, DH).transpose(0, 2, 1, 3)
        slice_logits = (x_mid @ Wslice.T + bslice) / temperature
        slice_weights = jax.nn.softmax(slice_logits, axis=-1)
        slice_norm = slice_weights.sum(axis=2)
        slice_token = jnp.einsum('bhnd,bhnm->bhmd', fx_mid, slice_weights)
        slice_token = slice_token / (slice_norm[:, :, :, None] + 1e-05)
        q = slice_token @ Wq.T
        k = slice_token @ Wk.T
        v = slice_token @ Wv.T
        attn = jax.nn.softmax(jnp.einsum('bhmd,bhkd->bhmk', q, k) * scale, axis=-1)
        out_slice = jnp.einsum('bhmk,bhkd->bhmd', attn, v)
        out_x = jnp.einsum('bhmd,bhnm->bhnd', out_slice, slice_weights)
        out_x = out_x.transpose(0, 2, 1, 3).reshape(B, N, INNER)
        return out_x @ Wout.T + bout

    def _L0_ffn_ref(x, Wg, bg, We, be):
        import jax, jax.numpy as jnp
        import numpy as np
        B, S, D, E, O = (256, 64, 128, 16, 128)
        scores = jax.nn.softmax(jnp.mean(x, axis=1) @ Wg + bg, axis=-1)
        idx = jnp.argmax(scores, axis=-1)
        gate = jnp.take_along_axis(scores, idx[:, None], axis=-1)
        W_sel = We[idx]
        b_sel = be[idx]
        y = jnp.einsum('bsd,bdo->bso', x, W_sel) + b_sel[:, None, :]
        return gate[:, :, None] * y
    h = _L0_tok_ref(x, L0_tok_conv_w, L0_tok_conv_b, L0_tok_cls_token, L0_tok_pos_embed, L0_tok_ln1_w, L0_tok_ln1_b, L0_tok_qkv_w, L0_tok_qkv_b, L0_tok_proj_w, L0_tok_proj_b, L0_tok_ln2_w, L0_tok_ln2_b, L0_tok_fc1_w, L0_tok_fc1_b, L0_tok_fc2_w, L0_tok_fc2_b, L0_tok_norm_w, L0_tok_norm_b)
    h = jnp.concatenate([jnp.broadcast_to(cls_tok, (h.shape[0], 1, h.shape[2])), h], axis=1)
    h = h + _L0_attn_ref(_layernorm(h, axis=-1), L0_attn_Wx, L0_attn_bx, L0_attn_Wfx, L0_attn_bfx, L0_attn_Wslice, L0_attn_bslice, L0_attn_Wq, L0_attn_Wk, L0_attn_Wv, L0_attn_Wout, L0_attn_bout, L0_attn_temperature)
    h = h + _L0_ffn_ref(_layernorm(h, axis=-1), L0_ffn_Wg, L0_ffn_bg, L0_ffn_We, L0_ffn_be)
    return h

_drawn_inputs = setup_inputs


def setup_inputs(seed=0):
    import zlib

    import numpy as np

    out = dict(_drawn_inputs(seed))
    spreads = {'L0_tok_conv_b': (0.0, 0.1),
     'L0_tok_ln1_w': (1.0, 0.552),
     'L0_tok_ln1_b': (0.0, 0.296),
     'L0_tok_qkv_b': (0.0, 0.1),
     'L0_tok_proj_b': (0.0, 0.1),
     'L0_tok_ln2_w': (1.0, 0.2),
     'L0_tok_ln2_b': (0.0, 0.343),
     'L0_tok_fc1_b': (0.0, 0.1),
     'L0_tok_fc2_b': (0.0, 0.1),
     'L0_tok_norm_w': (1.0, 0.2),
     'L0_tok_norm_b': (0.0, 0.1),
     'L0_attn_bx': (0.0, 2.0),
     'L0_attn_bfx': (0.0, 0.528),
     'L0_attn_bslice': (0.0, 2.0),
     'L0_attn_bout': (0.0, 0.1),
     'L0_attn_temperature': (0.5, 0.6)}
    factors = {'cls_tok': 18.454,
     'L0_tok_cls_token': 8.0,
     'L0_attn_Wx': 8.0,
     'L0_attn_Wfx': 3.487,
     'L0_attn_Wslice': 8.0,
     'L0_attn_Wq': 21.803,
     'L0_attn_Wk': 23.652,
     'L0_attn_Wout': 2.839,
     'L0_ffn_be': 8.0}
    for name, (base, spread) in spreads.items():
        noise = np.random.default_rng([zlib.crc32(name.encode()), seed]).standard_normal(out[name].shape)
        drawn = base * np.exp(spread * noise) if base else spread * noise
        out[name] = jnp.asarray(drawn.astype(out[name].dtype))
    for name, factor in factors.items():
        out[name] = (out[name] * factor).astype(out[name].dtype)
    return out
```

```python
import concourse.bass as bass
from concourse import mybir
from contextlib import ExitStack


def vit_slice_moe(nc, D, out):
    f32 = mybir.dt.float32
    f32r = mybir.dt.float32r
    i32 = mybir.dt.int32
    ALU = mybir.AluOpType
    ACT = mybir.ActivationFunctionType
    AX = mybir.AxisListType
    ds = bass.ds

    IMGS, _, KCH, NPATCH = D["patches"].shape
    LAYERS = D["qkv_w"].shape[0]
    DIM = 128
    HEADS = 8
    HD = DIM // HEADS
    TT = 99
    NT = 2 * TT
    VT = NT - 1
    R_CLS = NPATCH - TT
    R_OUT = R_CLS + 1
    NPAIR = IMGS // 2
    W2 = 2 * NT
    HID = D["fc1_w"].shape[2]
    EPS = 1e-5
    SCALE = float(HD) ** -0.5
    NBUF = 4
    START = 16

    ctx = ExitStack()
    with ctx:
        def sb(name, shape, dt=f32):
            return ctx.enter_context(nc.sbuf_tensor(name, shape, dt))

        def sem(name):
            return ctx.enter_context(nc.semaphore(name))

        H = sb("H", [TT, 2 * IMGS, DIM])
        ident = sb("ident", [128, 128])
        z = sb("z", [TT, 4, DIM])
        yT = sb("yT", [128, W2])
        bnst = sb("bnst", [TT, 4, 6])
        mv = sb("mv", [TT, 4, 2])
        ve = sb("ve", [TT, 4])
        rstd = sb("rstd", [TT, 4])
        half = sb("half", [TT, 4])
        spare = sb("spare", [1, 1])
        spare2 = sb("spare2", [1, 1])

        tower = ExitStack()

        def tb(name, shape, dt=f32):
            return tower.enter_context(nc.sbuf_tensor(name, shape, dt))

        U = tb("U", [128, NBUF * KCH * NPATCH])
        patch = U[:, :].rearrange("p (n c t) -> p n c t", n=NBUF, c=KCH)
        NV = 2 * 4 * HEADS * 32
        Vx = U[0:TT, 0:NV].rearrange("p (b t h e) -> p b t h e", b=2, t=4, h=HEADS)
        PT = U[0:TT, NV:NV + 4 * W2].rearrange("p (r c) -> p r c", r=4)
        gT = U[:, NV:NV + 4 * W2].rearrange("p (b c n) -> p b c n", b=2, c=2)
        qs = tb("qs", [128, 2, 4, W2], f32r)
        ks = tb("ks", [128, 2, HEADS, W2], f32r)
        qhi = tb("qhi", [128, W2], f32r)
        qlo = tb("qlo", [128, W2], f32r)
        khi = tb("khi", [128, W2], f32r)
        klo = tb("klo", [128, W2], f32r)
        oraw = tb("oraw", [128, W2])
        on = tb("on", [TT, 2, DIM])
        onT = tb("onT", [128, NT])
        mx = tb("mx", [TT, 2, HEADS])
        M2 = tb("M2", [TT, 2, 4, 32])
        rec = tb("rec", [TT, 2 * HEADS])
        mcols = tb("mcols", [128, 4])
        selq = tb("selq", [128, 4, 2, 128], f32r)
        selk = tb("selk", [128, 4, 2, 128], f32r)
        addend = tb("addend", [TT, 2, DIM])
        rowb = tb("rowb", [TT, DIM])
        clsrow = tb("clsrow", [1, 2, DIM])
        wc = tb("wc", [128, KCH, DIM])
        wqkv = tb("wqkv", [128, 3 * DIM])
        wpj = tb("wpj", [128, DIM])
        w1 = tb("w1", [128, HID])
        w2 = tb("w2", [128, 2, DIM])
        cols = tb("cols", [128, 8])
        bvrow = tb("bvrow", [TT, DIM])
        pbrow = tb("pbrow", [TT, DIM])
        fbrow = tb("fbrow", [TT, DIM])
        tower.close()

        SH, SM, SD = 8, 32, 64
        SL = SH * SM
        wnorm = sb("wnorm", [TT, 2, DIM])
        bnorm = sb("bnorm", [TT, 2, DIM])
        wx = sb("wx", [SD, SH, DIM])
        bx = sb("bx", [SD, SH])
        bxw = sb("bxw", [SD, SH, TT])
        wslT = sb("wslT", [SD, SM])
        bsl = sb("bsl", [TT, SM])
        rtemp = sb("rtemp", [128, SH])
        wcomb = sb("wcomb", [128, SL])
        bcomb = sb("bcomb", [TT, SL])
        wfxT = sb("wfxT", [128, SH * SD])
        bfx = sb("bfx", [128, 2, SD])
        wq3 = sb("wq3", [SD, 3, SD])
        mqk = sb("mqk", [SD, SD])
        woT = sb("woT", [SD, SH, DIM])
        wvo = sb("wvo", [SD, SH, DIM])
        smask = sb("smask", [128, 128])
        borow = sb("borow", [TT, DIM])
        x1e = sb("x1e", [TT, 4, DIM + 1])
        Lw = sb("Lw", [TT, 4, SL])
        gmx = sb("gmx", [TT, 4 * SH])
        gsum = sb("gsum", [TT, 4 * SH])
        grec = sb("grec", [TT, 4 * SH])
        wT = sb("wT", [128, 2, W2])
        Tp = sb("Tp", [128, 4, DIM + 1])
        seps = sb("seps", [128, 4])
        srec = sb("srec", [128, 4])
        TpT = sb("TpT", [128, 512])
        tok = sb("tok", [128, 4, SD])
        tokT = sb("tokT", [SD, 512])
        AT = sb("AT", [SD, 512])
        Us = sb("Us", [128, 4, DIM])
        Sm = sb("Sm", [128, 4, 128])
        rmx = sb("rmx", [128, 4])
        nmx = sb("nmx", [128, 4])
        asum = sb("asum", [128, 4])
        arec = sb("arec", [128, 4])
        ET = sb("ET", [128, 512])
        Gs = sb("Gs", [128, 4, DIM])
        NE = D["be"].shape[0]
        we = sb("we", [128, NE, DIM])
        wg = sb("wg", [128, NE])
        bg = sb("bg", [IMGS, NE])
        be = sb("be", [NE, DIM])
        iota = sb("iota", [IMGS, NE])
        onec = sb("onec", [TT, 1])
        mvall = sb("mvall", [TT, 2 * IMGS])
        rall = sb("rall", [TT, 2 * IMGS])
        means = sb("means", [128, IMGS])
        lg = sb("lg", [IMGS, NE])
        top = sb("top", [IMGS, 8])
        topi = sb("topi", [IMGS, 8], mybir.dt.uint32)
        ntop = sb("ntop", [IMGS, 1])
        topf = sb("topf", [IMGS, 1])
        lge = sb("lge", [IMGS, NE])
        lsum = sb("lsum", [IMGS, 1])
        gate = sb("gate", [IMGS, 1])
        onehot = sb("onehot", [IMGS, NE])
        onehotT = sb("onehotT", [NE, IMGS])
        gbe = sb("gbe", [IMGS, DIM])
        gateb = sb("gateb", [TT, IMGS])
        idxrow = sb("idxrow", [1, IMGS], mybir.dt.uint32)
        GB = sb("GB", [TT, 2, 2, DIM])
        OB = sb("OB", [TT, 2, 4, DIM])
        zT = sb("zT", [128, 2, W2])

        gate_d = nc.dram_tensor("gate_d", [1, IMGS], f32).ap()
        idx_d = nc.dram_tensor("idx_d", [1, IMGS], mybir.dt.uint32).ap()
        gbe_d = nc.dram_tensor("gbe_d", [IMGS, DIM], f32).ap()
        ps = ctx.enter_context(nc.psum_tensor("ps", [128, 8, 512], f32))
        S_BANK, T_BANK, O_BANK, P_BANK, R_BANK = 0, 2, 4, 5, 7

        c_in = sem("c_in")
        c_rows = sem("c_rows")
        p_in = [sem(f"p_in{i}") for i in range(NBUF)]
        wa_in = sem("wa_in")
        wb_in = sem("wb_in")
        init_done = sem("init_done")
        sel_cast = sem("sel_cast")
        add_ready = sem("add_ready")
        emb_done = sem("emb_done")
        vone_ready = sem("vone_ready")
        start_names = ("bn agg ve pw z tr yT q qhi qlo k khi klo v V sel selev hb "
                       "embu s smax mhi m2 nm nmq st ex pv oraw ot rec on t2 onT pj hA "
                       "Bbn Bagg Bve Bpw Bz Btr ByT Bf1 Bg Bf2 Bhb hB").split()
        X = {n: sem(n + "_n") for n in start_names}
        bn, agg, ves, pw, zs, tr, yTs, qd, qhis, qlos, kd, khis, klos, vd, Vs, seld, selev, hb = [X[n] for n in start_names[:18]]
        sd, smax, mhi, m2s, nm, nmq, st, ex, pv, oraws, ot, recs, ons, t2, onTs, pj, hA = [X[n] for n in start_names[19:36]]
        embu = X["embu"]
        Bbn, Bagg, Bve, Bpw, Bz, Btr, ByT, Bf1, Bg, Bf2, Bhb, hB = [X[n] for n in start_names[36:]]
        cn = ("Fbn Fagg Fve Fpw Fz F1 F2 Cbn Cagg Cve Cpw Cz Ctr CxT Clg CL Cmx Csub Cex Csum Crc Cw CT Cse Csr CTp CTt CTe "
              "Cwt Cwe Ctk Ctok Ctt Cte CA CAe CU CUe CS CSm CSr CSx CSe CEt CEe Cr2 CG CGe CO Chb CH "
              "Gbn Gagg Gve Gpw Gz Gm Egb Egl Ehb Ez Etr EzT Ey Eo").split()
        X.update({n: sem(n + "_n") for n in cn})
        (Fbn, Fagg, Fve, Fpw, Fz, F1, F2, Cbn, Cagg, Cve, Cpw, Cz, Ctr, CxT, Clg, CL, Cmx, Csub, Cex, Csum, Crc, Cw, CT, Cse, Csr,
         CTp, CTt, CTe, Cwt, Cwe, Ctk, Ctok, Ctt, Cte, CA, CAe, CU, CUe, CS, CSm, CSr, CSx, CSe, CEt, CEe, Cr2, CG, CGe, CO, Chb, CH,
         Gbn, Gagg, Gve, Gpw, Gz, Gm, Egb, Egl, Ehb, Ez, Etr, EzT, Ey, Eo) = [X[n] for n in cn]
        w_in = sem("w_in")
        w_pe = sem("w_pe")
        w_dv = sem("w_dv")
        w_pl = sem("w_pl")
        g_pe = sem("g_pe")
        g_dv = sem("g_dv")
        g_act = sem("g_act")
        g_out = sem("g_out")
        g_in = sem("g_in")
        gb_in = [sem(f"gb_in{i}") for i in range(2)]
        o_out = [sem(f"o_out{i}") for i in range(2)]

        block = ctx.enter_context(nc.Block())

        def bank(i, rows, cols_):
            return ps[0:rows, i, 0:cols_]

        @block.sync
        def _(sp):
            sp.dma_start(ident[:, :], D["ident"]).then_inc(c_in, 16)
            sp.dma_start(mcols[:, :], D["mcols"]).then_inc(c_in, 16)
            sp.dma_start(U[:, 1024:2048], D["selq"]).then_inc(c_in, 16)
            sp.dma_start(U[:, 0:1024], D["selk"]).then_inc(c_in, 16)
            sp.dma_start(wc[:, :, :], D["conv_w"].rearrange("(c p) n -> p c n", p=128)).then_inc(c_in, 16)
            sp.dma_start(addend[:, 0, :], D["pos"][1:1 + TT, :]).then_inc(c_in, 16)
            sp.dma_start(addend[0:R_CLS, 1, :], D["pos"][1 + TT:1 + NPATCH, :]).then_inc(c_in, 16)
            sp.dma_start(rowb[:, :], D["conv_b_row"].to_broadcast([TT, DIM])).then_inc(c_in, 16)
            sp.dma_start(clsrow[:, 0, :], D["cls_token"]).then_inc(c_in, 16)
            sp.dma_start(clsrow[:, 1, :], D["pos"][0:1, :]).then_inc(c_in, 16)

            sp.wait_ge(sel_cast, 2)
            for b in range(NBUF):
                sp.dma_start(U[:, b * KCH * NPATCH:(b + 1) * KCH * NPATCH],
                             D["patches"][b].rearrange("p c t -> p (c t)")).then_inc(p_in[b], 16)
            sp.wait_ge(add_ready, 2)
            odd = H[:, :, :].rearrange("p (n two) d -> p n two d", two=2)
            sp.dma_start(odd[R_CLS:R_CLS + 1, :, 1, :], clsrow[:, 0:1, :].to_broadcast([1, IMGS, DIM])).then_inc(c_rows, 16)
            sp.dma_start(odd[R_OUT:R_OUT + 1, :, 1, :], D["cls_tok"].unsqueeze(1).to_broadcast([1, IMGS, DIM])).then_inc(c_rows, 16)
            with sp.Fori(1, IMGS // NBUF) as it:
                for b in range(NBUF):
                    sp.wait_ge(emb_done, it * NBUF + (b - NBUF + 1))
                    sp.dma_start(U[:, b * KCH * NPATCH:(b + 1) * KCH * NPATCH],
                                 D["patches"][ds(it * NBUF + b, 1)].rearrange("a p c t -> (a p) (c t)")).then_inc(p_in[b], 16)

            with sp.Fori(0, LAYERS) as L:
                lay = lambda name: D[name][ds(L, 1)].rearrange("a p n -> (a p) n")
                sp.wait_ge(hA, L * IMGS + START)
                sp.dma_start(wqkv[:, :], lay("qkv_w")).then_inc(wa_in, 16)
                sp.dma_start(wpj[:, :], lay("proj_w")).then_inc(wa_in, 16)
                sp.dma_start(bvrow[:, :], lay("bv_row").to_broadcast([TT, DIM])).then_inc(wa_in, 16)
                sp.dma_start(pbrow[:, :], lay("pb_row").to_broadcast([TT, DIM])).then_inc(wa_in, 16)
                sp.wait_ge(hB, L * NPAIR + START + 1)
                sp.dma_start(cols[:, :], lay("cols")).then_inc(wa_in, 16)
                sp.dma_start(w1[:, :], lay("fc1_w")).then_inc(wb_in, 16)
                sp.dma_start(w2[:, :, :], D["fc2_w"][ds(L, 1)].rearrange("a (c p) n -> p (a c) n", p=128)).then_inc(wb_in, 16)
                sp.dma_start(fbrow[:, :], lay("fb_row").to_broadcast([TT, DIM])).then_inc(wb_in, 16)

            sp.wait_ge(hB, START + 1 + LAYERS * NPAIR)
            loads = [
                (wnorm[:, 0, :], D["norm_w_row"].to_broadcast([TT, DIM])),
                (wnorm[0:R_OUT, 1, :], D["norm_w_row"].to_broadcast([R_OUT, DIM])),
                (wnorm[R_OUT:TT, 1, :], D["zero_row"]),
                (bnorm[:, 0, :], D["norm_b_row"].to_broadcast([TT, DIM])),
                (bnorm[0:R_OUT, 1, :], D["norm_b_row"].to_broadcast([R_OUT, DIM])),
                (bnorm[R_OUT:TT, 1, :], D["cls_tok"]),
                (wx[:, :, :], D["wx"].rearrange("(h d) n -> d h n", h=SH)),
                (bx[:, :], D["bxT"]),
                (wslT[:, :], D["wslT"]),
                (bsl[:, :], D["bsl_row"].to_broadcast([TT, SM])),
                (rtemp[:, :], D["temp_row"].to_broadcast([128, SH])),
                (wfxT[:, :], D["wfxT"]),
                (bfx[:, :, :], D["bfx"]),
                (wq3[:, :, :], D["wq3"]),
                (woT[:, :, :], D["woT"]),
                (smask[:, :], D["smask"]),
                (borow[:, :], D["bo_row"].to_broadcast([TT, DIM])),
                (we[:, :, :], D["we"].rearrange("e d o -> d e o")),
                (wg[:, :], D["wg"]),
                (bg[:, :], D["bg_row"].to_broadcast([IMGS, NE])),
                (be[:, :], D["be"]),
                (iota[:, :], D["iota_row"].to_broadcast([IMGS, NE])),
            ]
            for dst, src in loads:
                sp.dma_start(dst, src).then_inc(w_in, 16)

            sp.wait_ge(g_dv, 9)
            sp.dma_start(gate_d.rearrange("a n -> n a"), gate[:, :]).then_inc(g_out, 16)
            sp.dma_start(idx_d.rearrange("a n -> n a"), topi[:, 0:1]).then_inc(g_out, 16)
            sp.dma_start(gbe_d, gbe[:, :]).then_inc(g_out, 16)
            sp.wait_ge(g_out, 48)
            sp.dma_start(gateb[:, :], gate_d.to_broadcast([TT, IMGS])).then_inc(g_in, 16)
            sp.dma_start(idxrow[:, :], idx_d).then_inc(g_in, 16)

            def load_gbe(p, b):
                sp.dma_start(GB[:, b, :, :], gbe_d[ds(p * 2, 2), :].unsqueeze(0).to_broadcast([TT, 2, DIM])).then_inc(gb_in[b], 16)

            def store(p, b):
                sp.wait_ge(Eo, START + p + 1)
                ob = OB[:, b, :, :].rearrange("p (i two) d -> p i two d", two=2)
                dst = out[ds(p * 2, 2), :, :].rearrange("i t d -> t i d")
                sp.dma_start(dst[2:2 + TT], ob[:, :, 0, :]).then_inc(o_out[b], 16)
                sp.dma_start(dst[2 + TT:NT], ob[0:R_CLS, :, 1, :]).then_inc(o_out[b], 16)
                sp.dma_start(dst[1:2], ob[R_CLS:R_CLS + 1, :, 1, :]).then_inc(o_out[b], 16)
                sp.dma_start(dst[0:1], ob[R_OUT:R_OUT + 1, :, 1, :]).then_inc(o_out[b], 16)
            with sp.Fori(0, NPAIR // 2) as r:
                for b in (0, 1):
                    p = 2 * r + b
                    sp.wait_ge(Ehb, START + p - 1)
                    load_gbe(p, b)
                    store(p, b)
            for b in range(2):
                sp.wait_ge(o_out[b], 64 * (NPAIR // 2))

        @block.gpsimd
        def _(pool):
            nc.gpsimd.memset(spare[:, :], 0.0)
            for name in X:
                pool.sem_inc(X[name], START)
            nc.gpsimd.memset(half[:, :], -0.5)
            nc.gpsimd.memset(M2[:, :, :, :], 0.0).then_inc(init_done, 1)
            pool.wait_ge(emb_done, IMGS)
            nc.gpsimd.memset(Vx[:, :, :, :, HD:32], 1.0).then_inc(vone_ready, 1)

            def attention_pair(L, gp, p):
                pool.wait_ge(ves, START + gp + 1)
                pool.wait_ge(zs, START + gp)
                nc.gpsimd.tensor_tensor(rstd[:, :], ve[:, :], half[:, :], ALU.pow).then_inc(pw, 1)
                pool.wait_ge(zs, START + gp + 1)
                pool.wait_ge(wa_in, 80 * L + 80)
                nc.gpsimd.tensor_tensor(H[:, ds(p * 4, 4), :], H[:, ds(p * 4, 4), :],
                                        pbrow[:, :].unsqueeze(1).to_broadcast([TT, 4, DIM]), ALU.add).then_inc(hb, 1)

            with pool.Fori(0, LAYERS) as L:
                with pool.Fori(0, NPAIR) as p:
                    attention_pair(L, L * NPAIR + p, p)
                with pool.Fori(0, NPAIR) as p:
                    gp = L * NPAIR + p
                    pool.wait_ge(Bve, START + gp + 1)
                    pool.wait_ge(Bz, START + gp)
                    nc.gpsimd.tensor_tensor(rstd[:, :], ve[:, :], half[:, :], ALU.pow).then_inc(Bpw, 1)
                    pool.wait_ge(Bz, START + gp + 1)
                    pool.wait_ge(wb_in, 48 * L + 48)
                    nc.gpsimd.tensor_tensor(H[:, ds(p * 4, 4), :], H[:, ds(p * 4, 4), :],
                                            fbrow[:, :].unsqueeze(1).to_broadcast([TT, 4, DIM]), ALU.add).then_inc(Bhb, 1)

            pool.wait_ge(hB, START + 1 + LAYERS * NPAIR)
            pool.wait_ge(w_in, 16 * 22)
            nc.gpsimd.memset(x1e[:, :, DIM:DIM + 1], 1.0)
            nc.gpsimd.memset(onec[:, :], 1.0).then_inc(w_pl, 1)

            def inv_std(p, s_ve, s_z, s_pw):
                pool.wait_ge(s_ve, START + p + 1)
                pool.wait_ge(s_z, START + p)
                nc.gpsimd.tensor_tensor(rstd[:, :], ve[:, :], half[:, :], ALU.pow).then_inc(s_pw, 1)

            with pool.Fori(0, NPAIR) as p:
                inv_std(p, Fve, Fz, Fpw)
                pool.wait_ge(Fz, START + p + 1)
                pool.wait_ge(F2, START + p)
                zp = z[:, :, :].rearrange("p (i t) d -> p i (t d)", i=2)
                nc.gpsimd.tensor_tensor(zp, zp, wnorm[:, :, :].rearrange("p t d -> p (t d)").unsqueeze(1)
                                        .to_broadcast([TT, 2, 2 * DIM]), ALU.mult).then_inc(F1, 1)

            def soft1(p):
                inv_std(p, Cve, Cz, Cpw)

            def soft2(p):
                pool.wait_ge(Cz, START + p + 1)
                nc.gpsimd.tensor_tensor(H[:, ds(p * 4, 4), :], H[:, ds(p * 4, 4), :],
                                        borow[:, :].unsqueeze(1).to_broadcast([TT, 4, DIM]), ALU.add).then_inc(Chb, 1)
                pool.wait_ge(Cmx, START + p + 1)
                lv = Lw[:, :, :].rearrange("p t (h m) -> p (t h) m", m=SM)
                nc.gpsimd.tensor_tensor(lv, lv, gmx[:, :].unsqueeze(2).to_broadcast([TT, 4 * SH, SM]),
                                        ALU.subtract).then_inc(Csub, 1)
                pool.wait_ge(Crc, START + p + 1)
                nc.gpsimd.tensor_tensor(lv, lv, grec[:, :].unsqueeze(2).to_broadcast([TT, 4 * SH, SM]),
                                        ALU.mult).then_inc(Cw, 1)
            with pool.Fori(0, NPAIR) as p:
                soft1(p)
                soft2(p)
            with pool.Fori(0, NPAIR) as p:
                inv_std(p, Gve, Gz, Gpw)
            with pool.Fori(0, NPAIR // 2) as r:
                for b in (0, 1):
                    p = 2 * r + b
                    pool.wait_ge(gb_in[b], 16 * r + 16)
                    pool.wait_ge(Ez, START + p + 1)
                    for i in range(2):
                        hh = H[:, ds(p * 4 + 2 * i, 2), :]
                        last = nc.gpsimd.tensor_tensor(hh, hh, GB[:, b, i:i + 1, :].to_broadcast([TT, 2, DIM]), ALU.add)
                    last.then_inc(Ehb, 1)

        @block.vector
        def _(dve):
            dve.wait_ge(init_done, 1)
            dve.wait_ge(c_in, 160)
            nc.vector.tensor_copy(selq[:, :, :, :], U[:, 1024:2048].rearrange("p (a b c) -> p a b c", a=4, b=2)).then_inc(sel_cast, 1)
            nc.vector.tensor_copy(selk[:, :, :, :], U[:, 0:1024].rearrange("p (a b c) -> p a b c", a=4, b=2)).then_inc(sel_cast, 1)
            nc.vector.tensor_tensor(clsrow[:, 0, :], clsrow[:, 0, :], clsrow[:, 1, :], ALU.add).then_inc(add_ready, 1)
            nc.vector.tensor_tensor(addend[:, 0, :], addend[:, 0, :], rowb[:, :], ALU.add)
            nc.vector.tensor_tensor(addend[0:R_CLS, 1, :], addend[0:R_CLS, 1, :], rowb[0:R_CLS, :], ALU.add).then_inc(add_ready, 1)
            dve.wait_ge(add_ready, 2)
            with dve.Fori(0, IMGS // NBUF) as it:
                for b in range(NBUF):
                    dve.wait_ge(emb_done, it * NBUF + b + 1)
                    nc.vector.tensor_tensor(H[:, ds((it * NBUF + b) * 2, 1), :], ps[0:TT, b:b + 1, 0:DIM],
                                            addend[:, 0:1, :], ALU.add)
                    nc.vector.tensor_tensor(H[0:R_CLS, ds((it * NBUF + b) * 2 + 1, 1), :], ps[0:R_CLS, b:b + 1, DIM:2 * DIM],
                                            addend[0:R_CLS, 1:2, :], ALU.add).then_inc(embu, 1)
            dve.wait_ge(embu, START + IMGS)
            dve.wait_ge(c_rows, 32)
            nc.vector.memset(spare[:, :], 0.0).then_inc(hB, 1)

            def stats(gp, p, s_bn, s_agg, s_ve, s_pw, s_z, s_tr):
                dve.wait_ge(s_z, START + gp)
                for t in range(4):
                    last = nc.vector.bn_stats(bnst[:, t, :], H[:, ds(p * 4 + t, 1), :].rearrange("p a d -> p (a d)"))
                last.then_inc(s_bn, 1)
                dve.wait_ge(s_bn, START + gp + 1)
                nc.vector.memset(spare2[:, :], 0.0)
                for t in range(4):
                    last = nc.vector.bn_aggr(mv[:, t, :], bnst[:, t, :])
                last.then_inc(s_agg, 1)
                dve.wait_ge(s_agg, START + gp + 1)
                dve.wait_ge(s_pw, START + gp)
                nc.vector.tensor_scalar(ve[:, :], mv[:, :, 1], EPS, None, ALU.add).then_inc(s_ve, 1)

            def normed(gp, p, s_pw, s_z, s_tr):
                dve.wait_ge(s_pw, START + gp + 1)
                dve.wait_ge(s_tr, START + gp)
                for t in range(4):
                    last = nc.vector.tensor_scalar(z[:, t, :], H[:, ds(p * 4 + t, 1), :].rearrange("p a d -> p (a d)"),
                                                   mv[:, t, 0:1], rstd[:, t:t + 1], ALU.subtract, ALU.mult)
                last.then_inc(s_z, 1)

            def low_parts(gp, src, bias, hi, lo, s_hi, s_sel, s_lo, selcount):
                dve.wait_ge(s_hi, START + gp + 1)
                dve.wait_ge(s_sel, selcount)
                nc.vector.scalar_tensor_tensor(out=lo[:, :], in0=src, scalar=bias, in1=hi[:, :].bitcast(f32),
                                               op0=ALU.add, op1=ALU.subtract).then_inc(s_lo, 1)

            def prep(gp, p, b, slot):
                if slot == "stats":
                    stats(gp, p, bn, agg, ves, pw, zs, tr)
                if slot == "norm":
                    normed(gp, p, pw, zs, tr)
                if slot == "qlo":
                    low_parts(gp, bank(P_BANK + 1, 128, W2), cols[:, 2:3], qhi, qlo, qhis, seld, qlos, START + 8 * gp)
                if slot == "klo":
                    low_parts(gp, bank(P_BANK, 128, W2), cols[:, 3:4], khi, klo, khis, seld, klos, START + 8 * gp)
                if slot == "V":
                    dve.wait_ge(vd, START + gp + 1)
                    dve.wait_ge(pv, START + 8 * (gp - 1))
                    for t in range(4):
                        last = nc.vector.tensor_tensor(
                            Vx[:, b, t, :, 0:HD],
                            ps[0:TT, P_BANK + 1, t * DIM:(t + 1) * DIM].rearrange("p (h d) -> p h d", h=HEADS),
                            bvrow[:, :].rearrange("p (h d) -> p h d", h=HEADS), ALU.add)
                    last.then_inc(Vs, 1)

            def period(gp, p, b, jj, S, T, O, P):
                n = gp * 2 + jj

                def smx(u):
                    if not S:
                        return
                    dve.wait_ge(sd, START + 8 * n + u + 1)
                    if u == 0:
                        dve.wait_ge(m2s, START + n)
                    t, qt = u // 2, u % 2
                    nc.vector.reduce_max(mx[:, qt, 2 * t:2 * t + 2],
                                         bank(S_BANK + u % 2, TT, W2).rearrange("p (e m) -> p e m", e=2)[:, :, 0:VT],
                                         AX.X).then_inc(smax, 1)

                def nx(slot):
                    if P:
                        prep(gp + 1, p + 1, 1 - b, slot)
                if jj == 0:
                    nx("stats")
                smx(0)
                if jj == 0:
                    nx("norm")
                smx(1)
                if O:
                    dve.wait_ge(ot, START + n - 1)
                    src = bank(R_BANK, TT, 512).rearrange("p (x e) -> p x e", e=32)
                    nc.vector.reciprocal(rec[:, :], src[:, :, HD]).then_inc(recs, 1)
                    dve.wait_ge(recs, START + n - 1)
                    dve.wait_ge(t2, START + n - 2)
                    nc.vector.tensor_tensor(on[:, :, :].rearrange("p q (x e) -> p (q x) e", e=HD), src[:, :, 0:HD],
                                            rec[:, :].unsqueeze(2).to_broadcast([TT, 2 * HEADS, HD]),
                                            ALU.mult).then_inc(ons, 1)
                smx(2)
                if jj == 0:
                    nx("qlo")
                smx(3)
                if jj == 0:
                    nx("klo")
                smx(4)
                if O:
                    dve.wait_ge(pj, START + n - 1)
                    dve.wait_ge(hb, START + gp)
                    tile0 = p * 4 + (2 * jj - 4)
                    nc.vector.tensor_tensor(H[:, ds(tile0, 2), :], H[:, ds(tile0, 2), :],
                                            bank(R_BANK, TT, 2 * DIM).rearrange("p (a d) -> p a d", a=2),
                                            ALU.add).then_inc(hA, 1)
                smx(5)
                smx(6)
                smx(7)
                if S:
                    dve.wait_ge(smax, START + 8 * n + 8)
                    dve.wait_ge(nm, START + 2 * n)
                    m2v = M2[:, :, :, :].rearrange("p q t c -> p (q t) c")
                    mxv = mx[:, :, :].rearrange("p q (t e) -> p (q t) e", e=2)
                    nc.vector.tensor_scalar(m2v[:, :, 0:4:2].bitcast(f32r), mxv, -1.0, None, ALU.mult).then_inc(mhi, 1)
                    dve.wait_ge(mhi, START + n + 1)
                    nc.vector.scalar_tensor_tensor(out=m2v[:, :, 1:4:2], in0=mxv, scalar=-1.0, in1=m2v[:, :, 0:4:2],
                                                   op0=ALU.mult, op1=ALU.subtract).then_inc(m2s, 1)
                if jj == 1:
                    nx("V")

            def alone(gp, p, b):
                for slot in ("stats", "norm", "qlo", "klo", "V"):
                    prep(gp, p, b, slot)

            with dve.Fori(0, LAYERS) as L:
                g0 = L * NPAIR
                dve.wait_ge(hB, START + g0 + 1)
                dve.wait_ge(wa_in, 80 * L + 80)
                dve.wait_ge(vone_ready, 1)
                alone(g0, 0, 0)
                period(g0, 0, 0, 0, True, False, False, True)
                period(g0, 0, 0, 1, True, True, False, True)
                with dve.Fori(0, NPAIR // 2 - 1) as r:
                    p = 2 * r + 1
                    for b in (1, 0):
                        for jj in (0, 1):
                            period(g0 + p + (1 - b), p + (1 - b), b, jj, True, True, True, True)
                for jj in (0, 1):
                    period(g0 + NPAIR - 1, NPAIR - 1, 1, jj, True, True, True, False)
                for jj in (0, 1):
                    period(g0 + NPAIR, NPAIR, 0, jj, False, jj == 0, True, False)

                dve.wait_ge(hA, START + g0 * 2 + IMGS)
                dve.wait_ge(wb_in, 48 * L + 48)

                def ln(gp, p):
                    stats(gp, p, Bbn, Bagg, Bve, Bpw, Bz, Btr)
                    normed(gp, p, Bpw, Bz, Btr)

                def resid(gp, p):
                    dve.wait_ge(Bf2, START + gp + 1)
                    dve.wait_ge(Bhb, START + gp + 1)
                    nc.vector.tensor_tensor(H[:, ds(p * 4, 4), :], H[:, ds(p * 4, 4), :],
                                            bank(4, TT, 512).rearrange("p (a d) -> p a d", a=4), ALU.add).then_inc(hB, 1)
                ln(g0, 0)
                ln(g0 + 1, 1)
                with dve.Fori(0, NPAIR - 2) as p:
                    ln(g0 + p + 2, p + 2)
                    resid(g0 + p, p)
                resid(g0 + NPAIR - 2, NPAIR - 2)
                resid(g0 + NPAIR - 1, NPAIR - 1)

            dve.wait_ge(hB, START + 1 + LAYERS * NPAIR)
            dve.wait_ge(w_in, 16 * 22)
            dve.wait_ge(w_pl, 1)

            def norm_out(p, dst, s_pw, s_z):
                dve.wait_ge(s_pw, START + p + 1)
                for t in range(4):
                    last = nc.vector.tensor_scalar(dst[:, t, 0:DIM], H[:, ds(p * 4 + t, 1), :].rearrange("p a d -> p (a d)"),
                                                   mv[:, t, 0:1], rstd[:, t:t + 1], ALU.subtract, ALU.mult)
                last.then_inc(s_z, 1)
            with dve.Fori(0, NPAIR) as p:
                dve.wait_ge(F2, START + p)
                stats(p, p, Fbn, Fagg, Fve, Fpw, Fz, None)
                norm_out(p, z, Fpw, Fz)
                dve.wait_ge(F1, START + p + 1)
                hp = H[:, ds(p * 4, 4), :].rearrange("p (i t) d -> p i (t d)", i=2)
                nc.vector.tensor_tensor(hp, z[:, :, :].rearrange("p (i t) d -> p i (t d)", i=2),
                                        bnorm[:, :, :].rearrange("p t d -> p (t d)").unsqueeze(1)
                                        .to_broadcast([TT, 2, 2 * DIM]), ALU.add).then_inc(F2, 1)
            dve.wait_ge(F2, START + NPAIR)

            nc.vector.reciprocal(rtemp[:, :], rtemp[:, :])
            nc.vector.tensor_copy(bxw[:, :, :], bx[:, :].unsqueeze(2).to_broadcast([SD, SH, TT])).then_inc(w_dv, 1)
            dve.wait_ge(w_dv, 1)
            dve.wait_ge(w_pe, 1)
            nc.vector.tensor_tensor(wcomb[:, :].rearrange("p (h m) -> p h m", m=SM),
                                    bank(0, 128, SL).rearrange("p (h m) -> p h m", m=SM),
                                    rtemp[:, :].unsqueeze(2).to_broadcast([128, SH, SM]), ALU.mult)
            nc.vector.tensor_tensor(bcomb[:, :].rearrange("p (h m) -> p h m", m=SM),
                                    bank(1, TT, SL).rearrange("p (h m) -> p h m", m=SM),
                                    bsl[:, :].unsqueeze(1).to_broadcast([TT, SH, SM]), ALU.add)
            nc.vector.tensor_copy(mqk[:, :], bank(2, SD, SD))
            nc.vector.tensor_copy(wvo[:, 0:4, :], bank(3, SD, 512).rearrange("p (h n) -> p h n", n=DIM))
            nc.vector.tensor_copy(wvo[:, 4:8, :], bank(4, SD, 512).rearrange("p (h n) -> p h n", n=DIM)).then_inc(w_dv, 1)
            dve.wait_ge(w_dv, 2)
            nc.vector.tensor_tensor(bcomb[:, :].rearrange("p (h m) -> p h m", m=SM),
                                    bcomb[:, :].rearrange("p (h m) -> p h m", m=SM),
                                    rtemp[0:TT, :].unsqueeze(2).to_broadcast([TT, SH, SM]), ALU.mult).then_inc(w_dv, 1)
            dve.wait_ge(w_dv, 3)

            lv = Lw[:, :, :].rearrange("p t (h m) -> p (t h) m", m=SM)

            def first_a(p):
                stats(p, p, Cbn, Cagg, Cve, Cpw, Cz, None)

            def first_b(p):
                dve.wait_ge(Ctr, START + p)
                dve.wait_ge(CT, START + p)
                norm_out(p, x1e, Cpw, Cz)

            def first_c(p):
                dve.wait_ge(Clg, START + p + 1)
                dve.wait_ge(Cwt, START + p)
                dve.wait_ge(CT, START + p)
                nc.vector.tensor_tensor(Lw[:, :, :], ps[0:TT, 1:3, :].rearrange("p b (t n) -> p (b t) n", n=SL),
                                        bcomb[:, :].unsqueeze(1).to_broadcast([TT, 4, SL]), ALU.add).then_inc(CL, 1)
                dve.wait_ge(CL, START + p + 1)
                dve.wait_ge(Csub, START + p)
                nc.vector.reduce_max(gmx[:, :], lv, AX.X).then_inc(Cmx, 1)

            def first_d(p):
                dve.wait_ge(Cex, START + p + 1)
                nc.vector.reduce_sum(gsum[:, :], lv, AX.X).then_inc(Csum, 1)
                dve.wait_ge(Csum, START + p + 1)
                dve.wait_ge(Cw, START + p)
                nc.vector.reciprocal(grec[:, :], gsum[:, :]).then_inc(Crc, 1)

            def second_a(p):
                dve.wait_ge(CT, START + p + 1)
                tv = ps[:, 3:5, 0:2 * (DIM + 1)].rearrange("p b (c n) -> p b c n", n=DIM + 1)
                nc.vector.tensor_scalar(seps[:, :].rearrange("p (b c) -> p b c", b=2), tv[:, :, :, DIM], 1e-5, None,
                                        ALU.add).then_inc(Cse, 1)
                dve.wait_ge(Cse, START + p + 1)
                nc.vector.reciprocal(srec[:, :], seps[:, :]).then_inc(Csr, 1)
                dve.wait_ge(Csr, START + p + 1)
                dve.wait_ge(CTt, START + p)
                dve.wait_ge(Ctok, START + p)
                nc.vector.tensor_tensor(Tp[:, :, :].rearrange("p (b c) n -> p b c n", b=2), tv,
                                        srec[:, :].rearrange("p (b c) -> p b c", b=2).unsqueeze(3)
                                        .to_broadcast([128, 2, 2, DIM + 1]), ALU.mult).then_inc(CTp, 1)

            def second_b(p):
                dve.wait_ge(Ctk, START + p + 1)
                dve.wait_ge(Ctt, START + p)
                for k in range(4):
                    last = nc.vector.scalar_tensor_tensor(out=tok[:, k, :], in0=bfx[:, k % 2, :], scalar=Tp[:, k, DIM:DIM + 1],
                                                          in1=ps[:, 3, k * SD:(k + 1) * SD], op0=ALU.mult, op1=ALU.add)
                last.then_inc(Ctok, 1)

            def second_c(p):
                dve.wait_ge(CS, START + p + 1)
                dve.wait_ge(CEt, START + p)
                nc.vector.tensor_tensor(Sm[:, :, :], bank(4, 128, 512).rearrange("p (k n) -> p k n", k=4),
                                        smask[:, :].unsqueeze(1).to_broadcast([128, 4, 128]), ALU.add).then_inc(CSm, 1)
                dve.wait_ge(CSm, START + p + 1)
                nc.vector.reduce_max(rmx[:, :], Sm[:, :, :], AX.X).then_inc(CSr, 1)
                dve.wait_ge(CSr, START + p + 1)
                nc.vector.tensor_scalar(nmx[:, :], rmx[:, :], -(float(SD) ** -0.5), None, ALU.mult).then_inc(CSx, 1)

            def second_d(p):
                dve.wait_ge(CSe, START + p + 1)
                nc.vector.reciprocal(arec[:, :], asum[:, :]).then_inc(Cr2, 1)
                dve.wait_ge(Cr2, START + p + 1)
                dve.wait_ge(CG, START + p + 1)
                dve.wait_ge(CO, START + p)
                nc.vector.tensor_tensor(Gs[:, :, :], bank(4, 128, 512).rearrange("p (k n) -> p k n", k=4),
                                        arec[:, :].unsqueeze(2).to_broadcast([128, 4, DIM]), ALU.mult).then_inc(CGe, 1)

            def second_e(p):
                dve.wait_ge(CO, START + p + 1)
                dve.wait_ge(Chb, START + p + 1)
                nc.vector.tensor_tensor(H[:, ds(p * 4, 4), :], H[:, ds(p * 4, 4), :],
                                        bank(5, TT, 512).rearrange("p (a d) -> p a d", a=4), ALU.add).then_inc(CH, 1)

            def slice_pair(p, more):
                if more:
                    first_a(p + 1)
                second_a(p)
                if more:
                    first_b(p + 1)
                second_b(p)
                if more:
                    first_c(p + 1)
                second_c(p)
                if more:
                    first_d(p + 1)
                second_d(p)
                second_e(p)
            first_a(0)
            first_b(0)
            first_c(0)
            first_d(0)
            with dve.Fori(0, NPAIR - 1) as p:
                slice_pair(p, True)
            slice_pair(NPAIR - 1, False)
            dve.wait_ge(CH, START + NPAIR)

            with dve.Fori(0, NPAIR) as p:
                stats(p, p, Gbn, Gagg, Gve, Gpw, Gz, None)
                dve.wait_ge(Gpw, START + p + 1)
                dve.wait_ge(Gm, START + p)
                for t in range(4):
                    nc.vector.tensor_scalar(z[:, t, :], H[:, ds(p * 4 + t, 1), :].rearrange("p a d -> p (a d)"),
                                            mv[:, t, 0:1], rstd[:, t:t + 1], ALU.subtract, ALU.mult)
                nc.vector.tensor_copy(mvall[:, ds(p * 4, 4)], mv[:, :, 0])
                nc.vector.tensor_copy(rall[:, ds(p * 4, 4)], rstd[:, :]).then_inc(Gz, 1)
            dve.wait_ge(g_pe, 1)
            nc.vector.tensor_scalar(means[:, :], bank(0, 128, IMGS), 1.0 / NT, None, ALU.mult).then_inc(g_dv, 1)
            dve.wait_ge(g_pe, 2)
            nc.vector.tensor_tensor(lg[:, :], bank(1, IMGS, NE), bg[:, :], ALU.add).then_inc(g_dv, 1)
            dve.wait_ge(g_dv, 2)
            nc.vector.max(top[:, :], lg[:, :]).then_inc(g_dv, 1)
            dve.wait_ge(g_dv, 3)
            nc.vector.max_index(topi[:, :], top[:, :], lg[:, :])
            nc.vector.tensor_scalar(ntop[:, :], top[:, 0:1], -1.0, None, ALU.mult).then_inc(g_dv, 1)
            dve.wait_ge(g_dv, 4)
            nc.vector.tensor_copy(topf[:, :], topi[:, 0:1]).then_inc(g_dv, 1)
            dve.wait_ge(g_act, 1)
            nc.vector.reciprocal(gate[:, :], lsum[:, :]).then_inc(g_dv, 1)
            dve.wait_ge(g_dv, 6)
            nc.vector.tensor_scalar(onehot[:, :], iota[:, :], topf[:, :], gate[:, :], ALU.is_equal, ALU.mult).then_inc(g_dv, 1)
            dve.wait_ge(g_pe, 3)
            nc.vector.tensor_copy(onehotT[:, :], bank(2, NE, IMGS)).then_inc(g_dv, 1)
            dve.wait_ge(g_pe, 4)
            nc.vector.tensor_copy(gbe[:, :], bank(3, IMGS, DIM)).then_inc(g_dv, 1)

            dve.wait_ge(g_in, 32)

            def renorm(p):
                dve.wait_ge(Etr, START + p)
                for t in range(4):
                    last = nc.vector.tensor_scalar(z[:, t, :], H[:, ds(p * 4 + t, 1), :].rearrange("p a d -> p (a d)"),
                                                   mvall[:, ds(p * 4 + t, 1)], rall[:, ds(p * 4 + t, 1)],
                                                   ALU.subtract, ALU.mult)
                last.then_inc(Ez, 1)

            def gated(p, b):
                dve.wait_ge(Ey, START + p + 1)
                dve.wait_ge(Ehb, START + p + 1)
                if b is not None:
                    dve.wait_ge(o_out[b], 64 * (p_half(p, b)))
                for i in range(2):
                    last = nc.vector.scalar_tensor_tensor(
                        out=OB[:, b, 2 * i:2 * i + 2, :], in0=ps[0:TT, 2 + b, 2 * i * DIM:(2 * i + 2) * DIM].rearrange("p (t d) -> p t d", t=2),
                        scalar=gateb[:, ds(p * 2 + i, 1)], in1=H[:, ds(p * 4 + 2 * i, 2), :],
                        op0=ALU.mult, op1=ALU.add)
                last.then_inc(Eo, 1)
            renorm(0)
            with dve.Fori(0, NPAIR // 2 - 1) as r:
                for b in (0, 1):
                    p = 2 * r + b
                    renorm(p + 1)
                    p_half = lambda p, b: r
                    gated(p, b)
            renorm(NPAIR - 1)
            p_half = lambda p, b: NPAIR // 2 - 1
            gated(NPAIR - 2, 0)
            gated(NPAIR - 1, 1)

        @block.scalar
        def _(act):
            act.wait_ge(init_done, 1)
            act.wait_ge(c_in, 160)

            def prep(gp, b, slot):
                if slot == "yT":
                    act.wait_ge(tr, START + gp + 1)
                    act.wait_ge(vd, START + gp)
                    nc.scalar.activation(yT[:, :], bank(P_BANK, 128, W2), ACT.Identity,
                                         bias=cols[:, 1:2], scale=cols[:, 0:1]).then_inc(yTs, 1)
                if slot == "qhi":
                    act.wait_ge(qd, START + gp + 1)
                    act.wait_ge(seld, START + 8 * gp)
                    nc.scalar.activation(qhi[:, :], bank(P_BANK + 1, 128, W2), ACT.Identity,
                                         bias=cols[:, 2:3]).then_inc(qhis, 1)
                if slot == "khi":
                    act.wait_ge(kd, START + gp + 1)
                    act.wait_ge(seld, START + 8 * gp)
                    nc.scalar.activation(khi[:, :], bank(P_BANK, 128, W2), ACT.Identity,
                                         bias=cols[:, 3:4]).then_inc(khis, 1)
                if isinstance(slot, int):
                    s = slot
                    act.wait_ge(seld, START + 8 * gp + s + 1)
                    src = bank(P_BANK + 1 - s % 2, 128, W2)
                    if s == 0:
                        act.wait_ge(st, START + 16 * (gp - 1))
                    if s < 4:
                        nc.scalar.activation(qs[:, b, s, :], src, ACT.Identity).then_inc(selev, 1)
                    else:
                        h = 2 * (s - 4)
                        nc.scalar.activation(ks[:, b, h, :], src, ACT.Identity, bias=mcols[:, 2:3], scale=mcols[:, 0:1])
                        nc.scalar.activation(ks[:, b, h + 1, :], src, ACT.Identity, bias=mcols[:, 3:4],
                                             scale=mcols[:, 1:2]).then_inc(selev, 1)

            def period(gp, b, jj, S, T, O, P):
                n = gp * 2 + jj
                s_img = n - 1
                sb_, sj = (1 - b, 1) if jj == 0 else (b, 0)

                def nx(j, slot):
                    if P and j == jj:
                        prep(gp + 1, 1 - b, slot)

                def negmax(hf):
                    if T:
                        act.wait_ge(nm, START + 2 * s_img + hf + 1)
                        nc.scalar.activation(qs[96:128, sb_, 2 * hf:2 * hf + 2, sj * NT:(sj + 1) * NT],
                                             ps[96:128, R_BANK, 0:W2].rearrange("p (t c) -> p t c", t=2),
                                             ACT.Identity).then_inc(nmq, 1)

                def expo(v):
                    if T:
                        act.wait_ge(st, START + 8 * s_img + v + 1)
                        if v % 2 == 0:
                            act.wait_ge(pv, START + 4 * s_img + v // 2 - 1)
                        nc.scalar.activation(PT[:, v % 4, :], bank(T_BANK + v % 2, TT, W2), ACT.Exp,
                                             scale=SCALE).then_inc(ex, 1)
                negmax(0)
                nx(0, "yT")
                nx(1, 2)
                if O:
                    act.wait_ge(pv, START + 4 * (n - 2) + 4)
                    act.wait_ge(ot, START + n - 2)
                    nc.scalar.activation(oraw[:, :], bank(O_BANK, 128, W2), ACT.Identity).then_inc(oraws, 1)
                negmax(1)
                nx(1, 3)
                expo(0)
                nx(0, "qhi")
                nx(1, 4)
                expo(1)
                nx(0, "khi")
                if O:
                    act.wait_ge(t2, START + n - 1)
                    act.wait_ge(pj, START + n - 2)
                    nc.scalar.activation(onT[:, :], bank(R_BANK, 128, NT), ACT.Identity).then_inc(onTs, 1)
                expo(2)
                nx(1, 5)
                expo(3)
                nx(1, 6)
                expo(4)
                nx(1, 7)
                expo(5)
                expo(6)
                expo(7)
                nx(0, 0)
                nx(0, 1)

            with act.Fori(0, LAYERS) as L:
                g0 = L * NPAIR
                act.wait_ge(wa_in, 80 * L + 80)
                act.wait_ge(vone_ready, 1)
                for slot in ("yT", "qhi", "khi", 0, 1, 2, 3, 4, 5, 6, 7):
                    prep(g0, 0, slot)
                period(g0, 0, 0, True, False, False, True)
                period(g0, 0, 1, True, True, False, True)
                with act.Fori(0, NPAIR // 2 - 1) as r:
                    p = 2 * r + 1
                    for b in (1, 0):
                        for jj in (0, 1):
                            period(g0 + p + (1 - b), b, jj, True, True, True, True)
                for jj in (0, 1):
                    period(g0 + NPAIR - 1, 1, jj, True, True, True, False)
                for jj in (0, 1):
                    period(g0 + NPAIR, 0, jj, False, jj == 0, True, False)

                act.wait_ge(wb_in, 48 * L + 48)

                def yTb(gp):
                    act.wait_ge(Btr, START + gp + 1)
                    act.wait_ge(Bf1, START + 2 * gp)
                    nc.scalar.activation(yT[:, :], bank(0, 128, W2), ACT.Identity,
                                         bias=cols[:, 5:6], scale=cols[:, 4:5]).then_inc(ByT, 1)

                def gelu(gp, b):
                    for c in range(2):
                        act.wait_ge(Bf1, START + 2 * gp + c + 1)
                        if c == 0:
                            act.wait_ge(Bf2, START + gp - 1)
                        nc.scalar.activation(gT[:, b, c, :], bank(2 + c, 128, W2), ACT.Gelu,
                                             bias=cols[:, 6 + c:7 + c]).then_inc(Bg, 1)
                yTb(g0)
                with act.Fori(0, NPAIR // 2 - 1) as r:
                    p = 2 * r
                    for b in (0, 1):
                        gelu(g0 + p + b, b)
                        yTb(g0 + p + b + 1)
                gelu(g0 + NPAIR - 2, 0)
                yTb(g0 + NPAIR - 1)
                gelu(g0 + NPAIR - 1, 1)

            act.wait_ge(w_dv, 3)
            act.wait_ge(hB, START + 1 + LAYERS * NPAIR)

            def first_x(p):
                act.wait_ge(Ctr, START + p + 1)
                act.wait_ge(Clg, START + p)
                nc.scalar.activation(yT[:, :], bank(0, 128, W2), ACT.Copy).then_inc(CxT, 1)

            def first_e(p):
                act.wait_ge(Csub, START + p + 1)
                nc.scalar.activation(Lw[:, :, :], Lw[:, :, :], ACT.Exp).then_inc(Cex, 1)

            def slice_pair(p, more):
                act.wait_ge(Cwt, START + p + 1)
                act.wait_ge(CO, START + p)
                nc.scalar.activation(wT[:, :, :], ps[:, 6:8, 0:W2], ACT.Copy).then_inc(Cwe, 1)
                if more:
                    first_x(p + 1)
                act.wait_ge(CTt, START + p + 1)
                act.wait_ge(Ctk, START + p)
                nc.scalar.activation(TpT[:, :], bank(5, 128, 512), ACT.Copy).then_inc(CTe, 1)
                act.wait_ge(Ctt, START + p + 1)
                act.wait_ge(CS, START + p)
                nc.scalar.activation(tokT[:, :], bank(4, SD, 512), ACT.Copy).then_inc(Cte, 1)
                act.wait_ge(CA, START + p + 1)
                nc.scalar.activation(AT[:, :], bank(3, SD, 512), ACT.Copy).then_inc(CAe, 1)
                act.wait_ge(CU, START + p + 1)
                act.wait_ge(CG, START + p)
                nc.scalar.activation(Us[:, :, :], bank(5, 128, 512).rearrange("p (k n) -> p k n", k=4), ACT.Copy).then_inc(CUe, 1)
                if more:
                    first_e(p + 1)
                act.wait_ge(CSx, START + p + 1)
                act.wait_ge(Cr2, START + p)
                for k in range(4):
                    last = nc.scalar.activation(Sm[:, k, :], Sm[:, k, :], ACT.Exp, bias=nmx[:, k:k + 1],
                                                scale=float(SD) ** -0.5, accum_out=asum[:, k:k + 1])
                last.then_inc(CSe, 1)
                act.wait_ge(CEt, START + p + 1)
                nc.scalar.activation(ET[:, :], bank(3, 128, 512), ACT.Copy).then_inc(CEe, 1)
            first_x(0)
            first_e(0)
            with act.Fori(0, NPAIR - 1) as p:
                slice_pair(p, True)
            slice_pair(NPAIR - 1, False)

            act.wait_ge(g_dv, 4)
            nc.scalar.activation(lge[:, :], lg[:, :], ACT.Exp, bias=ntop[:, :], accum_out=lsum[:, :]).then_inc(g_act, 1)
            with act.Fori(0, NPAIR // 2) as r:
                for b in (0, 1):
                    p = 2 * r + b
                    act.wait_ge(Etr, START + p + 1)
                    act.wait_ge(Ey, START + p - 1)
                    nc.scalar.activation(zT[:, b, :], bank(b, 128, W2), ACT.Copy).then_inc(EzT, 1)

        @block.tensor
        def _(pe):
            pe.wait_ge(init_done, 1)
            pe.wait_ge(c_in, 160)
            with pe.Fori(0, IMGS // NBUF) as it:
                for b in range(NBUF):
                    pe.wait_ge(p_in[b], 16 * it + 16)
                    pe.wait_ge(embu, START + it * NBUF + (b - NBUF + 1))
                    for t, rows in ((0, TT), (1, R_CLS)):
                        for c in range(KCH):
                            last = nc.tensor.matmul(ps[0:rows, b, t * DIM:(t + 1) * DIM],
                                                    patch[:, b, c, t * TT:t * TT + rows], wc[:, c, :],
                                                    start=(c == 0), stop=(c == KCH - 1))
                    last.then_inc(emb_done, 1)

            def prep(gp, b, slot):
                if slot == "tr":
                    pe.wait_ge(zs, START + gp + 1)
                    pe.wait_ge(selev, START + 8 * gp)
                    for t in range(4):
                        last = nc.tensor.transpose(ps[:, P_BANK, t * TT:(t + 1) * TT], z[:, t, :], ident[0:TT, 0:TT])
                    last.then_inc(tr, 1)
                if slot == "q":
                    pe.wait_ge(yTs, START + gp + 1)
                    pe.wait_ge(Vs, START + gp)
                    nc.tensor.matmul(bank(P_BANK + 1, 128, W2), wqkv[:, 0:DIM], yT[:, :], start=True, stop=True).then_inc(qd, 1)
                if slot == "k":
                    nc.tensor.matmul(bank(P_BANK, 128, W2), wqkv[:, DIM:2 * DIM], yT[:, :], start=True, stop=True).then_inc(kd, 1)
                if slot == "v":
                    pe.wait_ge(selev, START + 8 * gp + 7)
                    for t in range(4):
                        last = nc.tensor.matmul(ps[0:TT, P_BANK + 1, t * DIM:(t + 1) * DIM], yT[:, t * TT:(t + 1) * TT],
                                                wqkv[:, 2 * DIM:3 * DIM], start=True, stop=True)
                    last.then_inc(vd, 1)
                if isinstance(slot, int):
                    s = slot
                    if s == 0:
                        pe.wait_ge(qlos, START + gp + 1)
                    elif s == 1:
                        pe.wait_ge(klos, START + gp + 1)
                    else:
                        pe.wait_ge(selev, START + 8 * gp + s - 1)
                    sel, hi, lo = (selq, qhi, qlo) if s < 4 else (selk, khi, klo)
                    o = bank(P_BANK + 1 - s % 2, 128, W2)
                    nc.tensor.matmul(o, sel[:, s % 4, 0, :], hi[:, :], start=True, stop=False)
                    nc.tensor.matmul(o, sel[:, s % 4, 1, :], lo[:, :], start=False, stop=True).then_inc(seld, 1)

            def period(gp, b, jj, S, T, O, P):
                n = gp * 2 + jj
                si = n - 1
                sb_, sj = (1 - b, 1) if jj == 0 else (b, 0)
                ob, oj = 1 - b, jj

                def nx(j, slot):
                    if P and j == jj:
                        prep(gp + 1, 1 - b, slot)

                def scores(u):
                    if not S:
                        return
                    t, qt = u // 2, u % 2
                    if u == 0 and jj == 0:
                        pe.wait_ge(selev, START + 8 * gp + 8)
                    pe.wait_ge(smax, START + 8 * n + u - 1)
                    for e in range(2):
                        last = nc.tensor.matmul(
                            ps[0:TT, S_BANK + u % 2, e * NT:(e + 1) * NT],
                            qs[:, b, t, jj * NT + qt * TT:jj * NT + (qt + 1) * TT],
                            ks[:, b, 2 * t + e, jj * NT:(jj + 1) * NT], start=True, stop=True)
                    last.then_inc(sd, 1)

                def negmax(hf):
                    if not T:
                        return
                    if hf == 0:
                        pe.wait_ge(m2s, START + si + 1)
                        pe.wait_ge(hA, START + n - 2)
                    else:
                        pe.wait_ge(nmq, START + 2 * si + 1)
                    for t in range(2):
                        for qt in range(2):
                            last = nc.tensor.matmul(
                                ps[96:128, R_BANK, t * NT + qt * TT:t * NT + (qt + 1) * TT],
                                M2[:, qt, 2 * hf + t, :], ident[0:TT, 0:TT], start=True, stop=True)
                    last.then_inc(nm, 1)

                def tscores(v):
                    if not T:
                        return
                    g, kt, tt = v // 4, (v // 2) % 2, v % 2
                    t = 2 * g + tt
                    if v == 0 or v == 4:
                        pe.wait_ge(nmq, START + 2 * si + g + 1)
                    pe.wait_ge(ex, START + 8 * si + v - 1)
                    for e in range(2):
                        last = nc.tensor.matmul(
                            ps[0:TT, T_BANK + v % 2, e * NT:(e + 1) * NT],
                            ks[:, sb_, 2 * t + e, sj * NT + kt * TT:sj * NT + (kt + 1) * TT],
                            qs[:, sb_, t, sj * NT:(sj + 1) * NT], start=True, stop=True)
                    last.then_inc(st, 1)

                def values(img, vb, vj, w):
                    g, kt = w // 2, w % 2
                    pe.wait_ge(ex, START + 8 * img + 2 * w + 2)
                    if w == 0:
                        pe.wait_ge(oraws, START + img)
                        pe.wait_ge(Vs, START + (gp if jj == 0 else gp + 1))
                    K = TT if kt == 0 else VT - TT
                    for i in range(4):
                        last = nc.tensor.matmul(
                            ps[32 * i:32 * i + 32, O_BANK, g * NT:(g + 1) * NT],
                            Vx[0:K, vb, 2 * vj + kt, 4 * g + i, :],
                            PT[0:K, 2 * (w % 2) + i // 2, (i % 2) * NT:(i % 2 + 1) * NT],
                            start=(kt == 0), stop=(kt == 1))
                    last.then_inc(pv, 1)

                scores(0)
                negmax(0)
                scores(1)
                nx(0, "tr")
                nx(1, 2)
                if O:
                    values(n - 2, ob, oj, 3)
                negmax(1)
                nx(1, 3)
                scores(2)
                tscores(0)
                if O:
                    pe.wait_ge(oraws, START + n - 1)
                    if T:
                        pe.wait_ge(nmq, START + 2 * si + 2)
                    else:
                        pe.wait_ge(hA, START + n - 2)
                    for qt in range(2):
                        for g in range(2):
                            last = nc.tensor.transpose(ps[0:TT, R_BANK, (2 * qt + g) * DIM:(2 * qt + g + 1) * DIM],
                                                       oraw[:, g * NT + qt * TT:g * NT + (qt + 1) * TT], ident[:, :])
                    last.then_inc(ot, 1)
                nx(0, "q")
                nx(1, 4)
                scores(3)
                tscores(1)
                nx(0, "k")
                if O:
                    pe.wait_ge(ons, START + n - 1)
                    for qt in range(2):
                        last = nc.tensor.transpose(ps[:, R_BANK, qt * TT:(qt + 1) * TT], on[:, qt, :], ident[0:TT, 0:TT])
                    last.then_inc(t2, 1)
                scores(4)
                tscores(2)
                if T:
                    values(si, sb_, sj, 0)
                nx(1, 5)
                if O:
                    pe.wait_ge(onTs, START + n - 1)
                    for qt in range(2):
                        last = nc.tensor.matmul(ps[0:TT, R_BANK, qt * DIM:(qt + 1) * DIM], onT[:, qt * TT:(qt + 1) * TT],
                                                wpj[:, :], start=True, stop=True)
                    last.then_inc(pj, 1)
                scores(5)
                tscores(3)
                nx(1, 6)
                scores(6)
                tscores(4)
                if T:
                    values(si, sb_, sj, 1)
                nx(1, 7)
                scores(7)
                tscores(5)
                nx(0, 0)
                tscores(6)
                if T:
                    values(si, sb_, sj, 2)
                nx(0, 1)
                nx(1, "v")
                tscores(7)

            with pe.Fori(0, LAYERS) as L:
                g0 = L * NPAIR
                pe.wait_ge(wa_in, 80 * L + 80)
                pe.wait_ge(vone_ready, 1)
                for slot in ("tr", "q", "k", 0, 1, 2, 3, 4, 5, 6, 7, "v"):
                    prep(g0, 0, slot)
                period(g0, 0, 0, True, False, False, True)
                period(g0, 0, 1, True, True, False, True)
                with pe.Fori(0, NPAIR // 2 - 1) as r:
                    p = 2 * r + 1
                    for b in (1, 0):
                        for jj in (0, 1):
                            period(g0 + p + (1 - b), b, jj, True, True, True, True)
                for jj in (0, 1):
                    period(g0 + NPAIR - 1, 1, jj, True, True, True, False)
                for jj in (0, 1):
                    period(g0 + NPAIR, 0, jj, False, jj == 0, True, False)

                pe.wait_ge(wb_in, 48 * L + 48)
                pe.wait_ge(hA, START + g0 * 2 + IMGS)

                def trb(gp):
                    pe.wait_ge(Bz, START + gp + 1)
                    pe.wait_ge(ByT, START + gp)
                    for t in range(4):
                        last = nc.tensor.transpose(ps[:, 0, t * TT:(t + 1) * TT], z[:, t, :], ident[0:TT, 0:TT])
                    last.then_inc(Btr, 1)

                def fc1(gp):
                    pe.wait_ge(ByT, START + gp + 1)
                    pe.wait_ge(Bg, START + 2 * gp)
                    for c in range(2):
                        nc.tensor.matmul(bank(2 + c, 128, W2), w1[:, c * 128:(c + 1) * 128], yT[:, :],
                                         start=True, stop=True).then_inc(Bf1, 1)

                def fc2(gp, b):
                    pe.wait_ge(Bg, START + 2 * gp + 2)
                    pe.wait_ge(hB, START + 1 + gp)
                    for t in range(4):
                        for c in range(2):
                            last = nc.tensor.matmul(ps[0:TT, 4, t * DIM:(t + 1) * DIM], gT[:, b, c, t * TT:(t + 1) * TT],
                                                    w2[:, c, :], start=(c == 0), stop=(c == 1))
                    last.then_inc(Bf2, 1)
                trb(g0)
                fc1(g0)
                trb(g0 + 1)
                with pe.Fori(0, NPAIR // 2 - 1) as r:
                    p = 2 * r + 1
                    for b in (1, 0):
                        q = p + (1 - b)
                        fc1(g0 + q)
                        trb(g0 + q + 1)
                        fc2(g0 + q - 1, 1 - b)
                fc1(g0 + NPAIR - 1)
                fc2(g0 + NPAIR - 2, 0)
                fc2(g0 + NPAIR - 1, 1)

            pe.wait_ge(hB, START + 1 + LAYERS * NPAIR)
            pe.wait_ge(w_in, 16 * 22)
            pe.wait_ge(w_dv, 1)
            for h in range(SH):
                nc.tensor.matmul(ps[:, 0, h * SM:(h + 1) * SM], wx[:, h, :], wslT[:, :], start=True, stop=True)
                nc.tensor.matmul(ps[0:TT, 1, h * SM:(h + 1) * SM], bxw[:, h, :], wslT[:, :], start=True, stop=True)
            nc.tensor.matmul(bank(2, SD, SD), wq3[:, 0, :], wq3[:, 1, :], start=True, stop=True)
            for g in range(2):
                last = nc.tensor.matmul(bank(3 + g, SD, 512), wq3[:, 2, :],
                                        woT[:, 4 * g:4 * g + 4, :].rearrange("p h n -> p (h n)"), start=True, stop=True)
            last.then_inc(w_pe, 1)
            pe.wait_ge(w_dv, 3)

            def first_t(p):
                pe.wait_ge(Cz, START + p + 1)
                pe.wait_ge(CxT, START + p)
                for t in range(4):
                    last = nc.tensor.transpose(ps[:, 0, t * TT:(t + 1) * TT], x1e[:, t, 0:DIM], ident[0:TT, 0:TT])
                last.then_inc(Ctr, 1)

            def first_l(p):
                pe.wait_ge(CxT, START + p + 1)
                pe.wait_ge(CL, START + p)
                for t in range(4):
                    last = nc.tensor.matmul(ps[0:TT, 1 + t // 2, (t % 2) * SL:(t % 2 + 1) * SL], yT[:, t * TT:(t + 1) * TT],
                                            wcomb[:, :], start=True, stop=True)
                last.then_inc(Clg, 1)

            def slice_pair(p, more):
                pe.wait_ge(Cw, START + p + 1)
                pe.wait_ge(CEe, START + p)
                pe.wait_ge(CGe, START + p)
                for i in range(2):
                    for c in range(2):
                        for t in range(2):
                            last = nc.tensor.matmul(ps[:, 3 + i, c * (DIM + 1):(c + 1) * (DIM + 1)],
                                                    Lw[:, 2 * i + t, c * 128:(c + 1) * 128], x1e[:, 2 * i + t, :],
                                                    start=(t == 0), stop=(t == 1))
                last.then_inc(CT, 1)
                pe.wait_ge(Cwe, START + p)
                for c in range(2):
                    for t in range(4):
                        last = nc.tensor.transpose(ps[:, 6 + c, t * TT:(t + 1) * TT], Lw[:, t, c * 128:(c + 1) * 128],
                                                   ident[0:TT, 0:TT])
                last.then_inc(Cwt, 1)
                if more:
                    first_t(p + 1)
                pe.wait_ge(CTp, START + p + 1)
                pe.wait_ge(CH, START + p)
                for k in range(4):
                    last = nc.tensor.transpose(ps[:, 5, k * 128:(k + 1) * 128], Tp[:, k, 0:DIM], ident[:, :])
                last.then_inc(CTt, 1)
                if more:
                    first_l(p + 1)
                pe.wait_ge(CTe, START + p + 1)
                for k in range(4):
                    for i in range(4):
                        h = 4 * (k % 2) + i
                        last = nc.tensor.matmul(ps[32 * i:32 * i + 32, 3, k * SD:(k + 1) * SD],
                                                TpT[:, k * 128 + 32 * i:k * 128 + 32 * i + 32],
                                                wfxT[:, h * SD:(h + 1) * SD], start=True, stop=True)
                last.then_inc(Ctk, 1)
                pe.wait_ge(init_done, 1)
                pe.wait_ge(Ctok, START + p + 1)
                for k in range(4):
                    last = nc.tensor.transpose(ps[0:SD, 4, k * 128:(k + 1) * 128], tok[:, k, :], ident[:, :])
                last.then_inc(Ctt, 1)
                pe.wait_ge(init_done, 1)
                pe.wait_ge(Cte, START + p + 1)
                nc.tensor.matmul(bank(3, SD, 512), mqk[:, :], tokT[:, :], start=True, stop=True).then_inc(CA, 1)
                for k in range(4):
                    for i in range(4):
                        h = 4 * (k % 2) + i
                        last = nc.tensor.matmul(ps[32 * i:32 * i + 32, 5, k * DIM:(k + 1) * DIM],
                                                tokT[:, k * 128 + 32 * i:k * 128 + 32 * i + 32],
                                                wvo[:, h, :], start=True, stop=True)
                last.then_inc(CU, 1)
                pe.wait_ge(CAe, START + p + 1)
                for k in range(4):
                    last = nc.tensor.matmul(ps[:, 4, k * 128:(k + 1) * 128], AT[:, k * 128:(k + 1) * 128],
                                            tokT[:, k * 128:(k + 1) * 128], start=True, stop=True)
                last.then_inc(CS, 1)
                pe.wait_ge(CSe, START + p + 1)
                for k in range(4):
                    last = nc.tensor.transpose(ps[:, 3, k * 128:(k + 1) * 128], Sm[:, k, :], ident[:, :])
                last.then_inc(CEt, 1)
                pe.wait_ge(CEe, START + p + 1)
                pe.wait_ge(CUe, START + p + 1)
                for k in range(4):
                    last = nc.tensor.matmul(ps[:, 4, k * 128:(k + 1) * 128], ET[:, k * 128:(k + 1) * 128], Us[:, k, :],
                                            start=True, stop=True)
                last.then_inc(CG, 1)
                pe.wait_ge(CGe, START + p + 1)
                pe.wait_ge(Cwe, START + p + 1)
                for t in range(4):
                    for c in range(2):
                        last = nc.tensor.matmul(ps[0:TT, 5, t * DIM:(t + 1) * DIM], wT[:, c, t * TT:(t + 1) * TT],
                                                Gs[:, 2 * (t // 2) + c, :], start=(c == 0), stop=(c == 1))
                last.then_inc(CO, 1)
            first_t(0)
            first_l(0)
            with pe.Fori(0, NPAIR - 1) as p:
                slice_pair(p, True)
            slice_pair(NPAIR - 1, False)

            with pe.Fori(0, NPAIR) as p:
                pe.wait_ge(Gz, START + p + 1)
                for i in range(2):
                    for t in range(2):
                        last = nc.tensor.matmul(ps[:, 0, ds(p * 2 + i, 1)], z[:, 2 * i + t, :], onec[:, :],
                                                start=(t == 0), stop=(t == 1))
                last.then_inc(Gm, 1)
            pe.wait_ge(Gm, START + NPAIR)
            nc.tensor.matmul(ps[0:1, 1, 0:1], onec[:, :], onec[:, :], start=True, stop=True).then_inc(g_pe, 1)
            pe.wait_ge(g_dv, 1)
            nc.tensor.matmul(bank(1, IMGS, NE), means[:, :], wg[:, :], start=True, stop=True).then_inc(g_pe, 1)
            pe.wait_ge(g_dv, 7)
            nc.tensor.transpose(bank(2, NE, IMGS), onehot[:, :], ident[0:IMGS, 0:IMGS]).then_inc(g_pe, 1)
            pe.wait_ge(g_dv, 8)
            nc.tensor.matmul(bank(3, IMGS, DIM), onehotT[:, :], be[:, :], start=True, stop=True).then_inc(g_pe, 1)

            pe.wait_ge(g_dv, 9)
            pe.wait_ge(g_in, 32)

            def turn(p, b):
                pe.wait_ge(Ez, START + p + 1)
                pe.wait_ge(EzT, START + p - 1)
                for t in range(4):
                    last = nc.tensor.transpose(ps[:, b, t * TT:(t + 1) * TT], z[:, t, :], ident[0:TT, 0:TT])
                last.then_inc(Etr, 1)

            def expert(p, b):
                pe.wait_ge(EzT, START + p + 1)
                pe.wait_ge(Eo, START + p - 1)
                for i in range(2):
                    e = pe.value_load(idxrow[0:1, ds(p * 2 + i, 1)], min_val=0, max_val=NE - 1)
                    for t in (2 * i, 2 * i + 1):
                        last = nc.tensor.matmul(ps[0:TT, 2 + b, t * DIM:(t + 1) * DIM], zT[:, b, t * TT:(t + 1) * TT],
                                                we[:, ds(e, 1), :].rearrange("p a n -> p (a n)"), start=True, stop=True)
                last.then_inc(Ey, 1)
            turn(0, 0)
            with pe.Fori(0, NPAIR // 2 - 1) as r:
                for b in (0, 1):
                    turn(2 * r + b + 1, 1 - b)
                    expert(2 * r + b, b)
            turn(NPAIR - 1, 1)
            expert(NPAIR - 2, 0)
            expert(NPAIR - 1, 1)


def _constants():
    import numpy as np

    heads, hd = 8, 16
    sel = np.zeros((2, 128, 4, 2, 128), np.float32)
    d = np.arange(hd)
    for t in range(heads // 2):
        a, b = 2 * t * hd, (2 * t + 1) * hd
        for which, part, col, row in (
            (0, 0, 0, a), (0, 0, 16, a), (0, 1, 32, a), (0, 1, 48, b), (0, 0, 64, b), (0, 0, 80, b),
            (1, 0, 0, a), (1, 1, 16, a), (1, 0, 32, a), (1, 0, 48, b), (1, 0, 64, b), (1, 1, 80, b),
        ):
            sel[which, row + d, t, part, col + d] = 1.0
    mcols = np.zeros((128, 4), np.float32)
    mcols[0:48, 0] = 1.0
    mcols[48:96, 1] = 1.0
    mcols[96:98, 2] = 1.0
    mcols[98:100, 3] = 1.0
    return sel, mcols


def _inputs(x, cls_tok, a):
    import numpy as np

    B, C, S, _ = x.shape
    P = 16
    G = S // P
    k = C * P * P
    patches = x.reshape(B, C, G, P, G, P).transpose(0, 1, 3, 5, 2, 4).reshape(B, k // 128, 128, G * G).transpose(0, 2, 1, 3)
    sel, mcols = _constants()
    tok = lambda n: a["L0_tok_" + n]
    L, dim = tok("ln1_w").shape
    q_b = tok("qkv_b")
    at = lambda n: a["L0_attn_" + n]
    ff = lambda n: a["L0_ffn_" + n]
    SM, SD = at("Wslice").shape
    SH = at("Wx").shape[0] // SD
    NE = ff("bg").shape[0]
    f1 = tok("fc1_b")
    cols = np.stack([tok("ln1_w"), tok("ln1_b"), q_b[:, 0:dim], q_b[:, dim:2 * dim], tok("ln2_w"), tok("ln2_b"),
                     f1[:, 0:dim], f1[:, dim:2 * dim]], axis=2)
    return {
        "patches": patches, "conv_w": tok("conv_w"), "conv_b_row": tok("conv_b")[None],
        "cls_token": tok("cls_token")[0], "pos": tok("pos_embed")[0], "cls_tok": cls_tok[0],
        "cols": cols, "qkv_w": tok("qkv_w"), "proj_w": tok("proj_w"), "fc1_w": tok("fc1_w"), "fc2_w": tok("fc2_w"),
        "bv_row": q_b[:, None, 2 * dim:], "pb_row": tok("proj_b")[:, None], "fb_row": tok("fc2_b")[:, None],
        "ident": np.eye(128, dtype=np.float32), "mcols": mcols,
        "norm_w_row": tok("norm_w")[None], "norm_b_row": tok("norm_b")[None], "zero_row": np.zeros((1, dim), np.float32),
        "wx": at("Wx"), "bxT": at("bx").reshape(SH, SD).T, "wslT": at("Wslice").T, "bsl_row": at("bslice")[None],
        "temp_row": at("temperature").reshape(1, SH), "wfxT": at("Wfx").T,
        "bfx": np.repeat(at("bfx").reshape(2, 4, 1, SD), SM, axis=2).reshape(2, 4 * SM, SD).transpose(1, 0, 2),
        "wq3": np.stack([at("Wq"), at("Wk"), at("Wv")], axis=1),
        "woT": at("Wout").T.reshape(SH, SD, dim).transpose(1, 0, 2), "bo_row": at("bout")[None],
        "smask": np.where(np.arange(128)[:, None] // SM == np.arange(128)[None] // SM, 0.0, -1e30).astype(np.float32),
        "we": ff("We"), "be": ff("be"), "wg": ff("Wg"), "bg_row": ff("bg")[None],
        "iota_row": np.arange(NE, dtype=np.float32)[None],
        "selq": sel[0].reshape(128, -1), "selk": sel[1].reshape(128, -1),
    }


def kernel(x, cls_tok, **a):
    import numpy as np
    import concourse.bacc as bacc
    from concourse import mybir
    from concourse.bass_utils import run_bass_kernel_spmd

    named = _inputs(np.asarray(x), np.asarray(cls_tok), {k: np.asarray(v) for k, v in a.items()})
    arrays = {f"in_{k}": np.ascontiguousarray(v) for k, v in named.items()}
    nc = bacc.Bacc("TRN2", target_bir_lowering=False, num_devices=1, dynamic_dma_scratch_size=4096)
    D = {k[3:]: nc.dram_tensor(k, v.shape, mybir.dt.from_np(v.dtype), kind="ExternalInput").ap() for k, v in arrays.items()}
    B, NT, DIM = x.shape[0], 198, cls_tok.shape[2]
    out = nc.dram_tensor("out_h", (B, NT, DIM), mybir.dt.float32, kind="ExternalOutput").ap()
    vit_slice_moe(nc, D, out)
    r = run_bass_kernel_spmd(nc, [arrays], core_ids=[0])
    return r.results[0]["out_h"]
```

```python
import concourse.bass as bass
from concourse import mybir
from contextlib import ExitStack


def vit_slice_moe(nc, D, out):
    f32 = mybir.dt.float32
    f32r = mybir.dt.float32r
    i32 = mybir.dt.int32
    ALU = mybir.AluOpType
    ACT = mybir.ActivationFunctionType
    AX = mybir.AxisListType
    ds = bass.ds

    IMGS, _, KCH, NPATCH = D["patches"].shape
    LAYERS = D["qkv_w"].shape[0]
    DIM = 128
    HEADS = 8
    HD = DIM // HEADS
    TT = 99
    NT = 2 * TT
    VT = NT - 1
    R_CLS = NPATCH - TT
    R_OUT = R_CLS + 1
    NPAIR = IMGS // 2
    W2 = 2 * NT
    HID = D["fc1_w"].shape[2]
    EPS = 1e-5
    SCALE = float(HD) ** -0.5
    NBUF = 4
    START = 24

    ctx = ExitStack()
    with ctx:
        def sb(name, shape, dt=f32):
            return ctx.enter_context(nc.sbuf_tensor(name, shape, dt))

        def sem(name):
            return ctx.enter_context(nc.semaphore(name))

        H = sb("H", [TT, 2 * IMGS, DIM])
        ident = sb("ident", [128, 128])
        z = sb("z", [TT, 4, DIM])
        yT = sb("yT", [128, W2])
        bnst = sb("bnst", [TT, 2, 4, 6])
        mv = sb("mv", [TT, 2, 4, 2])
        ve = sb("ve", [TT, 2, 4])
        rstd = sb("rstd", [TT, 2, 4])
        half = sb("half", [TT, 4])
        spare = sb("spare", [1, 1])
        spare2 = sb("spare2", [1, 1])

        tower = ExitStack()

        def tb(name, shape, dt=f32):
            return tower.enter_context(nc.sbuf_tensor(name, shape, dt))

        U = tb("U", [128, NBUF * KCH * NPATCH])
        patch = U[:, :].rearrange("p (n c t) -> p n c t", n=NBUF, c=KCH)
        NV = 2 * 4 * HEADS * 32
        Vx = U[0:TT, 0:NV].rearrange("p (b t h e) -> p b t h e", b=2, t=4, h=HEADS)
        PT = U[0:TT, NV:NV + 4 * W2].rearrange("p (r c) -> p r c", r=4)
        gT = U[:, NV:NV + 4 * W2].rearrange("p (b c n) -> p b c n", b=2, c=2)
        qs = tb("qs", [128, 2, 4, W2], f32r)
        ks = tb("ks", [128, 2, HEADS, W2], f32r)
        qhi = tb("qhi", [128, W2], f32r)
        qlo = tb("qlo", [128, W2], f32r)
        khi = tb("khi", [128, W2], f32r)
        klo = tb("klo", [128, W2], f32r)
        oraw = tb("oraw", [128, W2])
        on = tb("on", [TT, 2, DIM])
        onT = tb("onT", [128, NT])
        mx = tb("mx", [TT, 2, HEADS])
        M2 = tb("M2", [TT, 2, 4, 32])
        rec = tb("rec", [TT, 2 * HEADS])
        mcols = tb("mcols", [128, 4])
        selq = tb("selq", [128, 4, 2, 128], f32r)
        selk = tb("selk", [128, 4, 2, 128], f32r)
        addend = tb("addend", [TT, 2, DIM])
        rowb = tb("rowb", [TT, DIM])
        clsrow = tb("clsrow", [1, 2, DIM])
        wc = tb("wc", [128, KCH, DIM])
        wqkv = tb("wqkv", [128, 3 * DIM])
        wpj = tb("wpj", [128, DIM])
        w1 = tb("w1", [128, HID])
        w2 = tb("w2", [128, 2, DIM])
        cols = tb("cols", [128, 8])
        bvrow = tb("bvrow", [TT, DIM])
        pbrow = tb("pbrow", [TT, DIM])
        fbrow = tb("fbrow", [TT, DIM])
        tower.close()

        SH, SM, SD = 8, 32, 64
        SL = SH * SM
        wnorm = sb("wnorm", [TT, 2, DIM])
        bnorm = sb("bnorm", [TT, 2, DIM])
        wx = sb("wx", [SD, SH, DIM])
        bx = sb("bx", [SD, SH])
        bxw = sb("bxw", [SD, SH, TT])
        wslT = sb("wslT", [SD, SM])
        bsl = sb("bsl", [TT, SM])
        rtemp = sb("rtemp", [128, SH])
        wcomb = sb("wcomb", [128, SL])
        bcomb = sb("bcomb", [TT, SL])
        wfxT = sb("wfxT", [128, SH * SD])
        bfx = sb("bfx", [128, 2, SD])
        wq3 = sb("wq3", [SD, 3, SD])
        mqk = sb("mqk", [SD, SD])
        woT = sb("woT", [SD, SH, DIM])
        wvo = sb("wvo", [SD, SH, DIM])
        smask = sb("smask", [128, 128])
        borow = sb("borow", [TT, DIM])
        x1e = sb("x1e", [TT, 4, DIM + 1])
        Lw = sb("Lw", [TT, 4, SL])
        gmx = sb("gmx", [TT, 4 * SH])
        gsum = sb("gsum", [TT, 4 * SH])
        grec = sb("grec", [TT, 4 * SH])
        wT = sb("wT", [128, 2, W2])
        Tp = sb("Tp", [128, 4, DIM + 1])
        seps = sb("seps", [128, 4])
        srec = sb("srec", [128, 4])
        TpT = sb("TpT", [128, 512])
        tok = sb("tok", [128, 4, SD])
        tokT = sb("tokT", [SD, 512])
        AT = sb("AT", [SD, 512])
        Us = sb("Us", [128, 4, DIM])
        Sm = sb("Sm", [128, 4, 128])
        rmx = sb("rmx", [128, 4])
        nmx = sb("nmx", [128, 4])
        asum = sb("asum", [128, 4])
        arec = sb("arec", [128, 4])
        ET = sb("ET", [128, 512])
        Gs = sb("Gs", [128, 4, DIM])
        NE = D["be"].shape[0]
        we = sb("we", [128, NE, DIM])
        wg = sb("wg", [128, NE])
        bg = sb("bg", [IMGS, NE])
        be = sb("be", [NE, DIM])
        iota = sb("iota", [IMGS, NE])
        onec = sb("onec", [TT, 1])
        mvall = sb("mvall", [TT, 2 * IMGS])
        rall = sb("rall", [TT, 2 * IMGS])
        means = sb("means", [128, IMGS])
        lg = sb("lg", [IMGS, NE])
        top = sb("top", [IMGS, 8])
        topi = sb("topi", [IMGS, 8], mybir.dt.uint32)
        ntop = sb("ntop", [IMGS, 1])
        topf = sb("topf", [IMGS, 1])
        lge = sb("lge", [IMGS, NE])
        lsum = sb("lsum", [IMGS, 1])
        gate = sb("gate", [IMGS, 1])
        onehot = sb("onehot", [IMGS, NE])
        onehotT = sb("onehotT", [NE, IMGS])
        gbe = sb("gbe", [IMGS, DIM])
        gateb = sb("gateb", [TT, IMGS])
        idxrow = sb("idxrow", [1, IMGS], mybir.dt.uint32)
        GB = sb("GB", [TT, 2, 2, DIM])
        OB = sb("OB", [TT, 2, 4, DIM])
        zT = sb("zT", [128, 2, W2])

        gate_d = nc.dram_tensor("gate_d", [1, IMGS], f32).ap()
        idx_d = nc.dram_tensor("idx_d", [1, IMGS], mybir.dt.uint32).ap()
        gbe_d = nc.dram_tensor("gbe_d", [IMGS, DIM], f32).ap()
        ps = ctx.enter_context(nc.psum_tensor("ps", [128, 8, 512], f32))
        S_BANK, T_BANK, O_BANK, P_BANK, R_BANK = 0, 2, 4, 5, 7

        c_in = sem("c_in")
        c_rows = sem("c_rows")
        p_in = [sem(f"p_in{i}") for i in range(NBUF)]
        wa_in = sem("wa_in")
        wb_in = sem("wb_in")
        init_done = sem("init_done")
        sel_cast = sem("sel_cast")
        add_ready = sem("add_ready")
        emb_done = sem("emb_done")
        vone_ready = sem("vone_ready")
        start_names = ("bn agg ve pw z tr yT q qhi qlo k khi klo v V sel selev hb "
                       "embu s smax mhi m2 nm nmq st ex pv oraw ot rec on t2 onT pj hA "
                       "Bbn Bagg Bve Bpw Bz Btr ByT Bf1 Bg Bf2 Bhb hB selevb").split()
        X = {n: sem(n + "_n") for n in start_names}
        bn, agg, ves, pw, zs, tr, yTs, qd, qhis, qlos, kd, khis, klos, vd, Vs, seld, selev, hb = [X[n] for n in start_names[:18]]
        sd, smax, mhi, m2s, nm, nmq, st, ex, pv, oraws, ot, recs, ons, t2, onTs, pj, hA = [X[n] for n in start_names[19:36]]
        embu = X["embu"]
        selevb = X["selevb"]
        Bbn, Bagg, Bve, Bpw, Bz, Btr, ByT, Bf1, Bg, Bf2, Bhb, hB = [X[n] for n in start_names[36:48]]
        cn = ("Fbn Fagg Fve Fpw Fz F1 F2 Cbn Cagg Cve Cpw Cz Ctr CxT Clg CL Cmx Csub Cex Csum Crc Cw CT Cse Csr CTp CTt CTe "
              "Cwt Cwe Ctk Ctok Ctt Cte CA CAe CU CUe CS CSm CSr CSx CSe CEt CEe Cr2 CG CGe CO Chb CH "
              "Gbn Gagg Gve Gpw Gz Gm Egb Egl Ehb Ez Etr EzT Ey Eo").split()
        X.update({n: sem(n + "_n") for n in cn})
        (Fbn, Fagg, Fve, Fpw, Fz, F1, F2, Cbn, Cagg, Cve, Cpw, Cz, Ctr, CxT, Clg, CL, Cmx, Csub, Cex, Csum, Crc, Cw, CT, Cse, Csr,
         CTp, CTt, CTe, Cwt, Cwe, Ctk, Ctok, Ctt, Cte, CA, CAe, CU, CUe, CS, CSm, CSr, CSx, CSe, CEt, CEe, Cr2, CG, CGe, CO, Chb, CH,
         Gbn, Gagg, Gve, Gpw, Gz, Gm, Egb, Egl, Ehb, Ez, Etr, EzT, Ey, Eo) = [X[n] for n in cn]
        w_in = sem("w_in")
        w_pe = sem("w_pe")
        w_dv = sem("w_dv")
        w_pl = sem("w_pl")
        g_pe = sem("g_pe")
        g_dv = sem("g_dv")
        g_act = sem("g_act")
        g_out = sem("g_out")
        g_in = sem("g_in")
        gb_in = [sem(f"gb_in{i}") for i in range(2)]
        o_out = [sem(f"o_out{i}") for i in range(2)]

        block = ctx.enter_context(nc.Block())

        def bank(i, rows, cols_):
            return ps[0:rows, i, 0:cols_]

        STEPS = HEADS
        ON_DVE = (3,)
        ON_ACT = tuple(s for s in range(STEPS) if s not in ON_DVE)

        def copied(q, s):
            mine, done = (ON_DVE, selevb) if s in ON_DVE else (ON_ACT, selev)
            return done, START + len(mine) * q + mine.index(s) + 1

        def last_read(q, s):
            return START + 16 * (q - 1) - (4 if s < 4 else 0)

        @block.sync
        def _(sp):
            sp.dma_start(ident[:, :], D["ident"]).then_inc(c_in, 16)
            sp.dma_start(mcols[:, :], D["mcols"]).then_inc(c_in, 16)
            sp.dma_start(U[:, 1024:2048], D["selq"]).then_inc(c_in, 16)
            sp.dma_start(U[:, 0:1024], D["selk"]).then_inc(c_in, 16)
            sp.dma_start(wc[:, :, :], D["conv_w"].rearrange("(c p) n -> p c n", p=128)).then_inc(c_in, 16)
            sp.dma_start(addend[:, 0, :], D["pos"][1:1 + TT, :]).then_inc(c_in, 16)
            sp.dma_start(addend[0:R_CLS, 1, :], D["pos"][1 + TT:1 + NPATCH, :]).then_inc(c_in, 16)
            sp.dma_start(rowb[:, :], D["conv_b_row"].to_broadcast([TT, DIM])).then_inc(c_in, 16)
            sp.dma_start(clsrow[:, 0, :], D["cls_token"]).then_inc(c_in, 16)
            sp.dma_start(clsrow[:, 1, :], D["pos"][0:1, :]).then_inc(c_in, 16)

            sp.wait_ge(sel_cast, 2)
            for b in range(NBUF):
                sp.dma_start(U[:, b * KCH * NPATCH:(b + 1) * KCH * NPATCH],
                             D["patches"][b].rearrange("p c t -> p (c t)")).then_inc(p_in[b], 16)
            sp.wait_ge(add_ready, 2)
            odd = H[:, :, :].rearrange("p (n two) d -> p n two d", two=2)
            sp.dma_start(odd[R_CLS:R_CLS + 1, :, 1, :], clsrow[:, 0:1, :].to_broadcast([1, IMGS, DIM])).then_inc(c_rows, 16)
            sp.dma_start(odd[R_OUT:R_OUT + 1, :, 1, :], D["cls_tok"].unsqueeze(1).to_broadcast([1, IMGS, DIM])).then_inc(c_rows, 16)
            with sp.Fori(1, IMGS // NBUF) as it:
                for b in range(NBUF):
                    sp.wait_ge(emb_done, it * NBUF + (b - NBUF + 1))
                    sp.dma_start(U[:, b * KCH * NPATCH:(b + 1) * KCH * NPATCH],
                                 D["patches"][ds(it * NBUF + b, 1)].rearrange("a p c t -> (a p) (c t)")).then_inc(p_in[b], 16)

            with sp.Fori(0, LAYERS) as L:
                lay = lambda name: D[name][ds(L, 1)].rearrange("a p n -> (a p) n")
                sp.wait_ge(hA, L * IMGS + START)
                sp.dma_start(wqkv[:, :], lay("qkv_w")).then_inc(wa_in, 16)
                sp.dma_start(wpj[:, :], lay("proj_w")).then_inc(wa_in, 16)
                sp.dma_start(bvrow[:, :], lay("bv_row").to_broadcast([TT, DIM])).then_inc(wa_in, 16)
                sp.dma_start(pbrow[:, :], lay("pb_row").to_broadcast([TT, DIM])).then_inc(wa_in, 16)
                sp.wait_ge(hB, L * NPAIR + START + 1)
                sp.dma_start(cols[:, :], lay("cols")).then_inc(wa_in, 16)
                sp.dma_start(w1[:, :], lay("fc1_w")).then_inc(wb_in, 16)
                sp.dma_start(w2[:, :, :], D["fc2_w"][ds(L, 1)].rearrange("a (c p) n -> p (a c) n", p=128)).then_inc(wb_in, 16)
                sp.dma_start(fbrow[:, :], lay("fb_row").to_broadcast([TT, DIM])).then_inc(wb_in, 16)

            sp.wait_ge(hB, START + 1 + LAYERS * NPAIR)
            loads = [
                (wnorm[:, 0, :], D["norm_w_row"].to_broadcast([TT, DIM])),
                (wnorm[0:R_OUT, 1, :], D["norm_w_row"].to_broadcast([R_OUT, DIM])),
                (wnorm[R_OUT:TT, 1, :], D["zero_row"]),
                (bnorm[:, 0, :], D["norm_b_row"].to_broadcast([TT, DIM])),
                (bnorm[0:R_OUT, 1, :], D["norm_b_row"].to_broadcast([R_OUT, DIM])),
                (bnorm[R_OUT:TT, 1, :], D["cls_tok"]),
                (wx[:, :, :], D["wx"].rearrange("(h d) n -> d h n", h=SH)),
                (bx[:, :], D["bxT"]),
                (wslT[:, :], D["wslT"]),
                (bsl[:, :], D["bsl_row"].to_broadcast([TT, SM])),
                (rtemp[:, :], D["temp_row"].to_broadcast([128, SH])),
                (wfxT[:, :], D["wfxT"]),
                (bfx[:, :, :], D["bfx"]),
                (wq3[:, :, :], D["wq3"]),
                (woT[:, :, :], D["woT"]),
                (smask[:, :], D["smask"]),
                (borow[:, :], D["bo_row"].to_broadcast([TT, DIM])),
                (we[:, :, :], D["we"].rearrange("e d o -> d e o")),
                (wg[:, :], D["wg"]),
                (bg[:, :], D["bg_row"].to_broadcast([IMGS, NE])),
                (be[:, :], D["be"]),
                (iota[:, :], D["iota_row"].to_broadcast([IMGS, NE])),
            ]
            for dst, src in loads:
                sp.dma_start(dst, src).then_inc(w_in, 16)

            sp.wait_ge(g_dv, 9)
            sp.dma_start(gate_d.rearrange("a n -> n a"), gate[:, :]).then_inc(g_out, 16)
            sp.dma_start(idx_d.rearrange("a n -> n a"), topi[:, 0:1]).then_inc(g_out, 16)
            sp.dma_start(gbe_d, gbe[:, :]).then_inc(g_out, 16)
            sp.wait_ge(g_out, 48)
            sp.dma_start(gateb[:, :], gate_d.to_broadcast([TT, IMGS])).then_inc(g_in, 16)
            sp.dma_start(idxrow[:, :], idx_d).then_inc(g_in, 16)

            def load_gbe(p, b):
                sp.dma_start(GB[:, b, :, :], gbe_d[ds(p * 2, 2), :].unsqueeze(0).to_broadcast([TT, 2, DIM])).then_inc(gb_in[b], 16)

            def store(p, b):
                sp.wait_ge(Eo, START + p + 1)
                ob = OB[:, b, :, :].rearrange("p (i two) d -> p i two d", two=2)
                dst = out[ds(p * 2, 2), :, :].rearrange("i t d -> t i d")
                sp.dma_start(dst[2:2 + TT], ob[:, :, 0, :]).then_inc(o_out[b], 16)
                sp.dma_start(dst[2 + TT:NT], ob[0:R_CLS, :, 1, :]).then_inc(o_out[b], 16)
                sp.dma_start(dst[1:2], ob[R_CLS:R_CLS + 1, :, 1, :]).then_inc(o_out[b], 16)
                sp.dma_start(dst[0:1], ob[R_OUT:R_OUT + 1, :, 1, :]).then_inc(o_out[b], 16)
            with sp.Fori(0, NPAIR // 2) as r:
                for b in (0, 1):
                    p = 2 * r + b
                    sp.wait_ge(Ehb, START + p - 1)
                    load_gbe(p, b)
                    store(p, b)
            for b in range(2):
                sp.wait_ge(o_out[b], 64 * (NPAIR // 2))

        @block.gpsimd
        def _(pool):
            nc.gpsimd.memset(spare[:, :], 0.0)
            for name in X:
                pool.sem_inc(X[name], START)
            nc.gpsimd.memset(half[:, :], -0.5)
            nc.gpsimd.memset(M2[:, :, :, :], 0.0).then_inc(init_done, 1)
            pool.wait_ge(emb_done, IMGS)
            nc.gpsimd.memset(Vx[:, :, :, :, HD:32], 1.0).then_inc(vone_ready, 1)

            def inv_std(gp, b, s_ve, s_z, s_pw):
                pool.wait_ge(s_ve, START + gp + 1)
                pool.wait_ge(s_z, START + gp - 1)
                nc.gpsimd.tensor_tensor(rstd[:, b, :], ve[:, b, :], half[:, :], ALU.pow).then_inc(s_pw, 1)

            def add_row(gp, p, s_z, w_in_, count, row, s_out):
                pool.wait_ge(s_z, START + gp + 1)
                pool.wait_ge(w_in_, count)
                nc.gpsimd.tensor_tensor(H[:, ds(p * 4, 4), :], H[:, ds(p * 4, 4), :],
                                        row[:, :].unsqueeze(1).to_broadcast([TT, 4, DIM]), ALU.add).then_inc(s_out, 1)

            with pool.Fori(0, LAYERS) as L:
                g0 = L * NPAIR
                for ve_, pw_, z_, w_in_, count, row, hb_ in ((ves, pw, zs, wa_in, 80 * L + 80, pbrow, hb),
                                                             (Bve, Bpw, Bz, wb_in, 48 * L + 48, fbrow, Bhb)):
                    inv_std(g0, 0, ve_, z_, pw_)
                    with pool.Fori(0, NPAIR // 2 - 1) as r:
                        for b in (0, 1):
                            p = 2 * r + b
                            inv_std(g0 + p + 1, 1 - b, ve_, z_, pw_)
                            add_row(g0 + p, p, z_, w_in_, count, row, hb_)
                    inv_std(g0 + NPAIR - 1, 1, ve_, z_, pw_)
                    add_row(g0 + NPAIR - 2, NPAIR - 2, z_, w_in_, count, row, hb_)
                    add_row(g0 + NPAIR - 1, NPAIR - 1, z_, w_in_, count, row, hb_)

            pool.wait_ge(hB, START + 1 + LAYERS * NPAIR)
            pool.wait_ge(w_in, 16 * 22)
            nc.gpsimd.memset(x1e[:, :, DIM:DIM + 1], 1.0)
            nc.gpsimd.memset(onec[:, :], 1.0).then_inc(w_pl, 1)

            with pool.Fori(0, NPAIR // 2) as r:
                for b in (0, 1):
                    p = 2 * r + b
                    inv_std(p, b, Fve, Fz, Fpw)
                    pool.wait_ge(Fz, START + p + 1)
                    zp = z[:, :, :].rearrange("p (i t) d -> p i (t d)", i=2)
                    nc.gpsimd.tensor_tensor(zp, zp, wnorm[:, :, :].rearrange("p t d -> p (t d)").unsqueeze(1)
                                            .to_broadcast([TT, 2, 2 * DIM]), ALU.mult).then_inc(F1, 1)

            def softmaxes(p):
                pool.wait_ge(Cz, START + p + 1)
                nc.gpsimd.tensor_tensor(H[:, ds(p * 4, 4), :], H[:, ds(p * 4, 4), :],
                                        borow[:, :].unsqueeze(1).to_broadcast([TT, 4, DIM]), ALU.add).then_inc(Chb, 1)
                pool.wait_ge(Cmx, START + p + 1)
                lv = Lw[:, :, :].rearrange("p t (h m) -> p (t h) m", m=SM)
                nc.gpsimd.tensor_tensor(lv, lv, gmx[:, :].unsqueeze(2).to_broadcast([TT, 4 * SH, SM]),
                                        ALU.subtract).then_inc(Csub, 1)
                pool.wait_ge(Crc, START + p + 1)
                nc.gpsimd.tensor_tensor(lv, lv, grec[:, :].unsqueeze(2).to_broadcast([TT, 4 * SH, SM]),
                                        ALU.mult).then_inc(Cw, 1)
            with pool.Fori(0, NPAIR // 2) as r:
                for b in (0, 1):
                    inv_std(2 * r + b, b, Cve, Cz, Cpw)
                    softmaxes(2 * r + b)
            with pool.Fori(0, NPAIR // 2) as r:
                for b in (0, 1):
                    inv_std(2 * r + b, b, Gve, Gz, Gpw)
            with pool.Fori(0, NPAIR // 2) as r:
                for b in (0, 1):
                    p = 2 * r + b
                    pool.wait_ge(gb_in[b], 16 * r + 16)
                    pool.wait_ge(Ez, START + p + 1)
                    for i in range(2):
                        hh = H[:, ds(p * 4 + 2 * i, 2), :]
                        last = nc.gpsimd.tensor_tensor(hh, hh, GB[:, b, i:i + 1, :].to_broadcast([TT, 2, DIM]), ALU.add)
                    last.then_inc(Ehb, 1)

        @block.vector
        def _(dve):
            dve.wait_ge(init_done, 1)
            dve.wait_ge(c_in, 160)
            nc.vector.tensor_copy(selq[:, :, :, :], U[:, 1024:2048].rearrange("p (a b c) -> p a b c", a=4, b=2)).then_inc(sel_cast, 1)
            nc.vector.tensor_copy(selk[:, :, :, :], U[:, 0:1024].rearrange("p (a b c) -> p a b c", a=4, b=2)).then_inc(sel_cast, 1)
            nc.vector.tensor_tensor(clsrow[:, 0, :], clsrow[:, 0, :], clsrow[:, 1, :], ALU.add).then_inc(add_ready, 1)
            nc.vector.tensor_tensor(addend[:, 0, :], addend[:, 0, :], rowb[:, :], ALU.add)
            nc.vector.tensor_tensor(addend[0:R_CLS, 1, :], addend[0:R_CLS, 1, :], rowb[0:R_CLS, :], ALU.add).then_inc(add_ready, 1)
            dve.wait_ge(add_ready, 2)
            with dve.Fori(0, IMGS // NBUF) as it:
                for b in range(NBUF):
                    dve.wait_ge(emb_done, it * NBUF + b + 1)
                    nc.vector.tensor_tensor(H[:, ds((it * NBUF + b) * 2, 1), :], ps[0:TT, b:b + 1, 0:DIM],
                                            addend[:, 0:1, :], ALU.add)
                    nc.vector.tensor_tensor(H[0:R_CLS, ds((it * NBUF + b) * 2 + 1, 1), :], ps[0:R_CLS, b:b + 1, DIM:2 * DIM],
                                            addend[0:R_CLS, 1:2, :], ALU.add).then_inc(embu, 1)
            for e in range(2):
                for b in range(2):
                    nc.vector.tensor_copy(ks[96:128, b, e:HEADS:2, :],
                                          mcols[96:128, 2 + e:3 + e].unsqueeze(2).to_broadcast([32, HEADS // 2, W2]))
            dve.wait_ge(embu, START + IMGS)
            dve.wait_ge(c_rows, 32)
            nc.vector.memset(spare[:, :], 0.0).then_inc(hB, 1)

            def stats(gp, p, b, s_bn, s_agg, s_ve, s_pw, s_z):
                dve.wait_ge(s_z, START + gp - 1)
                for t in range(4):
                    last = nc.vector.bn_stats(bnst[:, b, t, :], H[:, ds(p * 4 + t, 1), :].rearrange("p a d -> p (a d)"))
                last.then_inc(s_bn, 1)
                dve.wait_ge(s_bn, START + gp + 1)
                nc.vector.memset(spare2[:, :], 0.0)
                for t in range(4):
                    last = nc.vector.bn_aggr(mv[:, b, t, :], bnst[:, b, t, :])
                last.then_inc(s_agg, 1)
                dve.wait_ge(s_agg, START + gp + 1)
                dve.wait_ge(s_pw, START + gp - 1)
                nc.vector.tensor_scalar(ve[:, b, :], mv[:, b, :, 1], EPS, None, ALU.add).then_inc(s_ve, 1)

            def normalise(dst, p, b):
                for t in range(4):
                    last = nc.vector.tensor_scalar(dst[:, t, 0:DIM], H[:, ds(p * 4 + t, 1), :].rearrange("p a d -> p (a d)"),
                                                   mv[:, b, t, 0:1], rstd[:, b, t:t + 1], ALU.subtract, ALU.mult)
                return last

            def normed(gp, p, b, s_pw, s_z, s_tr):
                dve.wait_ge(s_pw, START + gp + 1)
                dve.wait_ge(s_tr, START + gp)
                normalise(z, p, b).then_inc(s_z, 1)

            def low_parts(gp, src, bias, hi, lo, s_hi, s_sel, s_lo, selcount):
                dve.wait_ge(s_hi, START + gp + 1)
                dve.wait_ge(s_sel, selcount)
                nc.vector.scalar_tensor_tensor(out=lo[:, :], in0=src, scalar=bias, in1=hi[:, :].bitcast(f32),
                                               op0=ALU.add, op1=ALU.subtract).then_inc(s_lo, 1)

            def prep(gp, p, b, slot):
                if slot == "stats":
                    stats(gp, p, b, bn, agg, ves, pw, zs)
                if slot == "norm":
                    normed(gp, p, b, pw, zs, tr)
                if slot == "qlo":
                    low_parts(gp, bank(P_BANK + 1, 128, W2), cols[:, 2:3], qhi, qlo, qhis, seld, qlos, START + 8 * gp)
                if slot == "klo":
                    low_parts(gp, bank(P_BANK, 128, W2), cols[:, 3:4], khi, klo, khis, seld, klos, START + 8 * gp)
                if isinstance(slot, int):
                    dve.wait_ge(seld, START + STEPS * gp + slot + 1)
                    dve.wait_ge(st, last_read(gp, slot))
                    for e in range(2):
                        last = nc.vector.tensor_scalar(ks[0:96, b, slot - 1 + e, :], bank(P_BANK, 96, W2),
                                                       mcols[0:96, e:e + 1], None, ALU.mult)
                    last.then_inc(selevb, 1)
                if slot == "V":
                    dve.wait_ge(vd, START + gp + 1)
                    dve.wait_ge(pv, START + 8 * (gp - 1))
                    for t in range(4):
                        last = nc.vector.tensor_tensor(
                            Vx[:, b, t, :, 0:HD],
                            ps[0:TT, P_BANK + 1, t * DIM:(t + 1) * DIM].rearrange("p (h d) -> p h d", h=HEADS),
                            bvrow[:, :].rearrange("p (h d) -> p h d", h=HEADS), ALU.add)
                    last.then_inc(Vs, 1)

            def period(gp, p, b, jj, S, O, P, P2):
                n = gp * 2 + jj

                def smx(u):
                    if not S:
                        return
                    dve.wait_ge(sd, START + 8 * n + u + 1)
                    if u == 0:
                        dve.wait_ge(m2s, START + n)
                    t, qt = u // 2, u % 2
                    nc.vector.reduce_max(mx[:, qt, 2 * t:2 * t + 2],
                                         bank(S_BANK + u % 2, TT, W2).rearrange("p (e m) -> p e m", e=2)[:, :, 0:VT],
                                         AX.X).then_inc(smax, 1)

                def nx(j, slot):
                    if P and j == jj:
                        prep(gp + 1, p + 1, 1 - b, slot)

                def nx2(j, slot):
                    if P2 and j == jj:
                        prep(gp + 2, p + 2, b, slot)
                smx(0)
                smx(1)
                nx2(0, "stats")
                smx(2)
                if O:
                    dve.wait_ge(ot, START + n - 1)
                    src = bank(R_BANK, TT, 512).rearrange("p (x e) -> p x e", e=32)
                    nc.vector.reciprocal(rec[:, :], src[:, :, HD]).then_inc(recs, 1)
                    dve.wait_ge(recs, START + n - 1)
                    dve.wait_ge(t2, START + n - 2)
                    nc.vector.tensor_tensor(on[:, :, :].rearrange("p q (x e) -> p (q x) e", e=HD), src[:, :, 0:HD],
                                            rec[:, :].unsqueeze(2).to_broadcast([TT, 2 * HEADS, HD]),
                                            ALU.mult).then_inc(ons, 1)
                smx(3)
                nx(0, "qlo")
                smx(4)
                nx2(1, "norm")
                nx(0, "klo")
                if O:
                    dve.wait_ge(pj, START + n - 1)
                    dve.wait_ge(hb, START + gp)
                    tile0 = p * 4 + (2 * jj - 4)
                    nc.vector.tensor_tensor(H[:, ds(tile0, 2), :], H[:, ds(tile0, 2), :],
                                            bank(R_BANK, TT, 2 * DIM).rearrange("p (a d) -> p a d", a=2),
                                            ALU.add).then_inc(hA, 1)
                smx(5)
                smx(6)
                smx(7)
                nx(0, 3)
                if S:
                    dve.wait_ge(smax, START + 8 * n + 8)
                    dve.wait_ge(nm, START + 2 * n)
                    m2v = M2[:, :, :, :].rearrange("p q t c -> p (q t) c")
                    mxv = mx[:, :, :].rearrange("p q (t e) -> p (q t) e", e=2)
                    nc.vector.tensor_scalar(m2v[:, :, 0:4:2].bitcast(f32r), mxv, -1.0, None, ALU.mult).then_inc(mhi, 1)
                    dve.wait_ge(mhi, START + n + 1)
                    nc.vector.scalar_tensor_tensor(out=m2v[:, :, 1:4:2], in0=mxv, scalar=-1.0, in1=m2v[:, :, 0:4:2],
                                                   op0=ALU.mult, op1=ALU.subtract).then_inc(m2s, 1)
                nx(1, "V")

            with dve.Fori(0, LAYERS) as L:
                g0 = L * NPAIR
                dve.wait_ge(hB, START + g0 + 1)
                dve.wait_ge(wa_in, 80 * L + 80)
                dve.wait_ge(vone_ready, 1)
                for slot in ("stats", "norm", "qlo", "klo"):
                    prep(g0, 0, 0, slot)
                prep(g0 + 1, 1, 1, "stats")
                prep(g0 + 1, 1, 1, "norm")
                for slot in ON_DVE + ("V",):
                    prep(g0, 0, 0, slot)
                for jj in (0, 1):
                    period(g0, 0, 0, jj, True, False, True, True)
                with dve.Fori(0, NPAIR // 2 - 2) as r:
                    p = 2 * r + 1
                    for b in (1, 0):
                        for jj in (0, 1):
                            period(g0 + p + (1 - b), p + (1 - b), b, jj, True, True, True, True)
                for q in (NPAIR - 3, NPAIR - 2, NPAIR - 1):
                    for jj in (0, 1):
                        period(g0 + q, q, q % 2, jj, True, True, q < NPAIR - 1, q < NPAIR - 2)
                for jj in (0, 1):
                    period(g0 + NPAIR, NPAIR, 0, jj, False, True, False, False)

                dve.wait_ge(hA, START + g0 * 2 + IMGS)
                dve.wait_ge(wb_in, 48 * L + 48)

                def resid(gp, p, b):
                    dve.wait_ge(Bf2, START + gp + 1)
                    dve.wait_ge(Bhb, START + gp + 1)
                    nc.vector.tensor_tensor(H[:, ds(p * 4, 4), :], H[:, ds(p * 4, 4), :],
                                            bank(4 + b, TT, 512).rearrange("p (a d) -> p a d", a=4), ALU.add).then_inc(hB, 1)

                def step(p, b, more_stats=True, more_norm=True, back=True):
                    if more_stats:
                        stats(g0 + p + 3, p + 3, 1 - b, Bbn, Bagg, Bve, Bpw, Bz)
                    if more_norm:
                        normed(g0 + p + 2, p + 2, b, Bpw, Bz, Btr)
                    if back:
                        resid(g0 + p - 1, p - 1, 1 - b)
                stats(g0, 0, 0, Bbn, Bagg, Bve, Bpw, Bz)
                stats(g0 + 1, 1, 1, Bbn, Bagg, Bve, Bpw, Bz)
                normed(g0, 0, 0, Bpw, Bz, Btr)
                stats(g0 + 2, 2, 0, Bbn, Bagg, Bve, Bpw, Bz)
                normed(g0 + 1, 1, 1, Bpw, Bz, Btr)
                step(0, 0, back=False)
                with dve.Fori(0, NPAIR // 2 - 2) as r:
                    step(2 * r + 1, 1)
                    step(2 * r + 2, 0)
                for q in (NPAIR - 3, NPAIR - 2, NPAIR - 1):
                    step(q, q % 2, False, q < NPAIR - 2)
                resid(g0 + NPAIR - 1, NPAIR - 1, 1)

            dve.wait_ge(hB, START + 1 + LAYERS * NPAIR)
            dve.wait_ge(w_in, 16 * 22)
            dve.wait_ge(w_pl, 1)

            def norm_out(p, b, dst, s_pw, s_z):
                dve.wait_ge(s_pw, START + p + 1)
                normalise(dst, p, b).then_inc(s_z, 1)

            def last_norm(p, b, more):
                dve.wait_ge(F2, START + p)
                norm_out(p, b, z, Fpw, Fz)
                if more:
                    stats(p + 1, p + 1, 1 - b, Fbn, Fagg, Fve, Fpw, Fz)
                dve.wait_ge(F1, START + p + 1)
                hp = H[:, ds(p * 4, 4), :].rearrange("p (i t) d -> p i (t d)", i=2)
                nc.vector.tensor_tensor(hp, z[:, :, :].rearrange("p (i t) d -> p i (t d)", i=2),
                                        bnorm[:, :, :].rearrange("p t d -> p (t d)").unsqueeze(1)
                                        .to_broadcast([TT, 2, 2 * DIM]), ALU.add).then_inc(F2, 1)
            stats(0, 0, 0, Fbn, Fagg, Fve, Fpw, Fz)
            with dve.Fori(0, NPAIR // 2 - 1) as r:
                for b in (0, 1):
                    last_norm(2 * r + b, b, True)
            last_norm(NPAIR - 2, 0, True)
            last_norm(NPAIR - 1, 1, False)
            dve.wait_ge(F2, START + NPAIR)

            nc.vector.reciprocal(rtemp[:, :], rtemp[:, :])
            nc.vector.tensor_copy(bxw[:, :, :], bx[:, :].unsqueeze(2).to_broadcast([SD, SH, TT])).then_inc(w_dv, 1)
            dve.wait_ge(w_dv, 1)
            dve.wait_ge(w_pe, 1)
            nc.vector.tensor_tensor(wcomb[:, :].rearrange("p (h m) -> p h m", m=SM),
                                    bank(0, 128, SL).rearrange("p (h m) -> p h m", m=SM),
                                    rtemp[:, :].unsqueeze(2).to_broadcast([128, SH, SM]), ALU.mult)
            nc.vector.tensor_tensor(bcomb[:, :].rearrange("p (h m) -> p h m", m=SM),
                                    bank(1, TT, SL).rearrange("p (h m) -> p h m", m=SM),
                                    bsl[:, :].unsqueeze(1).to_broadcast([TT, SH, SM]), ALU.add)
            nc.vector.tensor_copy(mqk[:, :], bank(2, SD, SD))
            nc.vector.tensor_copy(wvo[:, 0:4, :], bank(3, SD, 512).rearrange("p (h n) -> p h n", n=DIM))
            nc.vector.tensor_copy(wvo[:, 4:8, :], bank(4, SD, 512).rearrange("p (h n) -> p h n", n=DIM)).then_inc(w_dv, 1)
            dve.wait_ge(w_dv, 2)
            nc.vector.tensor_tensor(bcomb[:, :].rearrange("p (h m) -> p h m", m=SM),
                                    bcomb[:, :].rearrange("p (h m) -> p h m", m=SM),
                                    rtemp[0:TT, :].unsqueeze(2).to_broadcast([TT, SH, SM]), ALU.mult).then_inc(w_dv, 1)
            dve.wait_ge(w_dv, 3)

            lv = Lw[:, :, :].rearrange("p t (h m) -> p (t h) m", m=SM)

            def first_a(p, b):
                stats(p, p, b, Cbn, Cagg, Cve, Cpw, Cz)

            def first_b(p, b):
                dve.wait_ge(Ctr, START + p)
                dve.wait_ge(CT, START + p)
                norm_out(p, b, x1e, Cpw, Cz)

            def first_c(p):
                dve.wait_ge(Clg, START + p + 1)
                dve.wait_ge(Cwt, START + p)
                dve.wait_ge(CT, START + p)
                nc.vector.tensor_tensor(Lw[:, :, :], ps[0:TT, 1:3, :].rearrange("p b (t n) -> p (b t) n", n=SL),
                                        bcomb[:, :].unsqueeze(1).to_broadcast([TT, 4, SL]), ALU.add).then_inc(CL, 1)
                dve.wait_ge(CL, START + p + 1)
                dve.wait_ge(Csub, START + p)
                nc.vector.reduce_max(gmx[:, :], lv, AX.X).then_inc(Cmx, 1)

            def first_d(p):
                dve.wait_ge(Cex, START + p + 1)
                nc.vector.reduce_sum(gsum[:, :], lv, AX.X).then_inc(Csum, 1)
                dve.wait_ge(Csum, START + p + 1)
                dve.wait_ge(Cw, START + p)
                nc.vector.reciprocal(grec[:, :], gsum[:, :]).then_inc(Crc, 1)

            def second_a(p):
                dve.wait_ge(CT, START + p + 1)
                tv = ps[:, 3:5, 0:2 * (DIM + 1)].rearrange("p b (c n) -> p b c n", n=DIM + 1)
                nc.vector.tensor_scalar(seps[:, :].rearrange("p (b c) -> p b c", b=2), tv[:, :, :, DIM], 1e-5, None,
                                        ALU.add).then_inc(Cse, 1)
                dve.wait_ge(Cse, START + p + 1)
                nc.vector.reciprocal(srec[:, :], seps[:, :]).then_inc(Csr, 1)
                dve.wait_ge(Csr, START + p + 1)
                dve.wait_ge(CTt, START + p)
                dve.wait_ge(Ctok, START + p)
                nc.vector.tensor_tensor(Tp[:, :, :].rearrange("p (b c) n -> p b c n", b=2), tv,
                                        srec[:, :].rearrange("p (b c) -> p b c", b=2).unsqueeze(3)
                                        .to_broadcast([128, 2, 2, DIM + 1]), ALU.mult).then_inc(CTp, 1)

            def second_b(p):
                dve.wait_ge(Ctk, START + p + 1)
                dve.wait_ge(Ctt, START + p)
                for k in range(4):
                    last = nc.vector.scalar_tensor_tensor(out=tok[:, k, :], in0=bfx[:, k % 2, :], scalar=Tp[:, k, DIM:DIM + 1],
                                                          in1=ps[:, 3, k * SD:(k + 1) * SD], op0=ALU.mult, op1=ALU.add)
                last.then_inc(Ctok, 1)

            def second_c(p):
                dve.wait_ge(CS, START + p + 1)
                dve.wait_ge(CEt, START + p)
                nc.vector.tensor_tensor(Sm[:, :, :], bank(4, 128, 512).rearrange("p (k n) -> p k n", k=4),
                                        smask[:, :].unsqueeze(1).to_broadcast([128, 4, 128]), ALU.add).then_inc(CSm, 1)
                dve.wait_ge(CSm, START + p + 1)
                nc.vector.reduce_max(rmx[:, :], Sm[:, :, :], AX.X).then_inc(CSr, 1)
                dve.wait_ge(CSr, START + p + 1)
                nc.vector.tensor_scalar(nmx[:, :], rmx[:, :], -(float(SD) ** -0.5), None, ALU.mult).then_inc(CSx, 1)

            def second_d(p):
                dve.wait_ge(CSe, START + p + 1)
                nc.vector.reciprocal(arec[:, :], asum[:, :]).then_inc(Cr2, 1)
                dve.wait_ge(Cr2, START + p + 1)
                dve.wait_ge(CG, START + p + 1)
                dve.wait_ge(CO, START + p)
                nc.vector.tensor_tensor(Gs[:, :, :], bank(4, 128, 512).rearrange("p (k n) -> p k n", k=4),
                                        arec[:, :].unsqueeze(2).to_broadcast([128, 4, DIM]), ALU.mult).then_inc(CGe, 1)

            def second_e(p):
                dve.wait_ge(CO, START + p + 1)
                dve.wait_ge(Chb, START + p + 1)
                nc.vector.tensor_tensor(H[:, ds(p * 4, 4), :], H[:, ds(p * 4, 4), :],
                                        bank(5, TT, 512).rearrange("p (a d) -> p a d", a=4), ALU.add).then_inc(CH, 1)

            def slice_pair(p, b, more):
                if more:
                    first_a(p + 1, 1 - b)
                second_a(p)
                if more:
                    first_b(p + 1, 1 - b)
                second_b(p)
                if more:
                    first_c(p + 1)
                second_c(p)
                if more:
                    first_d(p + 1)
                second_d(p)
                second_e(p)
            first_a(0, 0)
            first_b(0, 0)
            first_c(0)
            first_d(0)
            with dve.Fori(0, NPAIR // 2 - 1) as r:
                for b in (0, 1):
                    slice_pair(2 * r + b, b, True)
            slice_pair(NPAIR - 2, 0, True)
            slice_pair(NPAIR - 1, 1, False)
            dve.wait_ge(CH, START + NPAIR)

            def gate_pair(p, b, more):
                if more:
                    stats(p + 1, p + 1, 1 - b, Gbn, Gagg, Gve, Gpw, Gz)
                dve.wait_ge(Gpw, START + p + 1)
                dve.wait_ge(Gm, START + p)
                normalise(z, p, b)
                nc.vector.tensor_copy(mvall[:, ds(p * 4, 4)], mv[:, b, :, 0])
                nc.vector.tensor_copy(rall[:, ds(p * 4, 4)], rstd[:, b, :]).then_inc(Gz, 1)
            stats(0, 0, 0, Gbn, Gagg, Gve, Gpw, Gz)
            with dve.Fori(0, NPAIR // 2 - 1) as r:
                for b in (0, 1):
                    gate_pair(2 * r + b, b, True)
            gate_pair(NPAIR - 2, 0, True)
            gate_pair(NPAIR - 1, 1, False)
            dve.wait_ge(g_pe, 1)
            nc.vector.tensor_scalar(means[:, :], bank(0, 128, IMGS), 1.0 / NT, None, ALU.mult).then_inc(g_dv, 1)
            dve.wait_ge(g_pe, 2)
            nc.vector.tensor_tensor(lg[:, :], bank(1, IMGS, NE), bg[:, :], ALU.add).then_inc(g_dv, 1)
            dve.wait_ge(g_dv, 2)
            nc.vector.max(top[:, :], lg[:, :]).then_inc(g_dv, 1)
            dve.wait_ge(g_dv, 3)
            nc.vector.max_index(topi[:, :], top[:, :], lg[:, :])
            nc.vector.tensor_scalar(ntop[:, :], top[:, 0:1], -1.0, None, ALU.mult).then_inc(g_dv, 1)
            dve.wait_ge(g_dv, 4)
            nc.vector.tensor_copy(topf[:, :], topi[:, 0:1]).then_inc(g_dv, 1)
            dve.wait_ge(g_act, 1)
            nc.vector.reciprocal(gate[:, :], lsum[:, :]).then_inc(g_dv, 1)
            dve.wait_ge(g_dv, 6)
            nc.vector.tensor_scalar(onehot[:, :], iota[:, :], topf[:, :], gate[:, :], ALU.is_equal, ALU.mult).then_inc(g_dv, 1)
            dve.wait_ge(g_pe, 3)
            nc.vector.tensor_copy(onehotT[:, :], bank(2, NE, IMGS)).then_inc(g_dv, 1)
            dve.wait_ge(g_pe, 4)
            nc.vector.tensor_copy(gbe[:, :], bank(3, IMGS, DIM)).then_inc(g_dv, 1)

            dve.wait_ge(g_in, 32)

            def renorm(p):
                dve.wait_ge(Etr, START + p)
                for t in range(4):
                    last = nc.vector.tensor_scalar(z[:, t, :], H[:, ds(p * 4 + t, 1), :].rearrange("p a d -> p (a d)"),
                                                   mvall[:, ds(p * 4 + t, 1)], rall[:, ds(p * 4 + t, 1)],
                                                   ALU.subtract, ALU.mult)
                last.then_inc(Ez, 1)

            def gated(p, b):
                dve.wait_ge(Ey, START + p + 1)
                dve.wait_ge(Ehb, START + p + 1)
                if b is not None:
                    dve.wait_ge(o_out[b], 64 * (p_half(p, b)))
                for i in range(2):
                    last = nc.vector.scalar_tensor_tensor(
                        out=OB[:, b, 2 * i:2 * i + 2, :], in0=ps[0:TT, 2 + b, 2 * i * DIM:(2 * i + 2) * DIM].rearrange("p (t d) -> p t d", t=2),
                        scalar=gateb[:, ds(p * 2 + i, 1)], in1=H[:, ds(p * 4 + 2 * i, 2), :],
                        op0=ALU.mult, op1=ALU.add)
                last.then_inc(Eo, 1)
            renorm(0)
            with dve.Fori(0, NPAIR // 2 - 1) as r:
                for b in (0, 1):
                    p = 2 * r + b
                    renorm(p + 1)
                    p_half = lambda p, b: r
                    gated(p, b)
            renorm(NPAIR - 1)
            p_half = lambda p, b: NPAIR // 2 - 1
            gated(NPAIR - 2, 0)
            gated(NPAIR - 1, 1)

        @block.scalar
        def _(act):
            act.wait_ge(init_done, 1)
            act.wait_ge(c_in, 160)

            def prep(gp, b, slot):
                if slot == "yT":
                    act.wait_ge(tr, START + gp + 1)
                    act.wait_ge(vd, START + gp)
                    nc.scalar.activation(yT[:, :], bank(P_BANK, 128, W2), ACT.Identity,
                                         bias=cols[:, 1:2], scale=cols[:, 0:1]).then_inc(yTs, 1)
                if slot == "qhi":
                    act.wait_ge(qd, START + gp + 1)
                    act.wait_ge(seld, START + 8 * gp)
                    nc.scalar.activation(qhi[:, :], bank(P_BANK + 1, 128, W2), ACT.Identity,
                                         bias=cols[:, 2:3]).then_inc(qhis, 1)
                if slot == "khi":
                    act.wait_ge(kd, START + gp + 1)
                    act.wait_ge(seld, START + 8 * gp)
                    nc.scalar.activation(khi[:, :], bank(P_BANK, 128, W2), ACT.Identity,
                                         bias=cols[:, 3:4]).then_inc(khis, 1)
                if slot in ON_ACT:
                    act.wait_ge(seld, START + STEPS * gp + slot + 1)
                    act.wait_ge(st, last_read(gp, slot))
                    if slot % 2 == 0:
                        nc.scalar.activation(qs[:, b, slot // 2, :], bank(P_BANK + 1, 128, W2), ACT.Identity).then_inc(selev, 1)
                    else:
                        for e in range(2):
                            last = nc.scalar.activation(ks[0:96, b, slot - 1 + e, :], bank(P_BANK, 96, W2), ACT.Identity,
                                                        scale=mcols[0:96, e:e + 1])
                        last.then_inc(selev, 1)

            def period(gp, b, jj, S, T, O, P):
                n = gp * 2 + jj
                s_img = n - 1
                sb_, sj = (1 - b, 1) if jj == 0 else (b, 0)

                def nx(j, slot):
                    if P and j == jj:
                        prep(gp + 1, 1 - b, slot)

                def negmax(hf):
                    if T:
                        act.wait_ge(nm, START + 2 * s_img + hf + 1)
                        nc.scalar.activation(qs[96:128, sb_, 2 * hf:2 * hf + 2, sj * NT:(sj + 1) * NT],
                                             ps[96:128, R_BANK, 0:W2].rearrange("p (t c) -> p t c", t=2),
                                             ACT.Identity).then_inc(nmq, 1)

                def expo(v):
                    if T:
                        act.wait_ge(st, START + 8 * s_img + v + 1)
                        if v % 2 == 0:
                            act.wait_ge(pv, START + 4 * s_img + v // 2 - 1)
                        nc.scalar.activation(PT[:, v % 4, :], bank(T_BANK + v % 2, TT, W2), ACT.Exp,
                                             scale=SCALE).then_inc(ex, 1)
                nx(0, "yT")
                negmax(0)
                nx(1, 4)
                if O:
                    act.wait_ge(pv, START + 4 * (n - 2) + 4)
                    act.wait_ge(ot, START + n - 2)
                    nc.scalar.activation(oraw[:, :], bank(O_BANK, 128, W2), ACT.Identity).then_inc(oraws, 1)
                negmax(1)
                nx(0, "qhi")
                expo(0)
                nx(0, "khi")
                nx(1, 5)
                expo(1)
                if O:
                    act.wait_ge(t2, START + n - 1)
                    act.wait_ge(pj, START + n - 2)
                    nc.scalar.activation(onT[:, :], bank(R_BANK, 128, NT), ACT.Identity).then_inc(onTs, 1)
                expo(2)
                nx(1, 6)
                expo(3)
                nx(1, 7)
                nx(0, 0)
                expo(4)
                nx(0, 1)
                expo(5)
                nx(0, 2)
                expo(6)
                expo(7)

            with act.Fori(0, LAYERS) as L:
                g0 = L * NPAIR
                act.wait_ge(wa_in, 80 * L + 80)
                act.wait_ge(vone_ready, 1)
                for slot in ("yT", "qhi", "khi") + ON_ACT:
                    prep(g0, 0, slot)
                period(g0, 0, 0, True, False, False, True)
                period(g0, 0, 1, True, True, False, True)
                with act.Fori(0, NPAIR // 2 - 1) as r:
                    p = 2 * r + 1
                    for b in (1, 0):
                        for jj in (0, 1):
                            period(g0 + p + (1 - b), b, jj, True, True, True, True)
                for jj in (0, 1):
                    period(g0 + NPAIR - 1, 1, jj, True, True, True, False)
                for jj in (0, 1):
                    period(g0 + NPAIR, 0, jj, False, jj == 0, True, False)

                act.wait_ge(wb_in, 48 * L + 48)

                def yTb(gp):
                    act.wait_ge(Btr, START + gp + 1)
                    act.wait_ge(Bf1, START + 2 * gp)
                    nc.scalar.activation(yT[:, :], bank(0, 128, W2), ACT.Identity,
                                         bias=cols[:, 5:6], scale=cols[:, 4:5]).then_inc(ByT, 1)

                def gelu(gp, b):
                    for c in range(2):
                        act.wait_ge(Bf1, START + 2 * gp + c + 1)
                        if c == 0:
                            act.wait_ge(Bf2, START + gp - 1)
                        nc.scalar.activation(gT[:, b, c, :], bank(2 + c, 128, W2), ACT.Gelu,
                                             bias=cols[:, 6 + c:7 + c]).then_inc(Bg, 1)
                yTb(g0)
                with act.Fori(0, NPAIR // 2 - 1) as r:
                    p = 2 * r
                    for b in (0, 1):
                        gelu(g0 + p + b, b)
                        yTb(g0 + p + b + 1)
                gelu(g0 + NPAIR - 2, 0)
                yTb(g0 + NPAIR - 1)
                gelu(g0 + NPAIR - 1, 1)

            act.wait_ge(w_dv, 3)
            act.wait_ge(hB, START + 1 + LAYERS * NPAIR)

            def first_x(p):
                act.wait_ge(Ctr, START + p + 1)
                act.wait_ge(Clg, START + p)
                nc.scalar.activation(yT[:, :], bank(0, 128, W2), ACT.Copy).then_inc(CxT, 1)

            def first_e(p):
                act.wait_ge(Csub, START + p + 1)
                nc.scalar.activation(Lw[:, :, :], Lw[:, :, :], ACT.Exp).then_inc(Cex, 1)

            def slice_pair(p, more):
                act.wait_ge(Cwt, START + p + 1)
                act.wait_ge(CO, START + p)
                nc.scalar.activation(wT[:, :, :], ps[:, 6:8, 0:W2], ACT.Copy).then_inc(Cwe, 1)
                if more:
                    first_x(p + 1)
                act.wait_ge(CTt, START + p + 1)
                act.wait_ge(Ctk, START + p)
                nc.scalar.activation(TpT[:, :], bank(5, 128, 512), ACT.Copy).then_inc(CTe, 1)
                act.wait_ge(Ctt, START + p + 1)
                act.wait_ge(CS, START + p)
                nc.scalar.activation(tokT[:, :], bank(4, SD, 512), ACT.Copy).then_inc(Cte, 1)
                act.wait_ge(CA, START + p + 1)
                nc.scalar.activation(AT[:, :], bank(3, SD, 512), ACT.Copy).then_inc(CAe, 1)
                act.wait_ge(CU, START + p + 1)
                act.wait_ge(CG, START + p)
                nc.scalar.activation(Us[:, :, :], bank(5, 128, 512).rearrange("p (k n) -> p k n", k=4), ACT.Copy).then_inc(CUe, 1)
                if more:
                    first_e(p + 1)
                act.wait_ge(CSx, START + p + 1)
                act.wait_ge(Cr2, START + p)
                for k in range(4):
                    last = nc.scalar.activation(Sm[:, k, :], Sm[:, k, :], ACT.Exp, bias=nmx[:, k:k + 1],
                                                scale=float(SD) ** -0.5, accum_out=asum[:, k:k + 1])
                last.then_inc(CSe, 1)
                act.wait_ge(CEt, START + p + 1)
                nc.scalar.activation(ET[:, :], bank(3, 128, 512), ACT.Copy).then_inc(CEe, 1)
            first_x(0)
            first_e(0)
            with act.Fori(0, NPAIR - 1) as p:
                slice_pair(p, True)
            slice_pair(NPAIR - 1, False)

            act.wait_ge(g_dv, 4)
            nc.scalar.activation(lge[:, :], lg[:, :], ACT.Exp, bias=ntop[:, :], accum_out=lsum[:, :]).then_inc(g_act, 1)
            with act.Fori(0, NPAIR // 2) as r:
                for b in (0, 1):
                    p = 2 * r + b
                    act.wait_ge(Etr, START + p + 1)
                    act.wait_ge(Ey, START + p - 1)
                    nc.scalar.activation(zT[:, b, :], bank(b, 128, W2), ACT.Copy).then_inc(EzT, 1)

        @block.tensor
        def _(pe):
            pe.wait_ge(init_done, 1)
            pe.wait_ge(c_in, 160)
            with pe.Fori(0, IMGS // NBUF) as it:
                for b in range(NBUF):
                    pe.wait_ge(p_in[b], 16 * it + 16)
                    pe.wait_ge(embu, START + it * NBUF + (b - NBUF + 1))
                    for t, rows in ((0, TT), (1, R_CLS)):
                        for c in range(KCH):
                            last = nc.tensor.matmul(ps[0:rows, b, t * DIM:(t + 1) * DIM],
                                                    patch[:, b, c, t * TT:t * TT + rows], wc[:, c, :],
                                                    start=(c == 0), stop=(c == KCH - 1))
                    last.then_inc(emb_done, 1)

            def prep(gp, b, slot):
                if slot == "tr":
                    pe.wait_ge(zs, START + gp + 1)
                    pe.wait_ge(*copied(gp - 1, STEPS - 1))
                    for t in range(4):
                        last = nc.tensor.transpose(ps[:, P_BANK, t * TT:(t + 1) * TT], z[:, t, :], ident[0:TT, 0:TT])
                    last.then_inc(tr, 1)
                if slot == "q":
                    pe.wait_ge(yTs, START + gp + 1)
                    pe.wait_ge(Vs, START + gp)
                    nc.tensor.matmul(bank(P_BANK + 1, 128, W2), wqkv[:, 0:DIM], yT[:, :], start=True, stop=True).then_inc(qd, 1)
                if slot == "k":
                    nc.tensor.matmul(bank(P_BANK, 128, W2), wqkv[:, DIM:2 * DIM], yT[:, :], start=True, stop=True).then_inc(kd, 1)
                if slot == "v":
                    pe.wait_ge(*copied(gp, STEPS - 2))
                    for t in range(4):
                        last = nc.tensor.matmul(ps[0:TT, P_BANK + 1, t * DIM:(t + 1) * DIM], yT[:, t * TT:(t + 1) * TT],
                                                wqkv[:, 2 * DIM:3 * DIM], start=True, stop=True)
                    last.then_inc(vd, 1)
                if isinstance(slot, int):
                    s = slot
                    if s == 0:
                        pe.wait_ge(qlos, START + gp + 1)
                    elif s == 1:
                        pe.wait_ge(klos, START + gp + 1)
                    else:
                        pe.wait_ge(*copied(gp, s - 2))
                    sel, hi, lo = (selq, qhi, qlo) if s % 2 == 0 else (selk, khi, klo)
                    o = bank(P_BANK + 1 - s % 2, 128, W2)
                    nc.tensor.matmul(o, sel[:, s // 2, 0, :], hi[:, :], start=True, stop=False)
                    nc.tensor.matmul(o, sel[:, s // 2, 1, :], lo[:, :], start=False, stop=True).then_inc(seld, 1)

            def period(gp, b, jj, S, T, O, P):
                n = gp * 2 + jj
                si = n - 1
                sb_, sj = (1 - b, 1) if jj == 0 else (b, 0)
                ob, oj = 1 - b, jj

                def nx(j, slot):
                    if P and j == jj:
                        prep(gp + 1, 1 - b, slot)

                def scores(u):
                    if not S:
                        return
                    t, qt = u // 2, u % 2
                    if u == 0 and jj == 0:
                        pe.wait_ge(*copied(gp, ON_ACT[-1]))
                        pe.wait_ge(*copied(gp, ON_DVE[-1]))
                    pe.wait_ge(smax, START + 8 * n + u - 1)
                    for e in range(2):
                        last = nc.tensor.matmul(
                            ps[0:TT, S_BANK + u % 2, e * NT:(e + 1) * NT],
                            qs[:, b, t, jj * NT + qt * TT:jj * NT + (qt + 1) * TT],
                            ks[:, b, 2 * t + e, jj * NT:(jj + 1) * NT], start=True, stop=True)
                    last.then_inc(sd, 1)

                def negmax(hf):
                    if not T:
                        return
                    if hf == 0:
                        pe.wait_ge(m2s, START + si + 1)
                        pe.wait_ge(hA, START + n - 2)
                    else:
                        pe.wait_ge(nmq, START + 2 * si + 1)
                    for t in range(2):
                        for qt in range(2):
                            last = nc.tensor.matmul(
                                ps[96:128, R_BANK, t * NT + qt * TT:t * NT + (qt + 1) * TT],
                                M2[:, qt, 2 * hf + t, :], ident[0:TT, 0:TT], start=True, stop=True)
                    last.then_inc(nm, 1)

                def tscores(v):
                    if not T:
                        return
                    g, kt, tt = v // 4, (v // 2) % 2, v % 2
                    t = 2 * g + tt
                    if v == 0 or v == 4:
                        pe.wait_ge(nmq, START + 2 * si + g + 1)
                    pe.wait_ge(ex, START + 8 * si + v - 1)
                    for e in range(2):
                        last = nc.tensor.matmul(
                            ps[0:TT, T_BANK + v % 2, e * NT:(e + 1) * NT],
                            ks[:, sb_, 2 * t + e, sj * NT + kt * TT:sj * NT + (kt + 1) * TT],
                            qs[:, sb_, t, sj * NT:(sj + 1) * NT], start=True, stop=True)
                    last.then_inc(st, 1)

                def values(img, vb, vj, w):
                    g, kt = w // 2, w % 2
                    pe.wait_ge(ex, START + 8 * img + 2 * w + 2)
                    if w == 0:
                        pe.wait_ge(oraws, START + img)
                        pe.wait_ge(Vs, START + (gp if jj == 0 else gp + 1))
                    K = TT if kt == 0 else VT - TT
                    for i in range(4):
                        last = nc.tensor.matmul(
                            ps[32 * i:32 * i + 32, O_BANK, g * NT:(g + 1) * NT],
                            Vx[0:K, vb, 2 * vj + kt, 4 * g + i, :],
                            PT[0:K, 2 * (w % 2) + i // 2, (i % 2) * NT:(i % 2 + 1) * NT],
                            start=(kt == 0), stop=(kt == 1))
                    last.then_inc(pv, 1)

                def to_tokens():
                    if not O:
                        return
                    pe.wait_ge(oraws, START + n - 1)
                    if T:
                        pe.wait_ge(nmq, START + 2 * si + 2)
                    else:
                        pe.wait_ge(hA, START + n - 2)
                    for qt in range(2):
                        for g in range(2):
                            last = nc.tensor.transpose(ps[0:TT, R_BANK, (2 * qt + g) * DIM:(2 * qt + g + 1) * DIM],
                                                       oraw[:, g * NT + qt * TT:g * NT + (qt + 1) * TT], ident[:, :])
                    last.then_inc(ot, 1)

                def to_channels():
                    if O:
                        pe.wait_ge(ons, START + n - 1)
                        for qt in range(2):
                            last = nc.tensor.transpose(ps[:, R_BANK, qt * TT:(qt + 1) * TT], on[:, qt, :], ident[0:TT, 0:TT])
                        last.then_inc(t2, 1)

                def project():
                    if O:
                        pe.wait_ge(onTs, START + n - 1)
                        for qt in range(2):
                            last = nc.tensor.matmul(ps[0:TT, R_BANK, qt * DIM:(qt + 1) * DIM], onT[:, qt * TT:(qt + 1) * TT],
                                                    wpj[:, :], start=True, stop=True)
                        last.then_inc(pj, 1)

                scores(0)
                nx(0, "tr")
                nx(1, 4)
                scores(1)
                negmax(0)
                if O:
                    values(n - 2, ob, oj, 3)
                scores(2)
                nx(0, "q")
                negmax(1)
                tscores(0)
                nx(1, 5)
                nx(0, "k")
                scores(3)
                to_tokens()
                tscores(1)
                scores(4)
                to_channels()
                tscores(2)
                if T:
                    values(si, sb_, sj, 0)
                nx(1, 6)
                tscores(3)
                project()
                nx(0, 0)
                scores(5)
                tscores(4)
                nx(0, 1)
                if T:
                    values(si, sb_, sj, 1)
                nx(1, 7)
                scores(6)
                tscores(5)
                nx(0, 2)
                scores(7)
                tscores(6)
                nx(0, 3)
                if T:
                    values(si, sb_, sj, 2)
                nx(1, "v")
                tscores(7)

            with pe.Fori(0, LAYERS) as L:
                g0 = L * NPAIR
                pe.wait_ge(wa_in, 80 * L + 80)
                pe.wait_ge(vone_ready, 1)
                for slot in ("tr", "q", "k", 0, 1, 2, 3, 4, 5, 6, 7, "v"):
                    prep(g0, 0, slot)
                period(g0, 0, 0, True, False, False, True)
                period(g0, 0, 1, True, True, False, True)
                with pe.Fori(0, NPAIR // 2 - 1) as r:
                    p = 2 * r + 1
                    for b in (1, 0):
                        for jj in (0, 1):
                            period(g0 + p + (1 - b), b, jj, True, True, True, True)
                for jj in (0, 1):
                    period(g0 + NPAIR - 1, 1, jj, True, True, True, False)
                for jj in (0, 1):
                    period(g0 + NPAIR, 0, jj, False, jj == 0, True, False)

                pe.wait_ge(wb_in, 48 * L + 48)
                pe.wait_ge(hA, START + g0 * 2 + IMGS)

                def trb(gp):
                    pe.wait_ge(Bz, START + gp + 1)
                    pe.wait_ge(ByT, START + gp)
                    for t in range(4):
                        last = nc.tensor.transpose(ps[:, 0, t * TT:(t + 1) * TT], z[:, t, :], ident[0:TT, 0:TT])
                    last.then_inc(Btr, 1)

                def fc1(gp):
                    pe.wait_ge(ByT, START + gp + 1)
                    pe.wait_ge(Bg, START + 2 * gp)
                    for c in range(2):
                        nc.tensor.matmul(bank(2 + c, 128, W2), w1[:, c * 128:(c + 1) * 128], yT[:, :],
                                         start=True, stop=True).then_inc(Bf1, 1)

                def fc2(gp, b):
                    pe.wait_ge(Bg, START + 2 * gp + 2)
                    pe.wait_ge(hB, START + gp)
                    for t in range(4):
                        for c in range(2):
                            last = nc.tensor.matmul(ps[0:TT, 4 + b, t * DIM:(t + 1) * DIM], gT[:, b, c, t * TT:(t + 1) * TT],
                                                    w2[:, c, :], start=(c == 0), stop=(c == 1))
                    last.then_inc(Bf2, 1)
                trb(g0)
                fc1(g0)
                trb(g0 + 1)
                with pe.Fori(0, NPAIR // 2 - 1) as r:
                    p = 2 * r + 1
                    for b in (1, 0):
                        q = p + (1 - b)
                        fc1(g0 + q)
                        trb(g0 + q + 1)
                        fc2(g0 + q - 1, 1 - b)
                fc1(g0 + NPAIR - 1)
                fc2(g0 + NPAIR - 2, 0)
                fc2(g0 + NPAIR - 1, 1)

            pe.wait_ge(hB, START + 1 + LAYERS * NPAIR)
            pe.wait_ge(w_in, 16 * 22)
            pe.wait_ge(w_dv, 1)
            for h in range(SH):
                nc.tensor.matmul(ps[:, 0, h * SM:(h + 1) * SM], wx[:, h, :], wslT[:, :], start=True, stop=True)
                nc.tensor.matmul(ps[0:TT, 1, h * SM:(h + 1) * SM], bxw[:, h, :], wslT[:, :], start=True, stop=True)
            nc.tensor.matmul(bank(2, SD, SD), wq3[:, 0, :], wq3[:, 1, :], start=True, stop=True)
            for g in range(2):
                last = nc.tensor.matmul(bank(3 + g, SD, 512), wq3[:, 2, :],
                                        woT[:, 4 * g:4 * g + 4, :].rearrange("p h n -> p (h n)"), start=True, stop=True)
            last.then_inc(w_pe, 1)
            pe.wait_ge(w_dv, 3)

            def first_t(p):
                pe.wait_ge(Cz, START + p + 1)
                pe.wait_ge(CxT, START + p)
                for t in range(4):
                    last = nc.tensor.transpose(ps[:, 0, t * TT:(t + 1) * TT], x1e[:, t, 0:DIM], ident[0:TT, 0:TT])
                last.then_inc(Ctr, 1)

            def first_l(p):
                pe.wait_ge(CxT, START + p + 1)
                pe.wait_ge(CL, START + p)
                for t in range(4):
                    last = nc.tensor.matmul(ps[0:TT, 1 + t // 2, (t % 2) * SL:(t % 2 + 1) * SL], yT[:, t * TT:(t + 1) * TT],
                                            wcomb[:, :], start=True, stop=True)
                last.then_inc(Clg, 1)

            def slice_pair(p, more):
                pe.wait_ge(Cw, START + p + 1)
                pe.wait_ge(CEe, START + p)
                pe.wait_ge(CGe, START + p)
                for i in range(2):
                    for c in range(2):
                        for t in range(2):
                            last = nc.tensor.matmul(ps[:, 3 + i, c * (DIM + 1):(c + 1) * (DIM + 1)],
                                                    Lw[:, 2 * i + t, c * 128:(c + 1) * 128], x1e[:, 2 * i + t, :],
                                                    start=(t == 0), stop=(t == 1))
                last.then_inc(CT, 1)
                pe.wait_ge(Cwe, START + p)
                for c in range(2):
                    for t in range(4):
                        last = nc.tensor.transpose(ps[:, 6 + c, t * TT:(t + 1) * TT], Lw[:, t, c * 128:(c + 1) * 128],
                                                   ident[0:TT, 0:TT])
                last.then_inc(Cwt, 1)
                if more:
                    first_t(p + 1)
                pe.wait_ge(CTp, START + p + 1)
                pe.wait_ge(CH, START + p)
                for k in range(4):
                    last = nc.tensor.transpose(ps[:, 5, k * 128:(k + 1) * 128], Tp[:, k, 0:DIM], ident[:, :])
                last.then_inc(CTt, 1)
                if more:
                    first_l(p + 1)
                pe.wait_ge(CTe, START + p + 1)
                for k in range(4):
                    for i in range(4):
                        h = 4 * (k % 2) + i
                        last = nc.tensor.matmul(ps[32 * i:32 * i + 32, 3, k * SD:(k + 1) * SD],
                                                TpT[:, k * 128 + 32 * i:k * 128 + 32 * i + 32],
                                                wfxT[:, h * SD:(h + 1) * SD], start=True, stop=True)
                last.then_inc(Ctk, 1)
                pe.wait_ge(init_done, 1)
                pe.wait_ge(Ctok, START + p + 1)
                for k in range(4):
                    last = nc.tensor.transpose(ps[0:SD, 4, k * 128:(k + 1) * 128], tok[:, k, :], ident[:, :])
                last.then_inc(Ctt, 1)
                pe.wait_ge(init_done, 1)
                pe.wait_ge(Cte, START + p + 1)
                nc.tensor.matmul(bank(3, SD, 512), mqk[:, :], tokT[:, :], start=True, stop=True).then_inc(CA, 1)
                for k in range(4):
                    for i in range(4):
                        h = 4 * (k % 2) + i
                        last = nc.tensor.matmul(ps[32 * i:32 * i + 32, 5, k * DIM:(k + 1) * DIM],
                                                tokT[:, k * 128 + 32 * i:k * 128 + 32 * i + 32],
                                                wvo[:, h, :], start=True, stop=True)
                last.then_inc(CU, 1)
                pe.wait_ge(CAe, START + p + 1)
                for k in range(4):
                    last = nc.tensor.matmul(ps[:, 4, k * 128:(k + 1) * 128], AT[:, k * 128:(k + 1) * 128],
                                            tokT[:, k * 128:(k + 1) * 128], start=True, stop=True)
                last.then_inc(CS, 1)
                pe.wait_ge(CSe, START + p + 1)
                for k in range(4):
                    last = nc.tensor.transpose(ps[:, 3, k * 128:(k + 1) * 128], Sm[:, k, :], ident[:, :])
                last.then_inc(CEt, 1)
                pe.wait_ge(CEe, START + p + 1)
                pe.wait_ge(CUe, START + p + 1)
                for k in range(4):
                    last = nc.tensor.matmul(ps[:, 4, k * 128:(k + 1) * 128], ET[:, k * 128:(k + 1) * 128], Us[:, k, :],
                                            start=True, stop=True)
                last.then_inc(CG, 1)
                pe.wait_ge(CGe, START + p + 1)
                pe.wait_ge(Cwe, START + p + 1)
                for t in range(4):
                    for c in range(2):
                        last = nc.tensor.matmul(ps[0:TT, 5, t * DIM:(t + 1) * DIM], wT[:, c, t * TT:(t + 1) * TT],
                                                Gs[:, 2 * (t // 2) + c, :], start=(c == 0), stop=(c == 1))
                last.then_inc(CO, 1)
            first_t(0)
            first_l(0)
            with pe.Fori(0, NPAIR - 1) as p:
                slice_pair(p, True)
            slice_pair(NPAIR - 1, False)

            with pe.Fori(0, NPAIR) as p:
                pe.wait_ge(Gz, START + p + 1)
                for i in range(2):
                    for t in range(2):
                        last = nc.tensor.matmul(ps[:, 0, ds(p * 2 + i, 1)], z[:, 2 * i + t, :], onec[:, :],
                                                start=(t == 0), stop=(t == 1))
                last.then_inc(Gm, 1)
            pe.wait_ge(Gm, START + NPAIR)
            nc.tensor.matmul(ps[0:1, 1, 0:1], onec[:, :], onec[:, :], start=True, stop=True).then_inc(g_pe, 1)
            pe.wait_ge(g_dv, 1)
            nc.tensor.matmul(bank(1, IMGS, NE), means[:, :], wg[:, :], start=True, stop=True).then_inc(g_pe, 1)
            pe.wait_ge(g_dv, 7)
            nc.tensor.transpose(bank(2, NE, IMGS), onehot[:, :], ident[0:IMGS, 0:IMGS]).then_inc(g_pe, 1)
            pe.wait_ge(g_dv, 8)
            nc.tensor.matmul(bank(3, IMGS, DIM), onehotT[:, :], be[:, :], start=True, stop=True).then_inc(g_pe, 1)

            pe.wait_ge(g_dv, 9)
            pe.wait_ge(g_in, 32)

            def turn(p, b):
                pe.wait_ge(Ez, START + p + 1)
                pe.wait_ge(EzT, START + p - 1)
                for t in range(4):
                    last = nc.tensor.transpose(ps[:, b, t * TT:(t + 1) * TT], z[:, t, :], ident[0:TT, 0:TT])
                last.then_inc(Etr, 1)

            def expert(p, b):
                pe.wait_ge(EzT, START + p + 1)
                pe.wait_ge(Eo, START + p - 1)
                for i in range(2):
                    e = pe.value_load(idxrow[0:1, ds(p * 2 + i, 1)], min_val=0, max_val=NE - 1)
                    for t in (2 * i, 2 * i + 1):
                        last = nc.tensor.matmul(ps[0:TT, 2 + b, t * DIM:(t + 1) * DIM], zT[:, b, t * TT:(t + 1) * TT],
                                                we[:, ds(e, 1), :].rearrange("p a n -> p (a n)"), start=True, stop=True)
                last.then_inc(Ey, 1)
            turn(0, 0)
            with pe.Fori(0, NPAIR // 2 - 1) as r:
                for b in (0, 1):
                    turn(2 * r + b + 1, 1 - b)
                    expert(2 * r + b, b)
            turn(NPAIR - 1, 1)
            expert(NPAIR - 2, 0)
            expert(NPAIR - 1, 1)


def _constants():
    import numpy as np

    heads, hd = 8, 16
    sel = np.zeros((2, 128, 4, 2, 128), np.float32)
    d = np.arange(hd)
    for t in range(heads // 2):
        a, b = 2 * t * hd, (2 * t + 1) * hd
        for which, part, col, row in (
            (0, 0, 0, a), (0, 0, 16, a), (0, 1, 32, a), (0, 1, 48, b), (0, 0, 64, b), (0, 0, 80, b),
            (1, 0, 0, a), (1, 1, 16, a), (1, 0, 32, a), (1, 0, 48, b), (1, 0, 64, b), (1, 1, 80, b),
        ):
            sel[which, row + d, t, part, col + d] = 1.0
    mcols = np.zeros((128, 4), np.float32)
    mcols[0:48, 0] = 1.0
    mcols[48:96, 1] = 1.0
    mcols[96:98, 2] = 1.0
    mcols[98:100, 3] = 1.0
    return sel, mcols


def _inputs(x, cls_tok, a):
    import numpy as np

    B, C, S, _ = x.shape
    P = 16
    G = S // P
    k = C * P * P
    patches = x.reshape(B, C, G, P, G, P).transpose(0, 1, 3, 5, 2, 4).reshape(B, k // 128, 128, G * G).transpose(0, 2, 1, 3)
    sel, mcols = _constants()
    tok = lambda n: a["L0_tok_" + n]
    L, dim = tok("ln1_w").shape
    q_b = tok("qkv_b")
    at = lambda n: a["L0_attn_" + n]
    ff = lambda n: a["L0_ffn_" + n]
    SM, SD = at("Wslice").shape
    SH = at("Wx").shape[0] // SD
    NE = ff("bg").shape[0]
    f1 = tok("fc1_b")
    cols = np.stack([tok("ln1_w"), tok("ln1_b"), q_b[:, 0:dim], q_b[:, dim:2 * dim], tok("ln2_w"), tok("ln2_b"),
                     f1[:, 0:dim], f1[:, dim:2 * dim]], axis=2)
    return {
        "patches": patches, "conv_w": tok("conv_w"), "conv_b_row": tok("conv_b")[None],
        "cls_token": tok("cls_token")[0], "pos": tok("pos_embed")[0], "cls_tok": cls_tok[0],
        "cols": cols, "qkv_w": tok("qkv_w"), "proj_w": tok("proj_w"), "fc1_w": tok("fc1_w"), "fc2_w": tok("fc2_w"),
        "bv_row": q_b[:, None, 2 * dim:], "pb_row": tok("proj_b")[:, None], "fb_row": tok("fc2_b")[:, None],
        "ident": np.eye(128, dtype=np.float32), "mcols": mcols,
        "norm_w_row": tok("norm_w")[None], "norm_b_row": tok("norm_b")[None], "zero_row": np.zeros((1, dim), np.float32),
        "wx": at("Wx"), "bxT": at("bx").reshape(SH, SD).T, "wslT": at("Wslice").T, "bsl_row": at("bslice")[None],
        "temp_row": at("temperature").reshape(1, SH), "wfxT": at("Wfx").T,
        "bfx": np.repeat(at("bfx").reshape(2, 4, 1, SD), SM, axis=2).reshape(2, 4 * SM, SD).transpose(1, 0, 2),
        "wq3": np.stack([at("Wq"), at("Wk"), at("Wv")], axis=1),
        "woT": at("Wout").T.reshape(SH, SD, dim).transpose(1, 0, 2), "bo_row": at("bout")[None],
        "smask": np.where(np.arange(128)[:, None] // SM == np.arange(128)[None] // SM, 0.0, -1e30).astype(np.float32),
        "we": ff("We"), "be": ff("be"), "wg": ff("Wg"), "bg_row": ff("bg")[None],
        "iota_row": np.arange(NE, dtype=np.float32)[None],
        "selq": sel[0].reshape(128, -1), "selk": sel[1].reshape(128, -1),
    }


def kernel(x, cls_tok, **a):
    import numpy as np
    import concourse.bacc as bacc
    from concourse import mybir
    from concourse.bass_utils import run_bass_kernel_spmd

    named = _inputs(np.asarray(x), np.asarray(cls_tok), {k: np.asarray(v) for k, v in a.items()})
    arrays = {f"in_{k}": np.ascontiguousarray(v) for k, v in named.items()}
    nc = bacc.Bacc("TRN2", target_bir_lowering=False, num_devices=1, dynamic_dma_scratch_size=4096)
    D = {k[3:]: nc.dram_tensor(k, v.shape, mybir.dt.from_np(v.dtype), kind="ExternalInput").ap() for k, v in arrays.items()}
    B, NT, DIM = x.shape[0], 198, cls_tok.shape[2]
    out = nc.dram_tensor("out_h", (B, NT, DIM), mybir.dt.float32, kind="ExternalOutput").ap()
    vit_slice_moe(nc, D, out)
    r = run_bass_kernel_spmd(nc, [arrays], core_ids=[0])
    return r.results[0]["out_h"]
```

```python
import concourse.bass as bass
from concourse import mybir
from contextlib import ExitStack


def vit_slice_moe(nc, D, out):
    f32 = mybir.dt.float32
    f32r = mybir.dt.float32r
    i32 = mybir.dt.int32
    ALU = mybir.AluOpType
    ACT = mybir.ActivationFunctionType
    AX = mybir.AxisListType
    ds = bass.ds

    IMGS, _, KCH, NPATCH = D["patches"].shape
    LAYERS = D["qkv_w"].shape[0]
    DIM = 128
    HEADS = 8
    HD = DIM // HEADS
    TT = 99
    NT = 2 * TT
    VT = NT - 1
    R_CLS = NPATCH - TT
    R_OUT = R_CLS + 1
    NPAIR = IMGS // 2
    W2 = 2 * NT
    HID = D["fc1_w"].shape[2]
    EPS = 1e-5
    SCALE = float(HD) ** -0.5
    NBUF = 4
    START = 24

    ctx = ExitStack()
    with ctx:
        def sb(name, shape, dt=f32):
            return ctx.enter_context(nc.sbuf_tensor(name, shape, dt))

        def sem(name):
            return ctx.enter_context(nc.semaphore(name))

        H = sb("H", [TT, 2 * IMGS, DIM])
        ident = sb("ident", [128, 128])
        z = sb("z", [TT, 4, DIM])
        yT = sb("yT", [128, W2])
        bnst = sb("bnst", [TT, 2, 4, 6])
        mv = sb("mv", [TT, 2, 4, 2])
        ve = sb("ve", [TT, 2, 4])
        rstd = sb("rstd", [TT, 2, 4])
        half = sb("half", [TT, 4])
        spare = sb("spare", [1, 1])
        spare2 = sb("spare2", [1, 1])

        tower = ExitStack()

        def tb(name, shape, dt=f32):
            return tower.enter_context(nc.sbuf_tensor(name, shape, dt))

        U = tb("U", [128, NBUF * KCH * NPATCH])
        patch = U[:, :].rearrange("p (n c t) -> p n c t", n=NBUF, c=KCH)
        NV = 2 * 4 * HEADS * 32
        Vx = U[0:TT, 0:NV].rearrange("p (b t h e) -> p b t h e", b=2, t=4, h=HEADS)
        PT = U[0:TT, NV:NV + 4 * W2].rearrange("p (r c) -> p r c", r=4)
        gT = U[:, NV:NV + 4 * W2].rearrange("p (b c n) -> p b c n", b=2, c=2)
        qs = tb("qs", [128, 2, 4, W2], f32r)
        ks = tb("ks", [128, 2, HEADS, W2], f32r)
        qhi = tb("qhi", [128, W2], f32r)
        qlo = tb("qlo", [128, W2], f32r)
        khi = tb("khi", [128, W2], f32r)
        klo = tb("klo", [128, W2], f32r)
        oraw = tb("oraw", [128, W2])
        on = tb("on", [TT, 2, DIM])
        onT = tb("onT", [128, NT])
        mx = tb("mx", [TT, 2, HEADS])
        M2 = tb("M2", [TT, 2, 4, 32])
        rec = tb("rec", [TT, 2 * HEADS])
        mcols = tb("mcols", [128, 4])
        selq = tb("selq", [128, 4, 2, 128], f32r)
        selk = tb("selk", [128, 4, 2, 128], f32r)
        addend = tb("addend", [TT, 2, DIM])
        rowb = tb("rowb", [TT, DIM])
        clsrow = tb("clsrow", [1, 2, DIM])
        wc = tb("wc", [128, KCH, DIM])
        wqkv = tb("wqkv", [128, 3 * DIM])
        wpj = tb("wpj", [128, DIM])
        w1 = tb("w1", [128, HID])
        w2 = tb("w2", [128, 2, DIM])
        cols = tb("cols", [128, 8])
        bvrow = tb("bvrow", [TT, DIM])
        pbrow = tb("pbrow", [TT, DIM])
        fbrow = tb("fbrow", [TT, DIM])
        tower.close()

        SH, SM, SD = 8, 32, 64
        SL = SH * SM
        wnorm = sb("wnorm", [TT, 2, DIM])
        bnorm = sb("bnorm", [TT, 2, DIM])
        wx = sb("wx", [SD, SH, DIM])
        bx = sb("bx", [SD, SH])
        bxw = sb("bxw", [SD, SH, TT])
        wslT = sb("wslT", [SD, SM])
        bsl = sb("bsl", [TT, SM])
        rtemp = sb("rtemp", [128, SH])
        wcomb = sb("wcomb", [128, SL])
        bcomb = sb("bcomb", [TT, SL])
        wfxT = sb("wfxT", [128, SH * SD])
        bfx = sb("bfx", [128, 2, SD])
        wq3 = sb("wq3", [SD, 3, SD])
        mqk = sb("mqk", [SD, SD])
        woT = sb("woT", [SD, SH, DIM])
        wvo = sb("wvo", [SD, SH, DIM])
        smask = sb("smask", [128, 128])
        borow = sb("borow", [TT, DIM])
        x1e = sb("x1e", [TT, 2, 4, DIM + 1])
        Lw = sb("Lw", [TT, 2, 4, SL])
        gmx = sb("gmx", [TT, 4 * SH])
        gsum = sb("gsum", [TT, 4 * SH])
        grec = sb("grec", [TT, 4 * SH])
        wT = sb("wT", [128, 2, 2, W2])
        Tp = sb("Tp", [128, 4, DIM + 1])
        seps = sb("seps", [128, 4])
        srec = sb("srec", [128, 4])
        TpT = sb("TpT", [128, 512])
        tok = sb("tok", [128, 4, SD])
        tokT = sb("tokT", [SD, 512])
        AT = sb("AT", [SD, 512])
        Us = sb("Us", [128, 4, DIM])
        Sm = sb("Sm", [128, 4, 128])
        rmx = sb("rmx", [128, 4])
        nmx = sb("nmx", [128, 4])
        asum = sb("asum", [128, 4])
        arec = sb("arec", [128, 4])
        ET = sb("ET", [128, 512])
        Gs = sb("Gs", [128, 4, DIM])
        NE = D["be"].shape[0]
        we = sb("we", [128, NE, DIM])
        wg = sb("wg", [128, NE])
        bg = sb("bg", [IMGS, NE])
        be = sb("be", [NE, DIM])
        iota = sb("iota", [IMGS, NE])
        onec = sb("onec", [TT, 1])
        mvall = sb("mvall", [TT, 2 * IMGS])
        rall = sb("rall", [TT, 2 * IMGS])
        means = sb("means", [128, IMGS])
        lg = sb("lg", [IMGS, NE])
        top = sb("top", [IMGS, 8])
        topi = sb("topi", [IMGS, 8], mybir.dt.uint32)
        ntop = sb("ntop", [IMGS, 1])
        topf = sb("topf", [IMGS, 1])
        lge = sb("lge", [IMGS, NE])
        lsum = sb("lsum", [IMGS, 1])
        gate = sb("gate", [IMGS, 1])
        onehot = sb("onehot", [IMGS, NE])
        onehotT = sb("onehotT", [NE, IMGS])
        gbe = sb("gbe", [IMGS, DIM])
        gateb = sb("gateb", [TT, IMGS])
        idxrow = sb("idxrow", [1, IMGS], mybir.dt.uint32)
        GB = sb("GB", [TT, 2, 2, DIM])
        OB = sb("OB", [TT, 2, 4, DIM])
        zT = sb("zT", [128, 2, W2])

        gate_d = nc.dram_tensor("gate_d", [1, IMGS], f32).ap()
        idx_d = nc.dram_tensor("idx_d", [1, IMGS], mybir.dt.uint32).ap()
        gbe_d = nc.dram_tensor("gbe_d", [IMGS, DIM], f32).ap()
        ps = ctx.enter_context(nc.psum_tensor("ps", [128, 8, 512], f32))
        S_BANK, T_BANK, O_BANK, P_BANK, R_BANK = 0, 2, 4, 5, 7

        c_in = sem("c_in")
        c_rows = sem("c_rows")
        p_in = [sem(f"p_in{i}") for i in range(NBUF)]
        wa_in = sem("wa_in")
        wb_in = sem("wb_in")
        init_done = sem("init_done")
        sel_cast = sem("sel_cast")
        add_ready = sem("add_ready")
        emb_done = sem("emb_done")
        vone_ready = sem("vone_ready")
        counters = []

        def counter(name):
            counters.append(sem(name))
            return counters[-1]

        att_stats = counter("att_stats")
        att_meanvar = counter("att_meanvar")
        att_var_eps = counter("att_var_eps")
        att_rstd = counter("att_rstd")
        att_centred = counter("att_centred")
        att_normed = counter("att_normed")
        att_normedT = counter("att_normedT")
        att_affine = counter("att_affine")
        q_projected = counter("q_projected")
        q_high = counter("q_high")
        q_low = counter("q_low")
        k_projected = counter("k_projected")
        k_high = counter("k_high")
        k_low = counter("k_low")
        v_projected = counter("v_projected")
        v_in = counter("v_in")
        stacked = counter("stacked")
        stack_by_act = counter("stack_by_act")
        stack_by_dve = counter("stack_by_dve")
        att_bias_in = counter("att_bias_in")
        embedded = counter("embedded")
        scores_ready = counter("scores_ready")
        scores_reduced = counter("scores_reduced")
        negmax_high = counter("negmax_high")
        negmax_split = counter("negmax_split")
        negmaxT = counter("negmaxT")
        negmax_in = counter("negmax_in")
        scoresT_ready = counter("scoresT_ready")
        probs_ready = counter("probs_ready")
        values_summed = counter("values_summed")
        out_copied = counter("out_copied")
        out_tokens = counter("out_tokens")
        out_sums_inverted = counter("out_sums_inverted")
        out_normed = counter("out_normed")
        out_normedT = counter("out_normedT")
        out_normedT_in = counter("out_normedT_in")
        projected = counter("projected")
        att_added = counter("att_added")
        mlp_stats = counter("mlp_stats")
        mlp_meanvar = counter("mlp_meanvar")
        mlp_var_eps = counter("mlp_var_eps")
        mlp_rstd = counter("mlp_rstd")
        mlp_normed = counter("mlp_normed")
        mlp_normedT = counter("mlp_normedT")
        mlp_affine = counter("mlp_affine")
        mlp_hidden = counter("mlp_hidden")
        mlp_gelu = counter("mlp_gelu")
        mlp_out = counter("mlp_out")
        mlp_bias_in = counter("mlp_bias_in")
        tower_added = counter("tower_added")
        fin_stats = counter("fin_stats")
        fin_meanvar = counter("fin_meanvar")
        fin_var_eps = counter("fin_var_eps")
        fin_rstd = counter("fin_rstd")
        fin_normed = counter("fin_normed")
        fin_weighted = counter("fin_weighted")
        fin_done = counter("fin_done")
        sl_stats = counter("sl_stats")
        sl_meanvar = counter("sl_meanvar")
        sl_var_eps = counter("sl_var_eps")
        sl_rstd = counter("sl_rstd")
        sl_normed = counter("sl_normed")
        sl_normedT = counter("sl_normedT")
        sl_normedT_in = counter("sl_normedT_in")
        sl_logits = counter("sl_logits")
        sl_logits_in = counter("sl_logits_in")
        sl_max = counter("sl_max")
        sl_shifted = counter("sl_shifted")
        sl_exp = counter("sl_exp")
        sl_sum = counter("sl_sum")
        sl_sum_inverted = counter("sl_sum_inverted")
        sl_weights = counter("sl_weights")
        sl_sums = counter("sl_sums")
        sl_norm_eps = counter("sl_norm_eps")
        sl_norm_inverted = counter("sl_norm_inverted")
        sl_mean = counter("sl_mean")
        sl_meanT = counter("sl_meanT")
        sl_meanT_in = counter("sl_meanT_in")
        sl_weightsT = counter("sl_weightsT")
        sl_weightsT_in = counter("sl_weightsT_in")
        sl_tokens = counter("sl_tokens")
        sl_tokens_in = counter("sl_tokens_in")
        sl_tokensT = counter("sl_tokensT")
        sl_tokensT_in = counter("sl_tokensT_in")
        sl_keys = counter("sl_keys")
        sl_keys_in = counter("sl_keys_in")
        sl_values = counter("sl_values")
        sl_values_in = counter("sl_values_in")
        sl_scores = counter("sl_scores")
        sl_scores_masked = counter("sl_scores_masked")
        sl_score_max = counter("sl_score_max")
        sl_score_negmax = counter("sl_score_negmax")
        sl_probs = counter("sl_probs")
        sl_probsT = counter("sl_probsT")
        sl_probsT_in = counter("sl_probsT_in")
        sl_prob_sums_inverted = counter("sl_prob_sums_inverted")
        sl_mixed = counter("sl_mixed")
        sl_mixed_in = counter("sl_mixed_in")
        sl_out = counter("sl_out")
        sl_bias_in = counter("sl_bias_in")
        sl_added = counter("sl_added")
        gate_stats = counter("gate_stats")
        gate_meanvar = counter("gate_meanvar")
        gate_var_eps = counter("gate_var_eps")
        gate_rstd = counter("gate_rstd")
        gate_kept = counter("gate_kept")
        gate_centred = counter("gate_centred")
        gate_normed = counter("gate_normed")
        gate_sums = counter("gate_sums")
        exp_bias_in = counter("exp_bias_in")
        exp_normed = counter("exp_normed")
        exp_normedT = counter("exp_normedT")
        exp_normedT_in = counter("exp_normedT_in")
        exp_out = counter("exp_out")
        exp_added = counter("exp_added")
        w_in = sem("w_in")
        w_pe = sem("w_pe")
        w_dv = sem("w_dv")
        w_pl = sem("w_pl")
        g_pe = sem("g_pe")
        g_dv = sem("g_dv")
        g_act = sem("g_act")
        g_out = sem("g_out")
        g_in = sem("g_in")
        gb_in = [sem(f"gb_in{i}") for i in range(2)]
        o_out = [sem(f"o_out{i}") for i in range(2)]

        block = ctx.enter_context(nc.Block())

        def bank(i, rows, cols_):
            return ps[0:rows, i, 0:cols_]

        STEPS = HEADS
        ON_DVE = (1,)
        ON_ACT = tuple(s for s in range(STEPS) if s not in ON_DVE)

        def copied(q, s):
            mine, done = (ON_DVE, stack_by_dve) if s in ON_DVE else (ON_ACT, stack_by_act)
            return done, START + len(mine) * q + mine.index(s) + 1

        def last_read(q, s):
            return START + 16 * (q - 1) - (4 if s < 4 else 0)

        @block.sync
        def _(sp):
            sp.dma_start(ident[:, :], D["ident"]).then_inc(c_in, 16)
            sp.dma_start(mcols[:, :], D["mcols"]).then_inc(c_in, 16)
            sp.dma_start(U[:, 1024:2048], D["selq"]).then_inc(c_in, 16)
            sp.dma_start(U[:, 0:1024], D["selk"]).then_inc(c_in, 16)
            sp.dma_start(wc[:, :, :], D["conv_w"].rearrange("(c p) n -> p c n", p=128)).then_inc(c_in, 16)
            sp.dma_start(addend[:, 0, :], D["pos"][1:1 + TT, :]).then_inc(c_in, 16)
            sp.dma_start(addend[0:R_CLS, 1, :], D["pos"][1 + TT:1 + NPATCH, :]).then_inc(c_in, 16)
            sp.dma_start(rowb[:, :], D["conv_b_row"].to_broadcast([TT, DIM])).then_inc(c_in, 16)
            sp.dma_start(clsrow[:, 0, :], D["cls_token"]).then_inc(c_in, 16)
            sp.dma_start(clsrow[:, 1, :], D["pos"][0:1, :]).then_inc(c_in, 16)

            sp.wait_ge(sel_cast, 2)
            for b in range(NBUF):
                sp.dma_start(U[:, b * KCH * NPATCH:(b + 1) * KCH * NPATCH],
                             D["patches"][b].rearrange("p c t -> p (c t)")).then_inc(p_in[b], 16)
            sp.wait_ge(add_ready, 2)
            odd = H[:, :, :].rearrange("p (n two) d -> p n two d", two=2)
            sp.dma_start(odd[R_CLS:R_CLS + 1, :, 1, :], clsrow[:, 0:1, :].to_broadcast([1, IMGS, DIM])).then_inc(c_rows, 16)
            sp.dma_start(odd[R_OUT:R_OUT + 1, :, 1, :], D["cls_tok"].unsqueeze(1).to_broadcast([1, IMGS, DIM])).then_inc(c_rows, 16)
            with sp.Fori(1, IMGS // NBUF) as it:
                for b in range(NBUF):
                    sp.wait_ge(emb_done, it * NBUF + (b - NBUF + 1))
                    sp.dma_start(U[:, b * KCH * NPATCH:(b + 1) * KCH * NPATCH],
                                 D["patches"][ds(it * NBUF + b, 1)].rearrange("a p c t -> (a p) (c t)")).then_inc(p_in[b], 16)

            with sp.Fori(0, LAYERS) as L:
                lay = lambda name: D[name][ds(L, 1)].rearrange("a p n -> (a p) n")
                sp.wait_ge(att_added, L * IMGS + START)
                sp.dma_start(wqkv[:, :], lay("qkv_w")).then_inc(wa_in, 16)
                sp.dma_start(wpj[:, :], lay("proj_w")).then_inc(wa_in, 16)
                sp.dma_start(bvrow[:, :], lay("bv_row").to_broadcast([TT, DIM])).then_inc(wa_in, 16)
                sp.dma_start(pbrow[:, :], lay("pb_row").to_broadcast([TT, DIM])).then_inc(wa_in, 16)
                sp.wait_ge(tower_added, L * NPAIR + START + 1)
                sp.dma_start(cols[:, :], lay("cols")).then_inc(wa_in, 16)
                sp.dma_start(w1[:, :], lay("fc1_w")).then_inc(wb_in, 16)
                sp.dma_start(w2[:, :, :], D["fc2_w"][ds(L, 1)].rearrange("a (c p) n -> p (a c) n", p=128)).then_inc(wb_in, 16)
                sp.dma_start(fbrow[:, :], lay("fb_row").to_broadcast([TT, DIM])).then_inc(wb_in, 16)

            sp.wait_ge(tower_added, START + 1 + LAYERS * NPAIR)
            loads = [
                (wnorm[:, 0, :], D["norm_w_row"].to_broadcast([TT, DIM])),
                (wnorm[0:R_OUT, 1, :], D["norm_w_row"].to_broadcast([R_OUT, DIM])),
                (wnorm[R_OUT:TT, 1, :], D["zero_row"]),
                (bnorm[:, 0, :], D["norm_b_row"].to_broadcast([TT, DIM])),
                (bnorm[0:R_OUT, 1, :], D["norm_b_row"].to_broadcast([R_OUT, DIM])),
                (bnorm[R_OUT:TT, 1, :], D["cls_tok"]),
                (wx[:, :, :], D["wx"].rearrange("(h d) n -> d h n", h=SH)),
                (bx[:, :], D["bxT"]),
                (wslT[:, :], D["wslT"]),
                (bsl[:, :], D["bsl_row"].to_broadcast([TT, SM])),
                (rtemp[:, :], D["temp_row"].to_broadcast([128, SH])),
                (wfxT[:, :], D["wfxT"]),
                (bfx[:, :, :], D["bfx"]),
                (wq3[:, :, :], D["wq3"]),
                (woT[:, :, :], D["woT"]),
                (smask[:, :], D["smask"]),
                (borow[:, :], D["bo_row"].to_broadcast([TT, DIM])),
                (we[:, :, :], D["we"].rearrange("e d o -> d e o")),
                (wg[:, :], D["wg"]),
                (bg[:, :], D["bg_row"].to_broadcast([IMGS, NE])),
                (be[:, :], D["be"]),
                (iota[:, :], D["iota_row"].to_broadcast([IMGS, NE])),
            ]
            for dst, src in loads:
                sp.dma_start(dst, src).then_inc(w_in, 16)

            sp.wait_ge(g_dv, 9)
            sp.dma_start(gate_d.rearrange("a n -> n a"), gate[:, :]).then_inc(g_out, 16)
            sp.dma_start(idx_d.rearrange("a n -> n a"), topi[:, 0:1]).then_inc(g_out, 16)
            sp.dma_start(gbe_d, gbe[:, :]).then_inc(g_out, 16)
            sp.wait_ge(g_out, 48)
            sp.dma_start(gateb[:, :], gate_d.to_broadcast([TT, IMGS])).then_inc(g_in, 16)
            sp.dma_start(idxrow[:, :], idx_d).then_inc(g_in, 16)

            def load_gbe(p, b):
                sp.dma_start(GB[:, b, :, :], gbe_d[ds(p * 2, 2), :].unsqueeze(0).to_broadcast([TT, 2, DIM])).then_inc(gb_in[b], 16)

            sp.wait_ge(init_done, 1)

            def store(p, b):
                sp.wait_ge(exp_added, START + p + 1)
                ob = OB[:, b, :, :].rearrange("p (i two) d -> p i two d", two=2)
                dst = out[ds(p * 2, 2), :, :].rearrange("i t d -> t i d")
                sp.dma_start(dst[2:2 + TT], ob[:, :, 0, :]).then_inc(o_out[b], 16)
                sp.dma_start(dst[2 + TT:NT], ob[0:R_CLS, :, 1, :]).then_inc(o_out[b], 16)
                sp.dma_start(dst[1:2], ob[R_CLS:R_CLS + 1, :, 1, :]).then_inc(o_out[b], 16)
                sp.dma_start(dst[0:1], ob[R_OUT:R_OUT + 1, :, 1, :]).then_inc(o_out[b], 16)
            load_gbe(0, 0)
            load_gbe(1, 1)
            with sp.Fori(0, NPAIR // 2 - 1) as r:
                for b in (0, 1):
                    p = 2 * r + b
                    sp.wait_ge(exp_bias_in, START + p + 1)
                    load_gbe(p + 2, b)
                    store(p, b)
            store(NPAIR - 2, 0)
            store(NPAIR - 1, 1)
            for b in range(2):
                sp.wait_ge(o_out[b], START + 64 * (NPAIR // 2))

        @block.gpsimd
        def _(pool):
            nc.gpsimd.memset(spare[:, :], 0.0)
            for each in counters + o_out:
                pool.sem_inc(each, START)
            nc.gpsimd.memset(half[:, :], -0.5)
            nc.gpsimd.memset(M2[:, :, :, :], 0.0).then_inc(init_done, 1)
            pool.wait_ge(emb_done, IMGS)
            nc.gpsimd.memset(Vx[:, :, :, :, HD:32], 1.0).then_inc(vone_ready, 1)

            def inv_std(gp, b, s_ve, s_z, s_pw):
                pool.wait_ge(s_ve, START + gp + 1)
                pool.wait_ge(s_z, START + gp - 1)
                nc.gpsimd.tensor_tensor(rstd[:, b, :], ve[:, b, :], half[:, :], ALU.pow).then_inc(s_pw, 1)

            def add_row(gp, p, s_z, row, s_out):
                pool.wait_ge(init_done, 1)
                pool.wait_ge(s_z, START + gp + 1)
                nc.gpsimd.tensor_tensor(H[:, ds(p * 4, 4), :], H[:, ds(p * 4, 4), :],
                                        row[:, :].unsqueeze(1).to_broadcast([TT, 4, DIM]), ALU.add).then_inc(s_out, 1)

            def normed(gp, p, b):
                pool.wait_ge(att_normedT, START + gp)
                nc.gpsimd.tensor_tensor(z[:, :, :], H[:, ds(p * 4, 4), :], mv[:, b, :, 0:1].to_broadcast([TT, 4, DIM]),
                                        ALU.subtract).then_inc(att_centred, 1)
                pool.wait_ge(att_centred, START + gp + 1)
                pool.wait_ge(att_rstd, START + gp + 1)
                nc.gpsimd.tensor_tensor(z[:, :, :], z[:, :, :], rstd[:, b, :].unsqueeze(2).to_broadcast([TT, 4, DIM]),
                                        ALU.mult).then_inc(att_normed, 1)

            with pool.Fori(0, LAYERS) as L:
                g0 = L * NPAIR

                def bias(p):
                    add_row(g0 + p, p, att_normed, pbrow, att_bias_in)

                def pair(p, b):
                    pool.wait_ge(wa_in, 80 * L + 80)
                    inv_std(g0 + p, b, att_var_eps, att_normed, att_rstd)
                    normed(g0 + p, p, b)
                    bias(p)
                with pool.Fori(0, NPAIR // 2) as r:
                    for b in (0, 1):
                        pair(2 * r + b, b)

                pool.wait_ge(wb_in, 48 * L + 48)
                inv_std(g0, 0, mlp_var_eps, mlp_normed, mlp_rstd)
                with pool.Fori(0, NPAIR // 2 - 1) as r:
                    for b in (0, 1):
                        p = 2 * r + b
                        inv_std(g0 + p + 1, 1 - b, mlp_var_eps, mlp_normed, mlp_rstd)
                        add_row(g0 + p, p, mlp_normed, fbrow, mlp_bias_in)
                inv_std(g0 + NPAIR - 1, 1, mlp_var_eps, mlp_normed, mlp_rstd)
                for p in (NPAIR - 2, NPAIR - 1):
                    add_row(g0 + p, p, mlp_normed, fbrow, mlp_bias_in)

            pool.wait_ge(tower_added, START + 1 + LAYERS * NPAIR)
            pool.wait_ge(w_in, 16 * 22)
            nc.gpsimd.memset(x1e[:, :, :, DIM:DIM + 1], 1.0)
            nc.gpsimd.memset(onec[:, :], 1.0).then_inc(w_pl, 1)

            def last_weight(p, b):
                pool.wait_ge(fin_normed, START + p + 1)
                for i in range(2):
                    two = x1e[:, b, 2 * i:2 * i + 2, 0:DIM]
                    last = nc.gpsimd.tensor_tensor(two, two, wnorm[:, :, :], ALU.mult)
                last.then_inc(fin_weighted, 1)
            inv_std(0, 0, fin_var_eps, fin_normed, fin_rstd)
            with pool.Fori(0, NPAIR // 2 - 1) as r:
                for b in (0, 1):
                    inv_std(2 * r + b + 1, 1 - b, fin_var_eps, fin_normed, fin_rstd)
                    last_weight(2 * r + b, b)
            inv_std(NPAIR - 1, 1, fin_var_eps, fin_normed, fin_rstd)
            last_weight(NPAIR - 2, 0)
            last_weight(NPAIR - 1, 1)

            def slice_step(p, b, A=True):
                f = p + 2
                lv = Lw[:, b, :, :].rearrange("p t (h m) -> p (t h) m", m=SM)
                pool.wait_ge(sl_normed, START + f + 1)
                nc.gpsimd.tensor_tensor(H[:, ds(f * 4, 4), :], H[:, ds(f * 4, 4), :],
                                        borow[:, :].unsqueeze(1).to_broadcast([TT, 4, DIM]), ALU.add).then_inc(sl_bias_in, 1)
                pool.wait_ge(sl_max, START + f + 1)
                nc.gpsimd.tensor_tensor(lv, lv, gmx[:, :].unsqueeze(2).to_broadcast([TT, 4 * SH, SM]),
                                        ALU.subtract).then_inc(sl_shifted, 1)
                pool.wait_ge(sl_sum_inverted, START + f + 1)
                nc.gpsimd.tensor_tensor(lv, lv, grec[:, :].unsqueeze(2).to_broadcast([TT, 4 * SH, SM]),
                                        ALU.mult).then_inc(sl_weights, 1)
                if A:
                    inv_std(p + 4, b, sl_var_eps, sl_normed, sl_rstd)
            inv_std(0, 0, sl_var_eps, sl_normed, sl_rstd)
            inv_std(1, 1, sl_var_eps, sl_normed, sl_rstd)
            slice_step(-2, 0)
            slice_step(-1, 1)
            with pool.Fori(0, NPAIR // 2 - 2) as r:
                for b in (0, 1):
                    slice_step(2 * r + b, b)
            slice_step(NPAIR - 4, 0, A=False)
            slice_step(NPAIR - 3, 1, A=False)
            with pool.Fori(0, NPAIR // 2) as r:
                for b in (0, 1):
                    p = 2 * r + b
                    pool.wait_ge(gate_kept, START + p - 1)
                    inv_std(p, b, gate_var_eps, gate_normed, gate_rstd)
                    pool.wait_ge(gate_sums, START + p - 1)
                    nc.gpsimd.tensor_tensor(x1e[:, b, :, 0:DIM], H[:, ds(p * 4, 4), :],
                                            mv[:, b, :, 0:1].to_broadcast([TT, 4, DIM]), ALU.subtract).then_inc(gate_centred, 1)
            with pool.Fori(0, NPAIR // 2) as r:
                for b in (0, 1):
                    p = 2 * r + b
                    pool.wait_ge(gb_in[b], 16 * r + 16)
                    pool.wait_ge(exp_normed, START + p + 1)
                    for i in range(2):
                        hh = H[:, ds(p * 4 + 2 * i, 2), :]
                        last = nc.gpsimd.tensor_tensor(hh, hh, GB[:, b, i:i + 1, :].to_broadcast([TT, 2, DIM]), ALU.add)
                    last.then_inc(exp_bias_in, 1)

        @block.vector
        def _(dve):
            dve.wait_ge(init_done, 1)
            dve.wait_ge(c_in, 160)
            nc.vector.tensor_copy(selq[:, :, :, :], U[:, 1024:2048].rearrange("p (a b c) -> p a b c", a=4, b=2)).then_inc(sel_cast, 1)
            nc.vector.tensor_copy(selk[:, :, :, :], U[:, 0:1024].rearrange("p (a b c) -> p a b c", a=4, b=2)).then_inc(sel_cast, 1)
            nc.vector.tensor_tensor(clsrow[:, 0, :], clsrow[:, 0, :], clsrow[:, 1, :], ALU.add).then_inc(add_ready, 1)
            nc.vector.tensor_tensor(addend[:, 0, :], addend[:, 0, :], rowb[:, :], ALU.add)
            nc.vector.tensor_tensor(addend[0:R_CLS, 1, :], addend[0:R_CLS, 1, :], rowb[0:R_CLS, :], ALU.add).then_inc(add_ready, 1)
            dve.wait_ge(add_ready, 2)
            with dve.Fori(0, IMGS // NBUF) as it:
                for b in range(NBUF):
                    dve.wait_ge(emb_done, it * NBUF + b + 1)
                    nc.vector.tensor_tensor(H[:, ds((it * NBUF + b) * 2, 1), :], ps[0:TT, b:b + 1, 0:DIM],
                                            addend[:, 0:1, :], ALU.add)
                    nc.vector.tensor_tensor(H[0:R_CLS, ds((it * NBUF + b) * 2 + 1, 1), :], ps[0:R_CLS, b:b + 1, DIM:2 * DIM],
                                            addend[0:R_CLS, 1:2, :], ALU.add).then_inc(embedded, 1)
            for e in range(2):
                for b in range(2):
                    nc.vector.tensor_copy(ks[96:128, b, e:HEADS:2, :],
                                          mcols[96:128, 2 + e:3 + e].unsqueeze(2).to_broadcast([32, HEADS // 2, W2]))
            dve.wait_ge(embedded, START + IMGS)
            dve.wait_ge(c_rows, 32)
            nc.vector.memset(spare[:, :], 0.0).then_inc(tower_added, 1)

            def stats(gp, p, b, s_bn, s_agg, s_ve, s_pw, s_z):
                dve.wait_ge(s_z, START + gp - 1)
                for t in range(4):
                    last = nc.vector.bn_stats(bnst[:, b, t, :], H[:, ds(p * 4 + t, 1), :].rearrange("p a d -> p (a d)"))
                last.then_inc(s_bn, 1)
                dve.wait_ge(s_bn, START + gp + 1)
                nc.vector.memset(spare2[:, :], 0.0)
                for t in range(4):
                    last = nc.vector.bn_aggr(mv[:, b, t, :], bnst[:, b, t, :])
                last.then_inc(s_agg, 1)
                dve.wait_ge(s_agg, START + gp + 1)
                dve.wait_ge(s_pw, START + gp - 1)
                nc.vector.tensor_scalar(ve[:, b, :], mv[:, b, :, 1], EPS, None, ALU.add).then_inc(s_ve, 1)

            def normalise(dst, p, b):
                for t in range(4):
                    last = nc.vector.tensor_scalar(dst[:, t, 0:DIM], H[:, ds(p * 4 + t, 1), :].rearrange("p a d -> p (a d)"),
                                                   mv[:, b, t, 0:1], rstd[:, b, t:t + 1], ALU.subtract, ALU.mult)
                return last

            def normed(gp, p, b, s_pw, s_z, s_tr):
                dve.wait_ge(s_pw, START + gp + 1)
                dve.wait_ge(s_tr, START + gp)
                normalise(z, p, b).then_inc(s_z, 1)

            def low_parts(gp, src, bias, hi, lo, s_hi, s_sel, s_lo, selcount):
                dve.wait_ge(s_hi, START + gp + 1)
                dve.wait_ge(s_sel, selcount)
                nc.vector.scalar_tensor_tensor(out=lo[:, :], in0=src, scalar=bias, in1=hi[:, :].bitcast(f32),
                                               op0=ALU.add, op1=ALU.subtract).then_inc(s_lo, 1)

            def prep(gp, p, b, slot):
                if slot == "stats":
                    stats(gp, p, b, att_stats, att_meanvar, att_var_eps, att_rstd, att_normed)
                if slot == "qlo":
                    low_parts(gp, bank(P_BANK + 1, 128, W2), cols[:, 2:3], qhi, qlo, q_high, stacked, q_low, START + 8 * gp)
                if slot == "klo":
                    low_parts(gp, bank(P_BANK, 128, W2), cols[:, 3:4], khi, klo, k_high, stacked, k_low, START + 8 * gp)
                if isinstance(slot, int):
                    dve.wait_ge(stacked, START + STEPS * gp + slot + 1)
                    dve.wait_ge(scoresT_ready, last_read(gp, slot))
                    for e in range(2):
                        last = nc.vector.tensor_scalar(ks[0:96, b, slot - 1 + e, :], bank(P_BANK, 96, W2),
                                                       mcols[0:96, e:e + 1], None, ALU.mult)
                    last.then_inc(stack_by_dve, 1)
                if slot == "V":
                    dve.wait_ge(v_projected, START + gp + 1)
                    dve.wait_ge(values_summed, START + 8 * (gp - 1))
                    for t in range(4):
                        last = nc.vector.tensor_tensor(
                            Vx[:, b, t, :, 0:HD],
                            ps[0:TT, P_BANK + 1, t * DIM:(t + 1) * DIM].rearrange("p (h d) -> p h d", h=HEADS),
                            bvrow[:, :].rearrange("p (h d) -> p h d", h=HEADS), ALU.add)
                    last.then_inc(v_in, 1)

            def period(gp, p, b, jj, S, O, P, P2):
                n = gp * 2 + jj

                def smx(u):
                    if not S:
                        return
                    dve.wait_ge(scores_ready, START + 8 * n + u + 1)
                    if u == 0:
                        dve.wait_ge(negmax_split, START + n)
                    t, qt = u // 2, u % 2
                    nc.vector.reduce_max(mx[:, qt, 2 * t:2 * t + 2],
                                         bank(S_BANK + u % 2, TT, W2).rearrange("p (e m) -> p e m", e=2)[:, :, 0:VT],
                                         AX.X).then_inc(scores_reduced, 1)

                def nx(j, slot):
                    if P and j == jj:
                        prep(gp + 1, p + 1, 1 - b, slot)

                def nx2(j, slot):
                    if P2 and j == jj:
                        prep(gp + 2, p + 2, b, slot)
                smx(0)
                smx(1)
                nx2(0, "stats")
                smx(2)
                nx(0, "qlo")
                if O:
                    dve.wait_ge(out_tokens, START + n - 1)
                    src = bank(R_BANK, TT, 512).rearrange("p (x e) -> p x e", e=32)
                    nc.vector.reciprocal(rec[:, :], src[:, :, HD]).then_inc(out_sums_inverted, 1)
                    dve.wait_ge(out_sums_inverted, START + n - 1)
                    dve.wait_ge(out_normedT, START + n - 2)
                    nc.vector.tensor_tensor(on[:, :, :].rearrange("p q (x e) -> p (q x) e", e=HD), src[:, :, 0:HD],
                                            rec[:, :].unsqueeze(2).to_broadcast([TT, 2 * HEADS, HD]),
                                            ALU.mult).then_inc(out_normed, 1)
                smx(3)
                nx(0, "klo")
                smx(4)
                smx(5)
                nx(0, 1)
                if O:
                    dve.wait_ge(projected, START + n - 1)
                    dve.wait_ge(att_bias_in, START + gp)
                    tile0 = p * 4 + (2 * jj - 4)
                    nc.vector.tensor_tensor(H[:, ds(tile0, 2), :], H[:, ds(tile0, 2), :],
                                            bank(R_BANK, TT, 2 * DIM).rearrange("p (a d) -> p a d", a=2),
                                            ALU.add).then_inc(att_added, 1)
                smx(6)
                smx(7)
                if S:
                    dve.wait_ge(scores_reduced, START + 8 * n + 8)
                    dve.wait_ge(negmaxT, START + 2 * n)
                    m2v = M2[:, :, :, :].rearrange("p q t c -> p (q t) c")
                    mxv = mx[:, :, :].rearrange("p q (t e) -> p (q t) e", e=2)
                    nc.vector.tensor_scalar(m2v[:, :, 0:4:2].bitcast(f32r), mxv, -1.0, None, ALU.mult).then_inc(negmax_high, 1)
                    dve.wait_ge(negmax_high, START + n + 1)
                    nc.vector.scalar_tensor_tensor(out=m2v[:, :, 1:4:2], in0=mxv, scalar=-1.0, in1=m2v[:, :, 0:4:2],
                                                   op0=ALU.mult, op1=ALU.subtract).then_inc(negmax_split, 1)
                nx(1, "V")

            with dve.Fori(0, LAYERS) as L:
                g0 = L * NPAIR
                dve.wait_ge(tower_added, START + g0 + 1)
                dve.wait_ge(wa_in, 80 * L + 80)
                dve.wait_ge(vone_ready, 1)
                for slot in ("stats", "qlo", "klo"):
                    prep(g0, 0, 0, slot)
                prep(g0 + 1, 1, 1, "stats")
                for slot in ON_DVE + ("V",):
                    prep(g0, 0, 0, slot)
                for jj in (0, 1):
                    period(g0, 0, 0, jj, True, False, True, True)
                with dve.Fori(0, NPAIR // 2 - 2) as r:
                    p = 2 * r + 1
                    for b in (1, 0):
                        for jj in (0, 1):
                            period(g0 + p + (1 - b), p + (1 - b), b, jj, True, True, True, True)
                for q in (NPAIR - 3, NPAIR - 2, NPAIR - 1):
                    for jj in (0, 1):
                        period(g0 + q, q, q % 2, jj, True, True, q < NPAIR - 1, q < NPAIR - 2)
                for jj in (0, 1):
                    period(g0 + NPAIR, NPAIR, 0, jj, False, True, False, False)

                dve.wait_ge(att_added, START + g0 * 2 + IMGS)
                dve.wait_ge(wb_in, 48 * L + 48)

                def resid(gp, p, b):
                    dve.wait_ge(mlp_out, START + gp + 1)
                    dve.wait_ge(mlp_bias_in, START + gp + 1)
                    nc.vector.tensor_tensor(H[:, ds(p * 4, 4), :], H[:, ds(p * 4, 4), :],
                                            bank(4 + b, TT, 512).rearrange("p (a d) -> p a d", a=4), ALU.add).then_inc(tower_added, 1)

                def step(p, b, more_stats=True, more_norm=True, back=True):
                    if more_stats:
                        stats(g0 + p + 3, p + 3, 1 - b, mlp_stats, mlp_meanvar, mlp_var_eps, mlp_rstd, mlp_normed)
                    if more_norm:
                        normed(g0 + p + 2, p + 2, b, mlp_rstd, mlp_normed, mlp_normedT)
                    if back:
                        resid(g0 + p - 1, p - 1, 1 - b)
                stats(g0, 0, 0, mlp_stats, mlp_meanvar, mlp_var_eps, mlp_rstd, mlp_normed)
                stats(g0 + 1, 1, 1, mlp_stats, mlp_meanvar, mlp_var_eps, mlp_rstd, mlp_normed)
                normed(g0, 0, 0, mlp_rstd, mlp_normed, mlp_normedT)
                stats(g0 + 2, 2, 0, mlp_stats, mlp_meanvar, mlp_var_eps, mlp_rstd, mlp_normed)
                normed(g0 + 1, 1, 1, mlp_rstd, mlp_normed, mlp_normedT)
                step(0, 0, back=False)
                with dve.Fori(0, NPAIR // 2 - 2) as r:
                    step(2 * r + 1, 1)
                    step(2 * r + 2, 0)
                for q in (NPAIR - 3, NPAIR - 2, NPAIR - 1):
                    step(q, q % 2, False, q < NPAIR - 2)
                resid(g0 + NPAIR - 1, NPAIR - 1, 1)

            dve.wait_ge(tower_added, START + 1 + LAYERS * NPAIR)
            dve.wait_ge(w_in, 16 * 22)
            dve.wait_ge(w_pl, 1)

            def norm_out(p, b, dst, s_pw, s_z):
                dve.wait_ge(s_pw, START + p + 1)
                normalise(dst, p, b).then_inc(s_z, 1)

            def last_norm(p, b):
                dve.wait_ge(fin_done, START + p - 1)
                norm_out(p, b, x1e[:, b], fin_rstd, fin_normed)

            def last_bias(p, b):
                dve.wait_ge(fin_weighted, START + p + 1)
                for i in range(2):
                    last = nc.vector.tensor_tensor(H[:, ds(p * 4 + 2 * i, 2), :], x1e[:, b, 2 * i:2 * i + 2, 0:DIM],
                                                   bnorm[:, :, :], ALU.add)
                last.then_inc(fin_done, 1)

            def fin_stats_of(p, b):
                stats(p, p, b, fin_stats, fin_meanvar, fin_var_eps, fin_rstd, fin_normed)
            fin_stats_of(0, 0)
            fin_stats_of(1, 1)
            last_norm(0, 0)
            with dve.Fori(0, NPAIR // 2 - 1) as r:
                for b in (0, 1):
                    p = 2 * r + b
                    fin_stats_of(p + 2, b)
                    last_norm(p + 1, 1 - b)
                    last_bias(p, b)
            last_norm(NPAIR - 1, 1)
            last_bias(NPAIR - 2, 0)
            last_bias(NPAIR - 1, 1)
            dve.wait_ge(fin_done, START + NPAIR)

            nc.vector.reciprocal(rtemp[:, :], rtemp[:, :])
            nc.vector.tensor_copy(bxw[:, :, :], bx[:, :].unsqueeze(2).to_broadcast([SD, SH, TT])).then_inc(w_dv, 1)
            dve.wait_ge(w_dv, 1)
            dve.wait_ge(w_pe, 1)
            nc.vector.tensor_tensor(wcomb[:, :].rearrange("p (h m) -> p h m", m=SM),
                                    bank(0, 128, SL).rearrange("p (h m) -> p h m", m=SM),
                                    rtemp[:, :].unsqueeze(2).to_broadcast([128, SH, SM]), ALU.mult)
            nc.vector.tensor_tensor(bcomb[:, :].rearrange("p (h m) -> p h m", m=SM),
                                    bank(1, TT, SL).rearrange("p (h m) -> p h m", m=SM),
                                    bsl[:, :].unsqueeze(1).to_broadcast([TT, SH, SM]), ALU.add)
            nc.vector.tensor_copy(mqk[:, :], bank(2, SD, SD))
            nc.vector.tensor_copy(wvo[:, 0:4, :], bank(3, SD, 512).rearrange("p (h n) -> p h n", n=DIM))
            nc.vector.tensor_copy(wvo[:, 4:8, :], bank(4, SD, 512).rearrange("p (h n) -> p h n", n=DIM)).then_inc(w_dv, 1)
            dve.wait_ge(w_dv, 2)
            nc.vector.tensor_tensor(bcomb[:, :].rearrange("p (h m) -> p h m", m=SM),
                                    bcomb[:, :].rearrange("p (h m) -> p h m", m=SM),
                                    rtemp[0:TT, :].unsqueeze(2).to_broadcast([TT, SH, SM]), ALU.mult).then_inc(w_dv, 1)
            dve.wait_ge(w_dv, 3)

            def heads_of(b):
                return Lw[:, b, :, :].rearrange("p t (h m) -> p (t h) m", m=SM)

            def first_a(p, b):
                stats(p, p, b, sl_stats, sl_meanvar, sl_var_eps, sl_rstd, sl_normed)

            def first_b(p, b):
                dve.wait_ge(sl_normedT, START + p - 1)
                dve.wait_ge(sl_sums, START + p - 1)
                norm_out(p, b, x1e[:, b], sl_rstd, sl_normed)

            def first_c(p, b):
                dve.wait_ge(sl_logits, START + p + 1)
                dve.wait_ge(sl_weightsT, START + p - 1)
                dve.wait_ge(sl_sums, START + p - 1)
                nc.vector.tensor_tensor(Lw[:, b, :, :], ps[0:TT, 1:3, :].rearrange("p b (t n) -> p (b t) n", n=SL),
                                        bcomb[:, :].unsqueeze(1).to_broadcast([TT, 4, SL]), ALU.add).then_inc(sl_logits_in, 1)

            def first_max(p, b):
                dve.wait_ge(sl_logits_in, START + p + 1)
                dve.wait_ge(sl_shifted, START + p)
                nc.vector.reduce_max(gmx[:, :], heads_of(b), AX.X).then_inc(sl_max, 1)

            def first_d(p, b):
                dve.wait_ge(sl_exp, START + p + 1)
                nc.vector.reduce_sum(gsum[:, :], heads_of(b), AX.X).then_inc(sl_sum, 1)
                dve.wait_ge(sl_sum, START + p + 1)
                dve.wait_ge(sl_weights, START + p)
                nc.vector.reciprocal(grec[:, :], gsum[:, :]).then_inc(sl_sum_inverted, 1)

            def second_a(p):
                dve.wait_ge(sl_sums, START + p + 1)
                tv = ps[:, 3:5, 0:2 * (DIM + 1)].rearrange("p b (c n) -> p b c n", n=DIM + 1)
                nc.vector.tensor_scalar(seps[:, :].rearrange("p (b c) -> p b c", b=2), tv[:, :, :, DIM], 1e-5, None,
                                        ALU.add).then_inc(sl_norm_eps, 1)
                dve.wait_ge(sl_norm_eps, START + p + 1)
                nc.vector.reciprocal(srec[:, :], seps[:, :]).then_inc(sl_norm_inverted, 1)
                dve.wait_ge(sl_norm_inverted, START + p + 1)
                dve.wait_ge(sl_meanT, START + p)
                dve.wait_ge(sl_tokens_in, START + p)
                nc.vector.tensor_tensor(Tp[:, :, :].rearrange("p (b c) n -> p b c n", b=2), tv,
                                        srec[:, :].rearrange("p (b c) -> p b c", b=2).unsqueeze(3)
                                        .to_broadcast([128, 2, 2, DIM + 1]), ALU.mult).then_inc(sl_mean, 1)

            def second_b(p):
                dve.wait_ge(sl_tokens, START + p + 1)
                dve.wait_ge(sl_tokensT, START + p)
                for k in range(4):
                    last = nc.vector.scalar_tensor_tensor(out=tok[:, k, :], in0=bfx[:, k % 2, :], scalar=Tp[:, k, DIM:DIM + 1],
                                                          in1=ps[:, 4, k * SD:(k + 1) * SD], op0=ALU.mult, op1=ALU.add)
                last.then_inc(sl_tokens_in, 1)

            def second_c(p):
                dve.wait_ge(sl_scores, START + p + 1)
                dve.wait_ge(sl_probsT, START + p)
                nc.vector.tensor_tensor(Sm[:, :, :], bank(4, 128, 512).rearrange("p (k n) -> p k n", k=4),
                                        smask[:, :].unsqueeze(1).to_broadcast([128, 4, 128]), ALU.add).then_inc(sl_scores_masked, 1)
                dve.wait_ge(sl_scores_masked, START + p + 1)
                nc.vector.reduce_max(rmx[:, :], Sm[:, :, :], AX.X).then_inc(sl_score_max, 1)
                dve.wait_ge(sl_score_max, START + p + 1)
                nc.vector.tensor_scalar(nmx[:, :], rmx[:, :], -(float(SD) ** -0.5), None, ALU.mult).then_inc(sl_score_negmax, 1)

            def third_a(p):
                dve.wait_ge(sl_probs, START + p + 1)
                nc.vector.reciprocal(arec[:, :], asum[:, :]).then_inc(sl_prob_sums_inverted, 1)

            def third_b(p):
                dve.wait_ge(sl_prob_sums_inverted, START + p + 1)
                dve.wait_ge(sl_mixed, START + p + 1)
                dve.wait_ge(sl_out, START + p)
                nc.vector.tensor_tensor(Gs[:, :, :], bank(5, 128, 512).rearrange("p (k n) -> p k n", k=4),
                                        arec[:, :].unsqueeze(2).to_broadcast([128, 4, DIM]), ALU.mult).then_inc(sl_mixed_in, 1)

            def third_c(p):
                dve.wait_ge(sl_out, START + p + 1)
                dve.wait_ge(sl_bias_in, START + p + 1)
                nc.vector.tensor_tensor(H[:, ds(p * 4, 4), :], H[:, ds(p * 4, 4), :],
                                        bank(5, TT, 512).rearrange("p (a d) -> p a d", a=4), ALU.add).then_inc(sl_added, 1)

            def slice_step(p, b, T=True, S=True, F=True, Z=True, A=True):
                if F:
                    first_c(p + 2, b)
                if S:
                    second_a(p + 1)
                if F:
                    first_max(p + 2, b)
                if T:
                    third_a(p)
                    third_b(p)
                if S:
                    second_b(p + 1)
                if Z:
                    first_b(p + 3, 1 - b)
                if F:
                    first_d(p + 2, b)
                if T:
                    third_c(p)
                if A:
                    first_a(p + 4, b)
                if S:
                    second_c(p + 1)
            first_a(0, 0)
            first_b(0, 0)
            first_a(1, 1)
            slice_step(-2, 0, T=False, S=False)
            slice_step(-1, 1, T=False)
            with dve.Fori(0, NPAIR // 2 - 2) as r:
                for b in (0, 1):
                    slice_step(2 * r + b, b)
            slice_step(NPAIR - 4, 0, A=False)
            slice_step(NPAIR - 3, 1, Z=False, A=False)
            slice_step(NPAIR - 2, 0, F=False, Z=False, A=False)
            slice_step(NPAIR - 1, 1, S=False, F=False, Z=False, A=False)
            dve.wait_ge(sl_added, START + NPAIR)

            def keep(p, b):
                dve.wait_ge(gate_rstd, START + p + 1)
                nc.vector.tensor_copy(mvall[:, ds(p * 4, 4)], mv[:, b, :, 0])
                nc.vector.tensor_copy(rall[:, ds(p * 4, 4)], rstd[:, b, :]).then_inc(gate_kept, 1)

            def gate_stats_of(p, b):
                dve.wait_ge(gate_kept, START + p - 1)
                stats(p, p, b, gate_stats, gate_meanvar, gate_var_eps, gate_rstd, gate_normed)
            gate_stats_of(0, 0)
            with dve.Fori(0, NPAIR // 2 - 1) as r:
                for b in (0, 1):
                    gate_stats_of(2 * r + b + 1, 1 - b)
                    keep(2 * r + b, b)
            gate_stats_of(NPAIR - 1, 1)
            keep(NPAIR - 2, 0)
            keep(NPAIR - 1, 1)
            dve.wait_ge(g_pe, 1)
            nc.vector.tensor_scalar(means[:, :], bank(0, 128, IMGS), 1.0 / NT, None, ALU.mult).then_inc(g_dv, 1)
            dve.wait_ge(g_pe, 2)
            nc.vector.tensor_tensor(lg[:, :], bank(1, IMGS, NE), bg[:, :], ALU.add).then_inc(g_dv, 1)
            dve.wait_ge(g_dv, 2)
            nc.vector.max(top[:, :], lg[:, :]).then_inc(g_dv, 1)
            dve.wait_ge(g_dv, 3)
            nc.vector.max_index(topi[:, :], top[:, :], lg[:, :])
            nc.vector.tensor_scalar(ntop[:, :], top[:, 0:1], -1.0, None, ALU.mult).then_inc(g_dv, 1)
            dve.wait_ge(g_dv, 4)
            nc.vector.tensor_copy(topf[:, :], topi[:, 0:1]).then_inc(g_dv, 1)
            dve.wait_ge(g_act, 1)
            nc.vector.reciprocal(gate[:, :], lsum[:, :]).then_inc(g_dv, 1)
            dve.wait_ge(g_dv, 6)
            nc.vector.tensor_scalar(onehot[:, :], iota[:, :], topf[:, :], gate[:, :], ALU.is_equal, ALU.mult).then_inc(g_dv, 1)
            dve.wait_ge(g_pe, 3)
            nc.vector.tensor_copy(onehotT[:, :], bank(2, NE, IMGS)).then_inc(g_dv, 1)
            dve.wait_ge(g_pe, 4)
            nc.vector.tensor_copy(gbe[:, :], bank(3, IMGS, DIM)).then_inc(g_dv, 1)

            dve.wait_ge(g_in, 32)

            def renorm(p):
                dve.wait_ge(exp_normedT, START + p)
                for t in range(4):
                    last = nc.vector.tensor_scalar(z[:, t, :], H[:, ds(p * 4 + t, 1), :].rearrange("p a d -> p (a d)"),
                                                   mvall[:, ds(p * 4 + t, 1)], rall[:, ds(p * 4 + t, 1)],
                                                   ALU.subtract, ALU.mult)
                last.then_inc(exp_normed, 1)

            def gated(p, b, r):
                dve.wait_ge(exp_out, START + p + 1)
                dve.wait_ge(exp_bias_in, START + p + 1)
                dve.wait_ge(o_out[b], START + 64 * r)
                for i in range(2):
                    last = nc.vector.scalar_tensor_tensor(
                        out=OB[:, b, 2 * i:2 * i + 2, :], in0=ps[0:TT, 2 + b, 2 * i * DIM:(2 * i + 2) * DIM].rearrange("p (t d) -> p t d", t=2),
                        scalar=gateb[:, ds(p * 2 + i, 1)], in1=H[:, ds(p * 4 + 2 * i, 2), :],
                        op0=ALU.mult, op1=ALU.add)
                last.then_inc(exp_added, 1)
            renorm(0)
            with dve.Fori(0, NPAIR // 2 - 1) as r:
                for b in (0, 1):
                    p = 2 * r + b
                    renorm(p + 1)
                    gated(p, b, r)
            renorm(NPAIR - 1)
            gated(NPAIR - 2, 0, NPAIR // 2 - 1)
            gated(NPAIR - 1, 1, NPAIR // 2 - 1)

        @block.scalar
        def _(act):
            act.wait_ge(init_done, 1)
            act.wait_ge(c_in, 160)

            def prep(gp, b, slot):
                if slot == "yT":
                    act.wait_ge(att_normedT, START + gp + 1)
                    act.wait_ge(v_projected, START + gp)
                    nc.scalar.activation(yT[:, :], bank(P_BANK, 128, W2), ACT.Identity,
                                         bias=cols[:, 1:2], scale=cols[:, 0:1]).then_inc(att_affine, 1)
                if slot == "qhi":
                    act.wait_ge(q_projected, START + gp + 1)
                    act.wait_ge(stacked, START + 8 * gp)
                    nc.scalar.activation(qhi[:, :], bank(P_BANK + 1, 128, W2), ACT.Identity,
                                         bias=cols[:, 2:3]).then_inc(q_high, 1)
                if slot == "khi":
                    act.wait_ge(k_projected, START + gp + 1)
                    act.wait_ge(stacked, START + 8 * gp)
                    nc.scalar.activation(khi[:, :], bank(P_BANK, 128, W2), ACT.Identity,
                                         bias=cols[:, 3:4]).then_inc(k_high, 1)
                if slot in ON_ACT:
                    act.wait_ge(stacked, START + STEPS * gp + slot + 1)
                    act.wait_ge(scoresT_ready, last_read(gp, slot))
                    if slot % 2 == 0:
                        nc.scalar.activation(qs[:, b, slot // 2, :], bank(P_BANK + 1, 128, W2), ACT.Identity).then_inc(stack_by_act, 1)
                    else:
                        for e in range(2):
                            last = nc.scalar.activation(ks[0:96, b, slot - 1 + e, :], bank(P_BANK, 96, W2), ACT.Identity,
                                                        scale=mcols[0:96, e:e + 1])
                        last.then_inc(stack_by_act, 1)

            def period(gp, b, jj, S, T, O, P):
                n = gp * 2 + jj
                s_img = n - 1
                sb_, sj = (1 - b, 1) if jj == 0 else (b, 0)

                def nx(j, slot):
                    if P and j == jj:
                        prep(gp + 1, 1 - b, slot)

                def negmax(hf):
                    if T:
                        act.wait_ge(negmaxT, START + 2 * s_img + hf + 1)
                        nc.scalar.activation(qs[96:128, sb_, 2 * hf:2 * hf + 2, sj * NT:(sj + 1) * NT],
                                             ps[96:128, R_BANK, 0:W2].rearrange("p (t c) -> p t c", t=2),
                                             ACT.Identity).then_inc(negmax_in, 1)

                def expo(v):
                    if T:
                        act.wait_ge(scoresT_ready, START + 8 * s_img + v + 1)
                        if v % 2 == 0:
                            act.wait_ge(values_summed, START + 4 * s_img + v // 2 - 1)
                        nc.scalar.activation(PT[:, v % 4, :], bank(T_BANK + v % 2, TT, W2), ACT.Exp,
                                             scale=SCALE).then_inc(probs_ready, 1)
                nx(0, "yT")
                negmax(0)
                if O:
                    act.wait_ge(values_summed, START + 4 * (n - 2) + 4)
                    act.wait_ge(out_tokens, START + n - 2)
                    nc.scalar.activation(oraw[:, :], bank(O_BANK, 128, W2), ACT.Identity).then_inc(out_copied, 1)
                negmax(1)
                nx(1, 4)
                nx(0, "qhi")
                expo(0)
                nx(0, "khi")
                expo(1)
                nx(1, 5)
                if O:
                    act.wait_ge(out_normedT, START + n - 1)
                    act.wait_ge(projected, START + n - 2)
                    nc.scalar.activation(onT[:, :], bank(R_BANK, 128, NT), ACT.Identity).then_inc(out_normedT_in, 1)
                nx(0, 0)
                expo(2)
                expo(3)
                nx(1, 6)
                expo(4)
                expo(5)
                nx(1, 7)
                nx(0, 2)
                expo(6)
                expo(7)
                nx(0, 3)

            with act.Fori(0, LAYERS) as L:
                g0 = L * NPAIR
                act.wait_ge(wa_in, 80 * L + 80)
                act.wait_ge(vone_ready, 1)
                for slot in ("yT", "qhi", "khi") + ON_ACT:
                    prep(g0, 0, slot)
                period(g0, 0, 0, True, False, False, True)
                period(g0, 0, 1, True, True, False, True)
                with act.Fori(0, NPAIR // 2 - 1) as r:
                    p = 2 * r + 1
                    for b in (1, 0):
                        for jj in (0, 1):
                            period(g0 + p + (1 - b), b, jj, True, True, True, True)
                for jj in (0, 1):
                    period(g0 + NPAIR - 1, 1, jj, True, True, True, False)
                for jj in (0, 1):
                    period(g0 + NPAIR, 0, jj, False, jj == 0, True, False)

                act.wait_ge(wb_in, 48 * L + 48)

                def yTb(gp):
                    act.wait_ge(mlp_normedT, START + gp + 1)
                    act.wait_ge(mlp_hidden, START + 2 * gp)
                    nc.scalar.activation(yT[:, :], bank(0, 128, W2), ACT.Identity,
                                         bias=cols[:, 5:6], scale=cols[:, 4:5]).then_inc(mlp_affine, 1)

                def gelu(gp, b):
                    for c in range(2):
                        act.wait_ge(mlp_hidden, START + 2 * gp + c + 1)
                        if c == 0:
                            act.wait_ge(mlp_out, START + gp - 1)
                        nc.scalar.activation(gT[:, b, c, :], bank(2 + c, 128, W2), ACT.Gelu,
                                             bias=cols[:, 6 + c:7 + c]).then_inc(mlp_gelu, 1)
                yTb(g0)
                with act.Fori(0, NPAIR // 2 - 1) as r:
                    p = 2 * r
                    for b in (0, 1):
                        gelu(g0 + p + b, b)
                        yTb(g0 + p + b + 1)
                gelu(g0 + NPAIR - 2, 0)
                yTb(g0 + NPAIR - 1)
                gelu(g0 + NPAIR - 1, 1)

            act.wait_ge(w_dv, 3)
            act.wait_ge(tower_added, START + 1 + LAYERS * NPAIR)

            def first_x(p):
                act.wait_ge(sl_normedT, START + p + 1)
                act.wait_ge(sl_logits, START + p)
                nc.scalar.activation(yT[:, :], bank(0, 128, W2), ACT.Identity).then_inc(sl_normedT_in, 1)

            def copy(dst, src, done):
                nc.scalar.activation(dst, src, ACT.Identity).then_inc(done, 1)

            def slice_step(p, b, T=True, S=True, F=True, Z=True):
                q = p + 1
                if T:
                    act.wait_ge(sl_probsT, START + p + 1)
                    copy(ET[:, :], bank(5, 128, 512), sl_probsT_in)
                if S:
                    act.wait_ge(sl_meanT, START + q + 1)
                    act.wait_ge(sl_tokens, START + q)
                    copy(TpT[:, :], bank(3, 128, 512), sl_meanT_in)
                    act.wait_ge(sl_weightsT, START + q + 1)
                    act.wait_ge(sl_out, START + q - 1)
                    copy(wT[:, 1 - b, :, :], ps[:, 6:8, 0:W2], sl_weightsT_in)
                if F:
                    act.wait_ge(sl_shifted, START + p + 3)
                    nc.scalar.activation(Lw[:, b, :, :], Lw[:, b, :, :], ACT.Exp).then_inc(sl_exp, 1)
                if S:
                    act.wait_ge(sl_tokensT, START + q + 1)
                    act.wait_ge(sl_scores, START + q)
                    copy(tokT[:, :], bank(3, SD, 512), sl_tokensT_in)
                    act.wait_ge(sl_keys, START + q + 1)
                    copy(AT[:, :], bank(4, SD, 512), sl_keys_in)
                if Z:
                    first_x(p + 3)
                if S:
                    act.wait_ge(sl_values, START + q + 1)
                    act.wait_ge(sl_mixed, START + q)
                    copy(Us[:, :, :], bank(3, 128, 512).rearrange("p (k n) -> p k n", k=4), sl_values_in)
                    act.wait_ge(sl_score_negmax, START + q + 1)
                    act.wait_ge(sl_prob_sums_inverted, START + q)
                    for k in range(4):
                        last = nc.scalar.activation(Sm[:, k, :], Sm[:, k, :], ACT.Exp, bias=nmx[:, k:k + 1],
                                                    scale=float(SD) ** -0.5, accum_out=asum[:, k:k + 1])
                    last.then_inc(sl_probs, 1)
            first_x(0)
            slice_step(-2, 0, T=False, S=False)
            slice_step(-1, 1, T=False)
            with act.Fori(0, NPAIR // 2 - 2) as r:
                for b in (0, 1):
                    slice_step(2 * r + b, b)
            slice_step(NPAIR - 4, 0)
            slice_step(NPAIR - 3, 1, Z=False)
            slice_step(NPAIR - 2, 0, F=False, Z=False)
            slice_step(NPAIR - 1, 1, S=False, F=False, Z=False)

            with act.Fori(0, NPAIR // 2) as r:
                for b in (0, 1):
                    act.wait_ge(gate_centred, START + 2 * r + b + 1)
                    for t in range(4):
                        last = nc.scalar.activation(x1e[:, b, t, 0:DIM], x1e[:, b, t, 0:DIM], ACT.Identity,
                                                    scale=rstd[:, b, t:t + 1])
                    last.then_inc(gate_normed, 1)
            act.wait_ge(g_dv, 4)
            nc.scalar.activation(lge[:, :], lg[:, :], ACT.Exp, bias=ntop[:, :], accum_out=lsum[:, :]).then_inc(g_act, 1)
            with act.Fori(0, NPAIR // 2) as r:
                for b in (0, 1):
                    p = 2 * r + b
                    act.wait_ge(exp_normedT, START + p + 1)
                    act.wait_ge(exp_out, START + p - 1)
                    nc.scalar.activation(zT[:, b, :], bank(b, 128, W2), ACT.Identity).then_inc(exp_normedT_in, 1)

        @block.tensor
        def _(pe):
            pe.wait_ge(init_done, 1)
            pe.wait_ge(c_in, 160)
            with pe.Fori(0, IMGS // NBUF) as it:
                for b in range(NBUF):
                    pe.wait_ge(p_in[b], 16 * it + 16)
                    pe.wait_ge(embedded, START + it * NBUF + (b - NBUF + 1))
                    for t, rows in ((0, TT), (1, R_CLS)):
                        for c in range(KCH):
                            last = nc.tensor.matmul(ps[0:rows, b, t * DIM:(t + 1) * DIM],
                                                    patch[:, b, c, t * TT:t * TT + rows], wc[:, c, :],
                                                    start=(c == 0), stop=(c == KCH - 1))
                    last.then_inc(emb_done, 1)

            def prep(gp, b, slot):
                if slot == "tr":
                    pe.wait_ge(att_normed, START + gp + 1)
                    pe.wait_ge(*copied(gp - 1, STEPS - 1))
                    for t in range(4):
                        last = nc.tensor.transpose(ps[:, P_BANK, t * TT:(t + 1) * TT], z[:, t, :], ident[0:TT, 0:TT])
                    last.then_inc(att_normedT, 1)
                if slot == "q":
                    pe.wait_ge(att_affine, START + gp + 1)
                    pe.wait_ge(v_in, START + gp)
                    nc.tensor.matmul(bank(P_BANK + 1, 128, W2), wqkv[:, 0:DIM], yT[:, :], start=True, stop=True).then_inc(q_projected, 1)
                if slot == "k":
                    nc.tensor.matmul(bank(P_BANK, 128, W2), wqkv[:, DIM:2 * DIM], yT[:, :], start=True, stop=True).then_inc(k_projected, 1)
                if slot == "v":
                    pe.wait_ge(*copied(gp, STEPS - 2))
                    for t in range(4):
                        last = nc.tensor.matmul(ps[0:TT, P_BANK + 1, t * DIM:(t + 1) * DIM], yT[:, t * TT:(t + 1) * TT],
                                                wqkv[:, 2 * DIM:3 * DIM], start=True, stop=True)
                    last.then_inc(v_projected, 1)
                if isinstance(slot, int):
                    s = slot
                    if s == 0:
                        pe.wait_ge(q_low, START + gp + 1)
                    elif s == 1:
                        pe.wait_ge(k_low, START + gp + 1)
                    else:
                        pe.wait_ge(*copied(gp, s - 2))
                    sel, hi, lo = (selq, qhi, qlo) if s % 2 == 0 else (selk, khi, klo)
                    o = bank(P_BANK + 1 - s % 2, 128, W2)
                    nc.tensor.matmul(o, sel[:, s // 2, 0, :], hi[:, :], start=True, stop=False)
                    nc.tensor.matmul(o, sel[:, s // 2, 1, :], lo[:, :], start=False, stop=True).then_inc(stacked, 1)

            def period(gp, b, jj, S, T, O, P):
                n = gp * 2 + jj
                si = n - 1
                sb_, sj = (1 - b, 1) if jj == 0 else (b, 0)
                ob, oj = 1 - b, jj

                def nx(j, slot):
                    if P and j == jj:
                        prep(gp + 1, 1 - b, slot)

                def scores(u):
                    if not S:
                        return
                    t, qt = u // 2, u % 2
                    if qt == 0 and jj == 0:
                        pe.wait_ge(*copied(gp, 2 * t))
                        pe.wait_ge(*copied(gp, 2 * t + 1))
                    pe.wait_ge(scores_reduced, START + 8 * n + u - 1)
                    for e in range(2):
                        last = nc.tensor.matmul(
                            ps[0:TT, S_BANK + u % 2, e * NT:(e + 1) * NT],
                            qs[:, b, t, jj * NT + qt * TT:jj * NT + (qt + 1) * TT],
                            ks[:, b, 2 * t + e, jj * NT:(jj + 1) * NT], start=True, stop=True)
                    last.then_inc(scores_ready, 1)

                def negmax(hf):
                    if not T:
                        return
                    if hf == 0:
                        pe.wait_ge(negmax_split, START + si + 1)
                        pe.wait_ge(att_added, START + n - 2)
                    else:
                        pe.wait_ge(negmax_in, START + 2 * si + 1)
                    for t in range(2):
                        for qt in range(2):
                            last = nc.tensor.matmul(
                                ps[96:128, R_BANK, t * NT + qt * TT:t * NT + (qt + 1) * TT],
                                M2[:, qt, 2 * hf + t, :], ident[0:TT, 0:TT], start=True, stop=True)
                    last.then_inc(negmaxT, 1)

                def tscores(v):
                    if not T:
                        return
                    g, kt, tt = v // 4, (v // 2) % 2, v % 2
                    t = 2 * g + tt
                    if v == 0 or v == 4:
                        pe.wait_ge(negmax_in, START + 2 * si + g + 1)
                    pe.wait_ge(probs_ready, START + 8 * si + v - 1)
                    for e in range(2):
                        last = nc.tensor.matmul(
                            ps[0:TT, T_BANK + v % 2, e * NT:(e + 1) * NT],
                            ks[:, sb_, 2 * t + e, sj * NT + kt * TT:sj * NT + (kt + 1) * TT],
                            qs[:, sb_, t, sj * NT:(sj + 1) * NT], start=True, stop=True)
                    last.then_inc(scoresT_ready, 1)

                def values(img, vb, vj, w):
                    g, kt = w // 2, w % 2
                    pe.wait_ge(probs_ready, START + 8 * img + 2 * w + 2)
                    if w == 0:
                        pe.wait_ge(out_copied, START + img)
                        pe.wait_ge(v_in, START + (gp if jj == 0 else gp + 1))
                    K = TT if kt == 0 else VT - TT
                    for i in range(4):
                        last = nc.tensor.matmul(
                            ps[32 * i:32 * i + 32, O_BANK, g * NT:(g + 1) * NT],
                            Vx[0:K, vb, 2 * vj + kt, 4 * g + i, :],
                            PT[0:K, 2 * (w % 2) + i // 2, (i % 2) * NT:(i % 2 + 1) * NT],
                            start=(kt == 0), stop=(kt == 1))
                    last.then_inc(values_summed, 1)

                def to_tokens():
                    if not O:
                        return
                    pe.wait_ge(out_copied, START + n - 1)
                    if T:
                        pe.wait_ge(negmax_in, START + 2 * si + 2)
                    else:
                        pe.wait_ge(att_added, START + n - 2)
                    for qt in range(2):
                        for g in range(2):
                            last = nc.tensor.transpose(ps[0:TT, R_BANK, (2 * qt + g) * DIM:(2 * qt + g + 1) * DIM],
                                                       oraw[:, g * NT + qt * TT:g * NT + (qt + 1) * TT], ident[:, :])
                    last.then_inc(out_tokens, 1)

                def to_channels():
                    if O:
                        pe.wait_ge(out_normed, START + n - 1)
                        for qt in range(2):
                            last = nc.tensor.transpose(ps[:, R_BANK, qt * TT:(qt + 1) * TT], on[:, qt, :], ident[0:TT, 0:TT])
                        last.then_inc(out_normedT, 1)

                def project():
                    if O:
                        pe.wait_ge(out_normedT_in, START + n - 1)
                        for qt in range(2):
                            last = nc.tensor.matmul(ps[0:TT, R_BANK, qt * DIM:(qt + 1) * DIM], onT[:, qt * TT:(qt + 1) * TT],
                                                    wpj[:, :], start=True, stop=True)
                        last.then_inc(projected, 1)

                scores(0)
                nx(1, 4)
                nx(0, "tr")
                scores(1)
                negmax(0)
                if O:
                    values(n - 2, ob, oj, 3)
                scores(2)
                nx(0, "q")
                negmax(1)
                tscores(0)
                tscores(1)
                nx(0, "k")
                scores(3)
                to_tokens()
                nx(1, 5)
                nx(1, 6)
                scores(4)
                tscores(2)
                nx(0, 0)
                tscores(3)
                to_channels()
                if T:
                    values(si, sb_, sj, 0)
                scores(5)
                project()
                nx(0, 1)
                tscores(4)
                scores(6)
                tscores(5)
                nx(0, 2)
                if T:
                    values(si, sb_, sj, 1)
                scores(7)
                tscores(6)
                nx(0, 3)
                nx(1, 7)
                nx(1, "v")
                tscores(7)
                if T:
                    values(si, sb_, sj, 2)

            with pe.Fori(0, LAYERS) as L:
                g0 = L * NPAIR
                pe.wait_ge(wa_in, 80 * L + 80)
                pe.wait_ge(vone_ready, 1)
                for slot in ("tr", "q", "k", 0, 1, 2, 3, 4, 5, 6, 7, "v"):
                    prep(g0, 0, slot)
                period(g0, 0, 0, True, False, False, True)
                period(g0, 0, 1, True, True, False, True)
                with pe.Fori(0, NPAIR // 2 - 1) as r:
                    p = 2 * r + 1
                    for b in (1, 0):
                        for jj in (0, 1):
                            period(g0 + p + (1 - b), b, jj, True, True, True, True)
                for jj in (0, 1):
                    period(g0 + NPAIR - 1, 1, jj, True, True, True, False)
                for jj in (0, 1):
                    period(g0 + NPAIR, 0, jj, False, jj == 0, True, False)

                pe.wait_ge(wb_in, 48 * L + 48)
                pe.wait_ge(att_added, START + g0 * 2 + IMGS)

                def trb(gp):
                    pe.wait_ge(mlp_normed, START + gp + 1)
                    pe.wait_ge(mlp_affine, START + gp)
                    for t in range(4):
                        last = nc.tensor.transpose(ps[:, 0, t * TT:(t + 1) * TT], z[:, t, :], ident[0:TT, 0:TT])
                    last.then_inc(mlp_normedT, 1)

                def fc1(gp):
                    pe.wait_ge(mlp_affine, START + gp + 1)
                    pe.wait_ge(mlp_gelu, START + 2 * gp)
                    for c in range(2):
                        nc.tensor.matmul(bank(2 + c, 128, W2), w1[:, c * 128:(c + 1) * 128], yT[:, :],
                                         start=True, stop=True).then_inc(mlp_hidden, 1)

                def fc2(gp, b):
                    pe.wait_ge(mlp_gelu, START + 2 * gp + 2)
                    pe.wait_ge(tower_added, START + gp)
                    for t in range(4):
                        for c in range(2):
                            last = nc.tensor.matmul(ps[0:TT, 4 + b, t * DIM:(t + 1) * DIM], gT[:, b, c, t * TT:(t + 1) * TT],
                                                    w2[:, c, :], start=(c == 0), stop=(c == 1))
                    last.then_inc(mlp_out, 1)
                trb(g0)
                fc1(g0)
                trb(g0 + 1)
                with pe.Fori(0, NPAIR // 2 - 1) as r:
                    p = 2 * r + 1
                    for b in (1, 0):
                        q = p + (1 - b)
                        fc1(g0 + q)
                        trb(g0 + q + 1)
                        fc2(g0 + q - 1, 1 - b)
                fc1(g0 + NPAIR - 1)
                fc2(g0 + NPAIR - 2, 0)
                fc2(g0 + NPAIR - 1, 1)

            pe.wait_ge(tower_added, START + 1 + LAYERS * NPAIR)
            pe.wait_ge(w_in, 16 * 22)
            pe.wait_ge(w_dv, 1)
            for h in range(SH):
                nc.tensor.matmul(ps[:, 0, h * SM:(h + 1) * SM], wx[:, h, :], wslT[:, :], start=True, stop=True)
                nc.tensor.matmul(ps[0:TT, 1, h * SM:(h + 1) * SM], bxw[:, h, :], wslT[:, :], start=True, stop=True)
            nc.tensor.matmul(bank(2, SD, SD), wq3[:, 0, :], wq3[:, 1, :], start=True, stop=True)
            for g in range(2):
                last = nc.tensor.matmul(bank(3 + g, SD, 512), wq3[:, 2, :],
                                        woT[:, 4 * g:4 * g + 4, :].rearrange("p h n -> p (h n)"), start=True, stop=True)
            last.then_inc(w_pe, 1)
            pe.wait_ge(w_dv, 3)

            def first_t(p, b):
                pe.wait_ge(sl_normed, START + p + 1)
                pe.wait_ge(sl_normedT_in, START + p)
                for t in range(4):
                    last = nc.tensor.transpose(ps[:, 0, t * TT:(t + 1) * TT], x1e[:, b, t, 0:DIM], ident[0:TT, 0:TT])
                last.then_inc(sl_normedT, 1)

            def first_l(p):
                pe.wait_ge(sl_normedT_in, START + p + 1)
                pe.wait_ge(sl_logits_in, START + p)
                for t in range(4):
                    last = nc.tensor.matmul(ps[0:TT, 1 + t // 2, (t % 2) * SL:(t % 2 + 1) * SL], yT[:, t * TT:(t + 1) * TT],
                                            wcomb[:, :], start=True, stop=True)
                last.then_inc(sl_logits, 1)

            def second_sums(p, b):
                pe.wait_ge(sl_weights, START + p + 1)
                pe.wait_ge(sl_values_in, START + p)
                pe.wait_ge(sl_scores_masked, START + p)
                for i in range(2):
                    for c in range(2):
                        for t in range(2):
                            last = nc.tensor.matmul(ps[:, 3 + i, c * (DIM + 1):(c + 1) * (DIM + 1)],
                                                    Lw[:, b, 2 * i + t, c * 128:(c + 1) * 128], x1e[:, b, 2 * i + t, :],
                                                    start=(t == 0), stop=(t == 1))
                last.then_inc(sl_sums, 1)

            def second_weights(p, b):
                pe.wait_ge(sl_weightsT_in, START + p)
                for c in range(2):
                    for t in range(4):
                        last = nc.tensor.transpose(ps[:, 6 + c, t * TT:(t + 1) * TT], Lw[:, b, t, c * 128:(c + 1) * 128],
                                                   ident[0:TT, 0:TT])
                last.then_inc(sl_weightsT, 1)

            def second_sumsT(p):
                pe.wait_ge(sl_mean, START + p + 1)
                for k in range(4):
                    last = nc.tensor.transpose(ps[:, 3, k * 128:(k + 1) * 128], Tp[:, k, 0:DIM], ident[:, :])
                last.then_inc(sl_meanT, 1)

            def second_tokens(p):
                pe.wait_ge(sl_meanT_in, START + p + 1)
                for k in range(4):
                    for i in range(4):
                        h = 4 * (k % 2) + i
                        last = nc.tensor.matmul(ps[32 * i:32 * i + 32, 4, k * SD:(k + 1) * SD],
                                                TpT[:, k * 128 + 32 * i:k * 128 + 32 * i + 32],
                                                wfxT[:, h * SD:(h + 1) * SD], start=True, stop=True)
                last.then_inc(sl_tokens, 1)

            def second_tokensT(p):
                pe.wait_ge(init_done, 1)
                pe.wait_ge(sl_tokens_in, START + p + 1)
                for k in range(4):
                    last = nc.tensor.transpose(ps[0:SD, 3, k * 128:(k + 1) * 128], tok[:, k, :], ident[:, :])
                last.then_inc(sl_tokensT, 1)

            def second_keys(p):
                pe.wait_ge(init_done, 1)
                pe.wait_ge(sl_tokensT_in, START + p + 1)
                nc.tensor.matmul(bank(4, SD, 512), mqk[:, :], tokT[:, :], start=True, stop=True).then_inc(sl_keys, 1)

            def second_values(p):
                for k in range(4):
                    for i in range(4):
                        h = 4 * (k % 2) + i
                        last = nc.tensor.matmul(ps[32 * i:32 * i + 32, 3, k * DIM:(k + 1) * DIM],
                                                tokT[:, k * 128 + 32 * i:k * 128 + 32 * i + 32],
                                                wvo[:, h, :], start=True, stop=True)
                last.then_inc(sl_values, 1)

            def second_scores(p):
                pe.wait_ge(sl_keys_in, START + p + 1)
                for k in range(4):
                    last = nc.tensor.matmul(ps[:, 4, k * 128:(k + 1) * 128], AT[:, k * 128:(k + 1) * 128],
                                            tokT[:, k * 128:(k + 1) * 128], start=True, stop=True)
                last.then_inc(sl_scores, 1)

            def third_probs(p):
                pe.wait_ge(sl_probs, START + p + 1)
                pe.wait_ge(sl_added, START + p)
                for k in range(4):
                    last = nc.tensor.transpose(ps[:, 5, k * 128:(k + 1) * 128], Sm[:, k, :], ident[:, :])
                last.then_inc(sl_probsT, 1)

            def third_values(p):
                pe.wait_ge(sl_probsT_in, START + p + 1)
                pe.wait_ge(sl_values_in, START + p + 1)
                for k in range(4):
                    last = nc.tensor.matmul(ps[:, 5, k * 128:(k + 1) * 128], ET[:, k * 128:(k + 1) * 128], Us[:, k, :],
                                            start=True, stop=True)
                last.then_inc(sl_mixed, 1)

            def third_out(p, b, i):
                if i == 0:
                    pe.wait_ge(sl_mixed_in, START + p + 1)
                    pe.wait_ge(sl_weightsT_in, START + p + 1)
                for t in (2 * i, 2 * i + 1):
                    for c in range(2):
                        last = nc.tensor.matmul(ps[0:TT, 5, t * DIM:(t + 1) * DIM], wT[:, b, c, t * TT:(t + 1) * TT],
                                                Gs[:, 2 * i + c, :], start=(c == 0), stop=(c == 1))
                if i == 1:
                    last.then_inc(sl_out, 1)

            def slice_step(p, b, T=True, S=True, F=True, Z=True):
                if F:
                    first_l(p + 2)
                if S:
                    second_sums(p + 1, 1 - b)
                if T:
                    third_probs(p)
                if S:
                    second_weights(p + 1, 1 - b)
                    second_sumsT(p + 1)
                if T:
                    third_values(p)
                if S:
                    second_tokens(p + 1)
                if T:
                    third_out(p, b, 0)
                if S:
                    second_tokensT(p + 1)
                if T:
                    third_out(p, b, 1)
                if S:
                    second_keys(p + 1)
                if Z:
                    first_t(p + 3, 1 - b)
                if S:
                    second_values(p + 1)
                    second_scores(p + 1)
            first_t(0, 0)
            slice_step(-2, 0, T=False, S=False)
            slice_step(-1, 1, T=False)
            with pe.Fori(0, NPAIR // 2 - 2) as r:
                for b in (0, 1):
                    slice_step(2 * r + b, b)
            slice_step(NPAIR - 4, 0)
            slice_step(NPAIR - 3, 1, Z=False)
            slice_step(NPAIR - 2, 0, F=False, Z=False)
            slice_step(NPAIR - 1, 1, S=False, F=False, Z=False)

            with pe.Fori(0, NPAIR // 2) as r:
                for b in (0, 1):
                    p = 2 * r + b
                    pe.wait_ge(gate_normed, START + p + 1)
                    for i in range(2):
                        for t in range(2):
                            last = nc.tensor.matmul(ps[:, 0, ds(p * 2 + i, 1)], x1e[:, b, 2 * i + t, 0:DIM], onec[:, :],
                                                    start=(t == 0), stop=(t == 1))
                    last.then_inc(gate_sums, 1)
            pe.wait_ge(gate_sums, START + NPAIR)
            nc.tensor.matmul(ps[0:1, 1, 0:1], onec[:, :], onec[:, :], start=True, stop=True).then_inc(g_pe, 1)
            pe.wait_ge(g_dv, 1)
            nc.tensor.matmul(bank(1, IMGS, NE), means[:, :], wg[:, :], start=True, stop=True).then_inc(g_pe, 1)
            pe.wait_ge(g_dv, 7)
            nc.tensor.transpose(bank(2, NE, IMGS), onehot[:, :], ident[0:IMGS, 0:IMGS]).then_inc(g_pe, 1)
            pe.wait_ge(g_dv, 8)
            nc.tensor.matmul(bank(3, IMGS, DIM), onehotT[:, :], be[:, :], start=True, stop=True).then_inc(g_pe, 1)

            pe.wait_ge(g_dv, 9)
            pe.wait_ge(g_in, 32)

            def turn(p, b):
                pe.wait_ge(exp_normed, START + p + 1)
                pe.wait_ge(exp_normedT_in, START + p - 1)
                for t in range(4):
                    last = nc.tensor.transpose(ps[:, b, t * TT:(t + 1) * TT], z[:, t, :], ident[0:TT, 0:TT])
                last.then_inc(exp_normedT, 1)

            def expert(p, b):
                pe.wait_ge(exp_normedT_in, START + p + 1)
                pe.wait_ge(exp_added, START + p - 1)
                for i in range(2):
                    e = pe.value_load(idxrow[0:1, ds(p * 2 + i, 1)], min_val=0, max_val=NE - 1)
                    for t in (2 * i, 2 * i + 1):
                        last = nc.tensor.matmul(ps[0:TT, 2 + b, t * DIM:(t + 1) * DIM], zT[:, b, t * TT:(t + 1) * TT],
                                                we[:, ds(e, 1), :].rearrange("p a n -> p (a n)"), start=True, stop=True)
                last.then_inc(exp_out, 1)
            turn(0, 0)
            with pe.Fori(0, NPAIR // 2 - 1) as r:
                for b in (0, 1):
                    expert(2 * r + b, b)
                    turn(2 * r + b + 1, 1 - b)
            expert(NPAIR - 2, 0)
            turn(NPAIR - 1, 1)
            expert(NPAIR - 1, 1)


def _constants():
    import numpy as np

    heads, hd = 8, 16
    sel = np.zeros((2, 128, 4, 2, 128), np.float32)
    d = np.arange(hd)
    for t in range(heads // 2):
        a, b = 2 * t * hd, (2 * t + 1) * hd
        for which, part, col, row in (
            (0, 0, 0, a), (0, 0, 16, a), (0, 1, 32, a), (0, 1, 48, b), (0, 0, 64, b), (0, 0, 80, b),
            (1, 0, 0, a), (1, 1, 16, a), (1, 0, 32, a), (1, 0, 48, b), (1, 0, 64, b), (1, 1, 80, b),
        ):
            sel[which, row + d, t, part, col + d] = 1.0
    mcols = np.zeros((128, 4), np.float32)
    mcols[0:48, 0] = 1.0
    mcols[48:96, 1] = 1.0
    mcols[96:98, 2] = 1.0
    mcols[98:100, 3] = 1.0
    return sel, mcols


def _inputs(x, cls_tok, a):
    import numpy as np

    B, C, S, _ = x.shape
    P = 16
    G = S // P
    k = C * P * P
    patches = x.reshape(B, C, G, P, G, P).transpose(0, 1, 3, 5, 2, 4).reshape(B, k // 128, 128, G * G).transpose(0, 2, 1, 3)
    sel, mcols = _constants()
    tok = lambda n: a["L0_tok_" + n]
    L, dim = tok("ln1_w").shape
    q_b = tok("qkv_b")
    at = lambda n: a["L0_attn_" + n]
    ff = lambda n: a["L0_ffn_" + n]
    SM, SD = at("Wslice").shape
    SH = at("Wx").shape[0] // SD
    NE = ff("bg").shape[0]
    f1 = tok("fc1_b")
    cols = np.stack([tok("ln1_w"), tok("ln1_b"), q_b[:, 0:dim], q_b[:, dim:2 * dim], tok("ln2_w"), tok("ln2_b"),
                     f1[:, 0:dim], f1[:, dim:2 * dim]], axis=2)
    return {
        "patches": patches, "conv_w": tok("conv_w"), "conv_b_row": tok("conv_b")[None],
        "cls_token": tok("cls_token")[0], "pos": tok("pos_embed")[0], "cls_tok": cls_tok[0],
        "cols": cols, "qkv_w": tok("qkv_w"), "proj_w": tok("proj_w"), "fc1_w": tok("fc1_w"), "fc2_w": tok("fc2_w"),
        "bv_row": q_b[:, None, 2 * dim:], "pb_row": tok("proj_b")[:, None], "fb_row": tok("fc2_b")[:, None],
        "ident": np.eye(128, dtype=np.float32), "mcols": mcols,
        "norm_w_row": tok("norm_w")[None], "norm_b_row": tok("norm_b")[None], "zero_row": np.zeros((1, dim), np.float32),
        "wx": at("Wx"), "bxT": at("bx").reshape(SH, SD).T, "wslT": at("Wslice").T, "bsl_row": at("bslice")[None],
        "temp_row": at("temperature").reshape(1, SH), "wfxT": at("Wfx").T,
        "bfx": np.repeat(at("bfx").reshape(2, 4, 1, SD), SM, axis=2).reshape(2, 4 * SM, SD).transpose(1, 0, 2),
        "wq3": np.stack([at("Wq"), at("Wk"), at("Wv")], axis=1),
        "woT": at("Wout").T.reshape(SH, SD, dim).transpose(1, 0, 2), "bo_row": at("bout")[None],
        "smask": np.where(np.arange(128)[:, None] // SM == np.arange(128)[None] // SM, 0.0, -1e30).astype(np.float32),
        "we": ff("We"), "be": ff("be"), "wg": ff("Wg"), "bg_row": ff("bg")[None],
        "iota_row": np.arange(NE, dtype=np.float32)[None],
        "selq": sel[0].reshape(128, -1), "selk": sel[1].reshape(128, -1),
    }


def kernel(x, cls_tok, **a):
    import numpy as np
    import concourse.bacc as bacc
    from concourse import mybir
    from concourse.bass_utils import run_bass_kernel_spmd

    named = _inputs(np.asarray(x), np.asarray(cls_tok), {k: np.asarray(v) for k, v in a.items()})
    arrays = {f"in_{k}": np.ascontiguousarray(v) for k, v in named.items()}
    nc = bacc.Bacc("TRN2", target_bir_lowering=False, num_devices=1, dynamic_dma_scratch_size=4096)
    D = {k[3:]: nc.dram_tensor(k, v.shape, mybir.dt.from_np(v.dtype), kind="ExternalInput").ap() for k, v in arrays.items()}
    B, NT, DIM = x.shape[0], 198, cls_tok.shape[2]
    out = nc.dram_tensor("out_h", (B, NT, DIM), mybir.dt.float32, kind="ExternalOutput").ap()
    vit_slice_moe(nc, D, out)
    r = run_bass_kernel_spmd(nc, [arrays], core_ids=[0])
    return r.results[0]["out_h"]
```
